# Optimizing a Trainium2 kernel written in Bass

```python
import numpy as np
import jax
import jax.numpy as jnp

def _softmax(x, axis=-1):
    return jax.nn.softmax(x, axis=axis)

def _gelu(x):
    return jax.nn.gelu(x, approximate=True)

def _silu(x):
    return jax.nn.silu(x)

def _sigmoid(x):
    return jax.nn.sigmoid(x)

def _layernorm(x, axis=-1, eps=1e-05):
    m = jnp.mean(x, axis=axis, keepdims=True)
    v = jnp.var(x, axis=axis, keepdims=True)
    return (x - m) / jnp.sqrt(v + eps)

def _scatter_add(tgt, idx, src, axis=0):
    return tgt.at[idx].add(src)

def _segment_sum(src, seg, n):
    return jax.ops.segment_sum(src, seg, n)
kernel_name = 'mk_perceiver_d2_seqx_r8_e464ef'

def setup_inputs(seed: int=0):
    np.random.seed(seed)
    _w = jnp.asarray

    def _rec_inputs():
        import jax
        import jax.numpy as jnp
        _rk = jax.random.key(seed)
        x = -0.0003929 + 0.9999 * jax.random.normal(jax.random.fold_in(_rk, 1), (2, 128, 128), jnp.float32)
        _lenS = 128 - jax.random.randint(jax.random.fold_in(_rk, 7), (2,), 0, max(1, 128 // 4) + 1, jnp.int32)
        _lenS2 = 2048 - jax.random.randint(jax.random.fold_in(_rk, 8), (2,), 0, max(1, 2048 // 4) + 1, jnp.int32)
        _ctx_1024P = jax.random.normal(jax.random.fold_in(_rk, 11), (2, 16, 128), jnp.float32)
        _ctx_1024c = jax.random.dirichlet(jax.random.fold_in(_rk, 511), 0.3 * jnp.ones((16,), jnp.float32), (2, 2048))
        _ctx_1024t = jnp.einsum('bsk,bkd->bsd', _ctx_1024c, _ctx_1024P)
        _ctx_1024t = _ctx_1024t * jax.lax.rsqrt(jnp.mean(jnp.square(_ctx_1024t)) + 1e-12) * 0.953939
        ctx_1024 = -1.39393e-06 + 0.999914 * (_ctx_1024t + 0.3 * jax.random.normal(jax.random.fold_in(_rk, 611), (2, 2048, 128), jnp.float32))
        _validS = jnp.arange(128)[None, :] < _lenS[:, None]
        _validS2 = jnp.arange(2048)[None, :] < _lenS2[:, None]
        _causal = jnp.tril(jnp.ones((128, 128), dtype=bool))
        mask_BxSxS2_if1 = jnp.where(jnp.ones((2, 128, 2048), dtype=bool), 1, 0).astype(jnp.int32)
        return (x, ctx_1024, mask_BxSxS2_if1)
    x, ctx_1024, mask_BxSxS2_if1 = _rec_inputs()

    def _L0_xattn_setup():
        import jax, jax.numpy as jnp
        import numpy as np
        B, C_LEN, Q_LEN, D = (8, 256, 64, 128)
        key = jax.random.key(seed)
        ks = jax.random.split(key, 10)
        scale = 1.0 / np.sqrt(D)
        return {'c': jax.random.normal(ks[0], (B, C_LEN, D), dtype=jnp.float32), 'q': jax.random.normal(ks[1], (B, Q_LEN, D), dtype=jnp.float32), 'w_cq': jax.random.normal(ks[2], (D,), dtype=jnp.float32) * scale, 'b_cq': jax.random.normal(ks[3], (), dtype=jnp.float32) * scale, 'w_c': jax.random.normal(ks[4], (D,), dtype=jnp.float32) * scale, 'b_c': jax.random.normal(ks[5], (), dtype=jnp.float32) * scale, 'w_q': jax.random.normal(ks[6], (D,), dtype=jnp.float32) * scale, 'b_q': jax.random.normal(ks[7], (), dtype=jnp.float32) * scale, 'W_l': jax.random.normal(ks[8], (D, 4 * D), dtype=jnp.float32) * (1.0 / np.sqrt(4 * D)), 'b_l': jax.random.normal(ks[9], (D,), dtype=jnp.float32) * (1.0 / np.sqrt(4 * D))}
    _L0_xattn_all = _L0_xattn_setup()
    _L0_xattn_in = {k: v for k, v in _L0_xattn_all.items() if k in ('w_cq', 'b_cq', 'w_c', 'b_c', 'w_q', 'b_q', 'W_l', 'b_l')}
    del _L0_xattn_all

    def _L0_attn_setup():
        import jax, jax.numpy as jnp
        import numpy as np
        D_MODEL = 128
        IDX_HEADS = 4
        IDX_DIM = 64
        TOP_K = 32

        def _rope(x):
            B, S, D = x.shape
            half = D // 2
            inv_freq = 1.0 / 10000.0 ** (jnp.arange(half, dtype=jnp.float32) / half)
            ang = jnp.arange(S, dtype=jnp.float32)[:, None] * inv_freq[None, :]
            cos, sin = (jnp.cos(ang), jnp.sin(ang))
            x1, x2 = (x[..., :half], x[..., half:])
            return jnp.concatenate([x1 * cos - x2 * sin, x1 * sin + x2 * cos], axis=-1)
        key = jax.random.key(seed)
        ks = jax.random.split(key, 11)
        B, S, D = (2, 512, D_MODEL)
        s = 0.02
        return {'x': jax.random.normal(ks[0], (B, S, D), dtype=jnp.float32), 'w_qkv': jax.random.normal(ks[1], (3 * D, D), dtype=jnp.float32) * s, 'b_qkv': jnp.zeros((3 * D,), dtype=jnp.float32), 'w_o': jax.random.normal(ks[2], (D, D), dtype=jnp.float32) * s, 'b_o': jnp.zeros((D,), dtype=jnp.float32), 'w_iq': jax.random.normal(ks[3], (IDX_HEADS * IDX_DIM, D), dtype=jnp.float32) * s, 'b_iq': jnp.zeros((IDX_HEADS * IDX_DIM,), dtype=jnp.float32), 'w_ik': jax.random.normal(ks[4], (IDX_DIM, D), dtype=jnp.float32) * s, 'b_ik': jnp.zeros((IDX_DIM,), dtype=jnp.float32), 'w_iw': jax.random.normal(ks[5], (IDX_HEADS, D), dtype=jnp.float32) * s, 'b_iw': jnp.zeros((IDX_HEADS,), dtype=jnp.float32)}
    _L0_attn_all = _L0_attn_setup()
    _L0_attn_in = {k: v for k, v in _L0_attn_all.items() if k in ('w_qkv', 'b_qkv', 'w_o', 'b_o', 'w_iq', 'b_iq', 'w_ik', 'b_ik', 'w_iw', 'b_iw')}
    del _L0_attn_all

    def _L0_ffn_setup():
        import jax, jax.numpy as jnp
        import numpy as np
        NUM_EXPERTS = 8
        TOP_K = 2
        key = jax.random.key(seed)
        ks = jax.random.split(key, 4)
        B, S, H, F = (4, 512, 128, 512)
        x = jax.random.normal(ks[0], (B, S, H), dtype=jnp.float32)
        router_w = jax.random.normal(ks[1], (H, NUM_EXPERTS), dtype=jnp.float32) * 0.02
        w1 = jax.random.normal(ks[2], (H, F), dtype=jnp.float32) * 0.02
        b1 = jnp.zeros((F,), dtype=jnp.float32)
        w2 = jax.random.normal(ks[3], (F, H), dtype=jnp.float32) * 0.02
        b2 = jnp.zeros((H,), dtype=jnp.float32)
        return {'x': x, 'router_w': router_w, 'w1': w1, 'b1': b1, 'w2': w2, 'b2': b2}
    _L0_ffn_all = _L0_ffn_setup()
    _L0_ffn_in = {k: v for k, v in _L0_ffn_all.items() if k in ('router_w', 'w1', 'b1', 'w2', 'b2')}
    del _L0_ffn_all

    def _L1_xattn_setup():
        import jax, jax.numpy as jnp
        import numpy as np
        D_MODEL = 128
        NUM_HEADS = 16
        D_K = D_MODEL // NUM_HEADS
        key = jax.random.key(seed)
        ks = jax.random.split(key, 12)
        B, S = (2, 256)
        s = 1.0 / np.sqrt(D_MODEL)
        inp = {'query': jax.random.normal(ks[0], (B, S, D_MODEL), jnp.float32), 'key': jax.random.normal(ks[1], (B, S, D_MODEL), jnp.float32), 'value': jax.random.normal(ks[2], (B, S, D_MODEL), jnp.float32), 'mask': jnp.ones((B, S, S), jnp.int32), 'Wq': jax.random.normal(ks[3], (D_MODEL, D_MODEL), jnp.float32) * s, 'bq': jax.random.normal(ks[4], (D_MODEL,), jnp.float32) * s, 'Wk': jax.random.normal(ks[5], (D_MODEL, D_MODEL), jnp.float32) * s, 'bk': jax.random.normal(ks[6], (D_MODEL,), jnp.float32) * s, 'Wv': jax.random.normal(ks[7], (D_MODEL, D_MODEL), jnp.float32) * s, 'bv': jax.random.normal(ks[8], (D_MODEL,), jnp.float32) * s, 'Wo': jax.random.normal(ks[9], (D_MODEL, D_MODEL), jnp.float32) * s, 'bo': jax.random.normal(ks[10], (D_MODEL,), jnp.float32) * s}
        return inp
    _L1_xattn_all = _L1_xattn_setup()
    _L1_xattn_in = {k: v for k, v in _L1_xattn_all.items() if k in ('Wq', 'bq', 'Wk', 'bk', 'Wv', 'bv', 'Wo', 'bo')}
    del _L1_xattn_all

    def _L1_attn_setup():
        import jax, jax.numpy as jnp
        import numpy as np
        import math
        DIM = 128
        NUM_HEADS = 16
        HEAD_DIM = DIM // NUM_HEADS

        def build_rope_matrix(dim, seq_len):
            position = jnp.arange(seq_len, dtype=jnp.float32)[:, None]
            dim_pair = jnp.arange(0, dim, 2, dtype=jnp.float32)[None, :]
            theta = 10000.0 ** (-dim_pair / dim)
            freqs = position * theta
            return jnp.concatenate([jnp.cos(freqs), jnp.sin(freqs)], axis=-1)

        def apply_rope(x, rope):
            x1, x2 = (x[..., ::2], x[..., 1::2])
            cos = rope[..., ::2]
            sin = rope[..., 1::2]
            return jnp.concatenate([x1 * cos - x2 * sin, x1 * sin + x2 * cos], axis=-1)
        key = jax.random.key(seed)
        ks = jax.random.split(key, 9)
        B, N = (2, 256)
        x = jax.random.normal(ks[0], (B, N, DIM), dtype=jnp.float32)
        bound = math.sqrt(6.0 / (DIM + DIM))

        def w(k):
            return jax.random.uniform(k, (DIM, DIM), jnp.float32, -bound, bound)

        def b(k):
            return jax.random.uniform(k, (DIM,), jnp.float32, -1.0 / math.sqrt(DIM), 1.0 / math.sqrt(DIM))
        return {'x': x, 'Wq': w(ks[1]), 'bq': b(ks[2]), 'Wk': w(ks[3]), 'bk': b(ks[4]), 'Wv': w(ks[5]), 'bv': b(ks[6]), 'Wo': w(ks[7]), 'bo': b(ks[8])}
    _L1_attn_all = _L1_attn_setup()
    _L1_attn_in = {k: v for k, v in _L1_attn_all.items() if k in ('Wq', 'bq', 'Wk', 'bk', 'Wv', 'bv', 'Wo', 'bo')}
    del _L1_attn_all

    def _L1_ffn_setup():
        import jax, jax.numpy as jnp
        import numpy as np
        D_MODEL = 128
        D_FF = 512
        N_EXPERTS = 8
        TOP_K = 2
        D_FF_PER = D_FF // N_EXPERTS
        B, T = (4, 256)
        key = jax.random.key(seed)
        ks = jax.random.split(key, 7)
        b1_bound = 1.0 / np.sqrt(D_MODEL)
        b2_bound = 1.0 / np.sqrt(D_FF_PER)
        return {'x': jax.random.normal(ks[0], (B, T, D_MODEL), dtype=jnp.float32), 'router_w': jax.random.uniform(ks[1], (D_MODEL, N_EXPERTS), minval=-b1_bound, maxval=b1_bound, dtype=jnp.float32), 'router_b': jax.random.uniform(ks[2], (N_EXPERTS,), minval=-b1_bound, maxval=b1_bound, dtype=jnp.float32), 'W1': jax.random.uniform(ks[3], (N_EXPERTS, D_MODEL, D_FF_PER), minval=-b1_bound, maxval=b1_bound, dtype=jnp.float32), 'b1': jax.random.uniform(ks[4], (N_EXPERTS, D_FF_PER), minval=-b1_bound, maxval=b1_bound, dtype=jnp.float32), 'W2': jax.random.uniform(ks[5], (N_EXPERTS, D_FF_PER, D_MODEL), minval=-b2_bound, maxval=b2_bound, dtype=jnp.float32), 'b2': jax.random.uniform(ks[6], (N_EXPERTS, D_MODEL), minval=-b2_bound, maxval=b2_bound, dtype=jnp.float32)}
    _L1_ffn_all = _L1_ffn_setup()
    _L1_ffn_in = {k: v for k, v in _L1_ffn_all.items() if k in ('router_w', 'router_b', 'W1', 'b1', 'W2', 'b2')}
    del _L1_ffn_all
    return {'x': x, 'ctx_1024': ctx_1024, 'mask_BxSxS2_if1': mask_BxSxS2_if1, 'L0_xattn_w_cq': _L0_xattn_in['w_cq'], 'L0_xattn_b_cq': _L0_xattn_in['b_cq'], 'L0_xattn_w_c': _L0_xattn_in['w_c'], 'L0_xattn_b_c': _L0_xattn_in['b_c'], 'L0_xattn_w_q': _L0_xattn_in['w_q'], 'L0_xattn_b_q': _L0_xattn_in['b_q'], 'L0_xattn_W_l': _L0_xattn_in['W_l'], 'L0_xattn_b_l': _L0_xattn_in['b_l'], 'L0_attn_w_qkv': _L0_attn_in['w_qkv'], 'L0_attn_b_qkv': _L0_attn_in['b_qkv'], 'L0_attn_w_o': _L0_attn_in['w_o'], 'L0_attn_b_o': _L0_attn_in['b_o'], 'L0_attn_w_iq': _L0_attn_in['w_iq'], 'L0_attn_b_iq': _L0_attn_in['b_iq'], 'L0_attn_w_ik': _L0_attn_in['w_ik'], 'L0_attn_b_ik': _L0_attn_in['b_ik'], 'L0_attn_w_iw': _L0_attn_in['w_iw'], 'L0_attn_b_iw': _L0_attn_in['b_iw'], 'L0_ffn_router_w': _L0_ffn_in['router_w'], 'L0_ffn_w1': _L0_ffn_in['w1'], 'L0_ffn_b1': _L0_ffn_in['b1'], 'L0_ffn_w2': _L0_ffn_in['w2'], 'L0_ffn_b2': _L0_ffn_in['b2'], 'L1_xattn_Wq': _L1_xattn_in['Wq'], 'L1_xattn_bq': _L1_xattn_in['bq'], 'L1_xattn_Wk': _L1_xattn_in['Wk'], 'L1_xattn_bk': _L1_xattn_in['bk'], 'L1_xattn_Wv': _L1_xattn_in['Wv'], 'L1_xattn_bv': _L1_xattn_in['bv'], 'L1_xattn_Wo': _L1_xattn_in['Wo'], 'L1_xattn_bo': _L1_xattn_in['bo'], 'L1_attn_Wq': _L1_attn_in['Wq'], 'L1_attn_bq': _L1_attn_in['bq'], 'L1_attn_Wk': _L1_attn_in['Wk'], 'L1_attn_bk': _L1_attn_in['bk'], 'L1_attn_Wv': _L1_attn_in['Wv'], 'L1_attn_bv': _L1_attn_in['bv'], 'L1_attn_Wo': _L1_attn_in['Wo'], 'L1_attn_bo': _L1_attn_in['bo'], 'L1_ffn_router_w': _L1_ffn_in['router_w'], 'L1_ffn_router_b': _L1_ffn_in['router_b'], 'L1_ffn_W1': _L1_ffn_in['W1'], 'L1_ffn_b1': _L1_ffn_in['b1'], 'L1_ffn_W2': _L1_ffn_in['W2'], 'L1_ffn_b2': _L1_ffn_in['b2']}

def reference(x, ctx_1024, mask_BxSxS2_if1, L0_xattn_w_cq, L0_xattn_b_cq, L0_xattn_w_c, L0_xattn_b_c, L0_xattn_w_q, L0_xattn_b_q, L0_xattn_W_l, L0_xattn_b_l, L0_attn_w_qkv, L0_attn_b_qkv, L0_attn_w_o, L0_attn_b_o, L0_attn_w_iq, L0_attn_b_iq, L0_attn_w_ik, L0_attn_b_ik, L0_attn_w_iw, L0_attn_b_iw, L0_ffn_router_w, L0_ffn_w1, L0_ffn_b1, L0_ffn_w2, L0_ffn_b2, L1_xattn_Wq, L1_xattn_bq, L1_xattn_Wk, L1_xattn_bk, L1_xattn_Wv, L1_xattn_bv, L1_xattn_Wo, L1_xattn_bo, L1_attn_Wq, L1_attn_bq, L1_attn_Wk, L1_attn_bk, L1_attn_Wv, L1_attn_bv, L1_attn_Wo, L1_attn_bo, L1_ffn_router_w, L1_ffn_router_b, L1_ffn_W1, L1_ffn_b1, L1_ffn_W2, L1_ffn_b2):
    import jax
    import jax.numpy as jnp

    def _L0_xattn_ref(c, q, w_cq, b_cq, w_c, b_c, w_q, b_q, W_l, b_l):
        import jax, jax.numpy as jnp
        import numpy as np
        B, C_LEN, Q_LEN, D = (8, 256, 64, 128)
        cq = jnp.einsum('bcd,bqd,d->bcq', c, q, w_cq) + b_cq
        s = (c @ w_c + b_c)[:, :, None] + (q @ w_q + b_q)[:, None, :] + cq
        a = jax.nn.softmax(s, axis=2)
        c2q_att = jnp.einsum('bcq,bqd->bcd', a, q)
        b_att = jax.nn.softmax(jnp.max(s, axis=2), axis=1)
        q2c_att = jnp.einsum('bc,bcd->bd', b_att, c)[:, None, :]
        x = jnp.concatenate([c, c2q_att, c * c2q_att, c * q2c_att], axis=-1)
        z = x @ W_l.T + b_l
        return z

    def _L0_attn_ref(x, w_qkv, b_qkv, w_o, b_o, w_iq, b_iq, w_ik, b_ik, w_iw, b_iw):
        import jax, jax.numpy as jnp
        import numpy as np
        D_MODEL = 128
        IDX_HEADS = 4
        IDX_DIM = 64
        TOP_K = 32

        def _rope(x):
            B, S, D = x.shape
            half = D // 2
            inv_freq = 1.0 / 10000.0 ** (jnp.arange(half, dtype=jnp.float32) / half)
            ang = jnp.arange(S, dtype=jnp.float32)[:, None] * inv_freq[None, :]
            cos, sin = (jnp.cos(ang), jnp.sin(ang))
            x1, x2 = (x[..., :half], x[..., half:])
            return jnp.concatenate([x1 * cos - x2 * sin, x1 * sin + x2 * cos], axis=-1)
        B, S, D = x.shape
        qkv = x @ w_qkv.T + b_qkv
        Q, K, V = jnp.split(qkv, 3, axis=-1)
        Q, K = (_rope(Q), _rope(K))
        iq = (x @ w_iq.T + b_iq).reshape(B, S, IDX_HEADS, IDX_DIM)
        ik = x @ w_ik.T + b_ik
        iw = x @ w_iw.T + b_iw
        head_scores = jax.nn.relu(jnp.einsum('bqhd,bkd->bhqk', iq, ik))
        index_scores = jnp.einsum('bhqk,bqh->bqk', head_scores, iw)
        k = min(TOP_K, S)
        _, top_idx = jax.lax.top_k(index_scores, k)
        mask = jnp.zeros((B, S, S), dtype=bool)
        mask = mask.at[jnp.arange(B)[:, None, None], jnp.arange(S)[None, :, None], top_idx].set(True)
        attn_bias = jnp.where(mask, 0.0, -jnp.inf)
        scale = 1.0 / np.sqrt(D).astype(np.float32)
        logits = jnp.einsum('bqd,bkd->bqk', Q, K) * scale + attn_bias
        attn = jax.nn.softmax(logits, axis=-1)
        attn_out = jnp.einsum('bqk,bkd->bqd', attn, V)
        return attn_out @ w_o.T + b_o

    def _L0_ffn_ref(x, router_w, w1, b1, w2, b2):
        import jax, jax.numpy as jnp
        import numpy as np
        NUM_EXPERTS = 8
        TOP_K = 2
        B, S, H = x.shape
        xt = x.reshape(-1, H)
        router_logits = jnp.matmul(xt, router_w)
        router_probs = jax.nn.softmax(router_logits, axis=-1)
        top_k_probs, top_k_indices = jax.lax.top_k(router_probs, TOP_K)
        top_k_probs = top_k_probs / jnp.sum(top_k_probs, axis=-1, keepdims=True)
        one_hot = jax.nn.one_hot(top_k_indices, NUM_EXPERTS, dtype=xt.dtype)
        combine = jnp.einsum('tk,tke->te', top_k_probs, one_hot)
        expert_out = jnp.matmul(jax.nn.gelu(jnp.matmul(xt, w1) + b1), w2) + b2
        out = expert_out * jnp.sum(combine, axis=-1, keepdims=True)
        return out.reshape(B, S, H)

    def _L1_xattn_ref(query, key, value, mask, Wq, bq, Wk, bk, Wv, bv, Wo, bo):
        import jax, jax.numpy as jnp
        import numpy as np
        D_MODEL = 128
        NUM_HEADS = 16
        D_K = D_MODEL // NUM_HEADS
        B, S, _ = query.shape

        def proj(x, W, b):
            return (x @ W.T + b).reshape(B, -1, NUM_HEADS, D_K).transpose(0, 2, 1, 3)
        q = proj(query, Wq, bq)
        k = proj(key, Wk, bk)
        v = proj(value, Wv, bv)
        scores = jnp.einsum('bhqd,bhkd->bhqk', q, k) / jnp.sqrt(jnp.float32(D_K))
        m = mask[:, None, :, :]
        scores = jnp.where(m == 0, jnp.float32(-1000000000.0), scores)
        attn = jax.nn.softmax(scores, axis=-1)
        x = jnp.einsum('bhqk,bhkd->bhqd', attn, v)
        x = x.transpose(0, 2, 1, 3).reshape(B, S, D_MODEL)
        return x @ Wo.T + bo

    def _L1_attn_ref(x, Wq, bq, Wk, bk, Wv, bv, Wo, bo):
        import jax, jax.numpy as jnp
        import numpy as np
        import math
        DIM = 128
        NUM_HEADS = 16
        HEAD_DIM = DIM // NUM_HEADS

        def build_rope_matrix(dim, seq_len):
            position = jnp.arange(seq_len, dtype=jnp.float32)[:, None]
            dim_pair = jnp.arange(0, dim, 2, dtype=jnp.float32)[None, :]
            theta = 10000.0 ** (-dim_pair / dim)
            freqs = position * theta
            return jnp.concatenate([jnp.cos(freqs), jnp.sin(freqs)], axis=-1)

        def apply_rope(x, rope):
            x1, x2 = (x[..., ::2], x[..., 1::2])
            cos = rope[..., ::2]
            sin = rope[..., 1::2]
            return jnp.concatenate([x1 * cos - x2 * sin, x1 * sin + x2 * cos], axis=-1)
        B, N, _ = x.shape
        H, hd = (NUM_HEADS, HEAD_DIM)
        rope = build_rope_matrix(hd, N)

        def proj(W, bias):
            y = x @ W.T + bias
            return y.reshape(B, N, H, hd).transpose(0, 2, 1, 3)
        q = apply_rope(proj(Wq, bq), rope)
        k = apply_rope(proj(Wk, bk), rope)
        v = apply_rope(proj(Wv, bv), rope)
        scores = jnp.einsum('bhqd,bhkd->bhqk', q, k) / math.sqrt(hd)
        probs = jax.nn.softmax(scores, axis=-1)
        out = jnp.einsum('bhqk,bhkd->bhqd', probs, v)
        out = apply_rope(out, -rope)
        out = out.transpose(0, 2, 1, 3).reshape(B, N, DIM)
        return out @ Wo.T + bo

    def _L1_ffn_ref(x, router_w, router_b, W1, b1, W2, b2):
        import jax, jax.numpy as jnp
        import numpy as np
        D_MODEL = 128
        D_FF = 512
        N_EXPERTS = 8
        TOP_K = 2
        D_FF_PER = D_FF // N_EXPERTS
        B, T = (4, 256)
        router_logits = x @ router_w + router_b
        routing_weights = jax.nn.softmax(router_logits, axis=-1)
        top_k_weights, top_k_indices = jax.lax.top_k(routing_weights, TOP_K)
        top_k_weights = top_k_weights / jnp.sum(top_k_weights, axis=-1, keepdims=True)
        routing_mask = jnp.zeros_like(routing_weights)
        routing_mask = jnp.take_along_axis(routing_mask, top_k_indices, axis=-1)
        b_idx = jnp.arange(x.shape[0])[:, None, None]
        t_idx = jnp.arange(x.shape[1])[None, :, None]
        routing_mask = jnp.zeros_like(routing_weights).at[b_idx, t_idx, top_k_indices].set(top_k_weights)
        h1 = jnp.einsum('btd,nde->btne', x, W1) + b1
        h1 = jax.nn.gelu(h1, approximate=False)
        out_per_expert = jnp.einsum('btne,nef->btnf', h1, W2) + b2
        output = jnp.sum(out_per_expert * routing_mask[..., None], axis=-2)
        return output
    x = x + _L0_xattn_ref(_layernorm(x, axis=-1), ctx_1024, L0_xattn_w_cq, L0_xattn_b_cq, L0_xattn_w_c, L0_xattn_b_c, L0_xattn_w_q, L0_xattn_b_q, L0_xattn_W_l, L0_xattn_b_l)
    x = x + _L0_attn_ref(_layernorm(x, axis=-1), L0_attn_w_qkv, L0_attn_b_qkv, L0_attn_w_o, L0_attn_b_o, L0_attn_w_iq, L0_attn_b_iq, L0_attn_w_ik, L0_attn_b_ik, L0_attn_w_iw, L0_attn_b_iw)
    x = x + _L0_ffn_ref(_layernorm(x, axis=-1), L0_ffn_router_w, L0_ffn_w1, L0_ffn_b1, L0_ffn_w2, L0_ffn_b2)
    x = x + _L1_xattn_ref(_layernorm(x, axis=-1), ctx_1024, ctx_1024, mask_BxSxS2_if1, L1_xattn_Wq, L1_xattn_bq, L1_xattn_Wk, L1_xattn_bk, L1_xattn_Wv, L1_xattn_bv, L1_xattn_Wo, L1_xattn_bo)
    x = x + _L1_attn_ref(_layernorm(x, axis=-1), L1_attn_Wq, L1_attn_bq, L1_attn_Wk, L1_attn_bk, L1_attn_Wv, L1_attn_bv, L1_attn_Wo, L1_attn_bo)
    x = x + _L1_ffn_ref(_layernorm(x, axis=-1), L1_ffn_router_w, L1_ffn_router_b, L1_ffn_W1, L1_ffn_b1, L1_ffn_W2, L1_ffn_b2)
    return x

_drawn_inputs = setup_inputs


def setup_inputs(seed=0):
    import zlib

    import numpy as np

    out = dict(_drawn_inputs(seed))
    spreads = {'L0_attn_b_qkv': (0.0, 0.287),
     'L0_attn_b_o': (0.0, 0.1),
     'L0_attn_b_iq': (0.0, 0.8),
     'L0_attn_b_ik': (0.0, 0.8),
     'L0_attn_b_iw': (0.0, 0.8),
     'L0_ffn_b1': (0.0, 0.286),
     'L0_ffn_b2': (0.0, 0.1)}
    factors = {'L0_attn_w_qkv': 3.116,
     'L0_attn_w_iq': 4.884,
     'L0_attn_w_ik': 4.431,
     'L0_attn_w_iw': 5.84,
     'L0_ffn_router_w': 8.0,
     'L1_xattn_bq': 2.962,
     'L1_xattn_bk': 8.0,
     'L1_attn_bq': 6.815,
     'L1_attn_bk': 6.498,
     'L1_ffn_b1': 6.073}
    for name, (base, spread) in spreads.items():
        noise = np.random.default_rng([zlib.crc32(name.encode()), seed]).standard_normal(out[name].shape)
        drawn = base * np.exp(spread * noise) if base else spread * noise
        out[name] = jnp.asarray(drawn.astype(out[name].dtype))
    for name, factor in factors.items():
        out[name] = (out[name] * factor).astype(out[name].dtype)
    return out
```

```python
from contextlib import ExitStack

import numpy as np

import concourse.bass as bass
from concourse import mybir

F32 = mybir.dt.float32
BF16 = mybir.dt.bfloat16
I32 = mybir.dt.int32
ALU = mybir.AluOpType
ACT = mybir.ActivationFunctionType
AX = mybir.AxisListType

B, S, D, SK = 2, 128, 128, 2048
H, DH = 16, 8
G = H // 2
CH = SK // 128
IH, TOPK = 4, 32
NE = 8
FC = 4
EPS = 1e-5
MASK_BIG = float(2.0 ** 100)
GONE = -3.0e38
VW = 2 * (DH + 1)
RING = 4
S_LEAD = 6

K_PARTS = (0, 1, 2, 0, 1, 0)
Q_PARTS = (0, 0, 0, 1, 1, 2)
NBLK = len(K_PARTS)
MAX_ROW = NBLK * DH

ROWS = (("b3", 3), ("b_l", D), ("a0_bv", D), ("b_iw", IH), ("a0_bo", D), ("f0_b2", D), ("x1_bv", D), ("x1_bo", D),
        ("a1_bv", 2 * D), ("a1_bo", D), ("f1_rb", NE))
PACKS = {
    "wA": (("wl", 4 * D), ("w_cq", 1), ("w_q", 1), ("w_c", 1)),
    "wB": (("wk", D), ("wv", D), ("bk", 1)),
    "wC": (("q", D), ("qs", D), ("k", D), ("ks", D), ("v", D), ("iq", 2 * D), ("ik", D), ("iw", IH), ("o", D),
           ("bq", 1), ("bqs", 1), ("bk", 1), ("bks", 1), ("biq", 2), ("bik", 1)),
    "wD": (("r", NE), ("w1", FC * D), ("w2", FC * D), ("b1", FC)),
    "wE": (("q", D), ("o", D), ("bq", 1)),
    "wF": (("qa", D), ("qb", D), ("ka", D), ("kb", D), ("v", 2 * D), ("o", D),
           ("bqa", 1), ("bqb", 1), ("bka", 1), ("bkb", 1)),
    "wG": (("r", NE), ("w1", FC * D), ("w2", FC * D), ("b1", FC)),
    "cst": (("ident", D), ("cos", S), ("sin", S), ("A", S), ("B", S), ("va", DH), ("vb", DH), ("na", DH), ("nb", DH),
            ("hm", H), ("R", VW)),
}


def offsets(fields):
    at, out = 0, {}
    for name, n in fields:
        out[name] = (at, at + n)
        at += n
    return out, at


def build(nc, A, out):
    rows_at, n_rows = offsets(ROWS)
    with ExitStack() as ctx:
        def sb(name, shape, dt=F32):
            return ctx.enter_context(nc.sbuf_tensor(name, shape, dt))

        names = {}

        def sem(name):
            if name not in names:
                names[name] = ctx.enter_context(nc.semaphore(name))
            return names[name]

        packs, at = {}, {}
        for name, fields in PACKS.items():
            at[name], n = offsets(fields)
            packs[name] = sb(name, [128, n])

        def w(pack, field):
            a, b = at[pack][field]
            return packs[pack][:, a:b]

        rows = sb("rows", [128, n_rows])

        def row(field):
            a, b = rows_at[field]
            return rows[:, a:b]

        X = [sb(f"x{i}", [128, B, D]) for i in range(7)]
        XB = [sb(f"xb{i}", [128, B, D]) for i in range(2)] * 3
        h = [sb(f"h{i}", [128, B, D]) for i in range(2)] * 3
        hT = [sb(f"hT{i}", [128, B * S]) for i in range(2)] * 3
        stats = sb("stats", [128, 6, B, 6])
        mv = sb("mv", [128, 6, B, 2])
        veps = sb("veps", [128, 6, B])
        rstd = sb("rstd", [128, 6, B])
        half = sb("half", [128, B])
        identb = sb("identb", [128, 128], BF16)
        sel = sb("sel", [128, G, 3, 128], BF16)
        ctxT = sb("ctxT", [128, B, SK])
        ctxN = sb("ctxN", [128, B, CH, D])
        kparts = sb("kparts", [128, 3, B, SK], BF16)
        kst = sb("kst", [128, RING, B, SK], BF16)
        kres = sb("kres", [128, 2, 512])
        vext = sb("vext", [128, B * CH * G * VW + 32 - VW])
        P0 = sb("P0", [128, B, SK])
        PT0 = sb("PT0", [128, B, SK])
        ident = w("cst", "ident")

        mask_q = P0[:, :, :].rearrange("p b k -> p (b k)").bitcast(I32)
        mask_k = PT0[:, :, :].rearrange("p b k -> p (b k)").bitcast(I32)
        mb = ctxN[:, 0, :, :].rearrange("p c d -> p (c d)").bitcast(BF16).rearrange("p (b k) -> p b k", b=B)
        mbT = ctxN[:, 1, :, :].rearrange("p c d -> p (c d)").bitcast(BF16).rearrange(
            "p (b c q) -> p b c q", b=B, c=CH)
        pt_ring = PT0[:, :, :].rearrange("p b k -> p (b k)").rearrange("p (r n) -> p r n", r=4)
        late = kparts[:, :, :, :].rearrange("p a b k -> p (a b k)").bitcast(F32)
        cut = [0]

        def lt(n):
            cut[0] += n
            return late[:, cut[0] - n:cut[0]]

        cm = sb("cm", [128, B * S])
        mx0 = sb("mx0", [128, B])
        den0 = sb("den0", [128, B])
        rden0 = sb("rden0", [128, B])
        after_keys = kres[:, :, :].rearrange("p a n -> p (a n)")
        c2q = after_keys[:, 0:256].rearrange("p (b d) -> p b d", b=B)
        c2qT, x3T, x4T = (after_keys[:, 256 * i:256 * (i + 1)] for i in range(1, 4))
        b3 = sb("b3", [128, 1])
        rowmax = sb("rowmax", [128, B])
        rmT = sb("rmT", [B, 128])
        rsm = sb("rsm", [B, 4])
        erow = sb("erow", [B, 128])
        brow = sb("brow", [B, 128])
        batt = sb("batt", [128, B])
        q2c = sb("q2c", [128, B])
        t_region = lt(1024)
        t1, t2, t3, t4 = (t_region[:, 256 * i:256 * (i + 1)] for i in range(4))
        qr, kr = lt(256), lt(256)
        iqT, ikT = lt(512), lt(256)
        V = lt(256).rearrange("p (b d) -> p b d", b=B)
        relu_region = lt(1024)
        relu = relu_region.rearrange("p (r b i k) -> p r b i k", r=2, b=B, i=IH // 2)
        idx = [lt(256).rearrange("p (b k) -> p b k", b=B) for _ in range(2)]
        keep = lt(256).rearrange("p (b k) -> p b k", b=B)
        lg = lt(256).rearrange("p (b k) -> p b k", b=B)
        Pm = lt(256).rearrange("p (b k) -> p b k", b=B)
        PmT, aT = lt(256), lt(256)
        iw = sb("iw", [128, B, IH])
        m8 = sb("m8", [128, B, TOPK // 8, 8])
        nmx1 = sb("nmx1", [128, B])
        den1 = sb("den1", [128, B])
        rden1 = sb("rden1", [128, B])
        g0 = relu_region.rearrange("p (c t) -> p c t", c=FC)
        g5 = g0
        gw = t_region.rearrange("p (c t) -> p c t", c=FC)
        rt = sb("rt", [128, 2, 160])
        rsel = sb("rsel", [8, 256])
        E8 = sb("E8", [NE, FC * D])
        b2e = sb("b2e", [NE, D])
        ob = sb("ob", [128, B, D])
        qp = sb("qp", [128, 3, B * S], BF16)
        cut[0] = 4 * 256
        O = lt(512).rearrange("p (b n) -> p b n", b=B)
        qres, att3T, r4T = lt(256), lt(256), lt(256)
        att3 = lt(256).rearrange("p (b h n) -> p b h n", b=B, h=H)
        assert cut[0] == 4 * 256 + 6 * 256
        cut[0] += 4 * 256
        v4 = lt(1024).rearrange("p (b h n) -> p b h n", b=B, h=H)
        qr4, kr4 = lt(256), lt(256)
        n4 = lt(256).rearrange("p (b d) -> p b d", b=B)
        r4 = lt(768).rearrange("p (u b d) -> p u b d", u=3, b=B)
        qs = sb("qs", [128, 2, 2, B, S], BF16)
        qt = sb("qt", [128, 2, B, 2, S], BF16)
        mt = sb("mt", [128, 2, B, 128], BF16)
        pmx = sb("pmx", [128, 2, 4, 4])
        nmx3 = sb("nmx3", [128, 2, 4])
        mres = sb("mres", [128, 2, 4])
        oq = sb("oq", [128, B, G, 2, DH + 1])
        rd3 = sb("rd3", [128, B, H])
        flagf = sb("flagf", [1, 1])
        flag = sb("flag", [1, 1], I32)
        onesb = sb("onesb", [128, 1], BF16)
        kbd = ctxT[:, :, :].rearrange("p b (h k) -> p b h k", h=H)
        sc4 = P0[:, :, :].rearrange("p b (h k) -> p b h k", h=H)
        pT4 = PT0[:, :, :].rearrange("p b (h q) -> p b h q", h=H)
        va4 = kst[:, 0, 0, :].bitcast(F32).rearrange("p (b n) -> p b n", b=B)
        vt4 = kst[:, 0, 1, :].bitcast(F32).rearrange("p (u b n) -> p u b n", u=4, b=B)
        mx4 = sb("mx4", [128, B, H])
        o4 = kst[:, 1, :, :].bitcast(F32)
        rd4 = sb("rd4", [128, B, H])

        PS = ctx.enter_context(nc.psum_tensor("psum", [128, 8 * 512], F32))

        def bank(i, n=1):
            return PS[:, 512 * i:512 * (i + n)]

        kdram = nc.dram_tensor("k_parts_dram", [3, 128, B, SK], BF16, kind="Internal").ap()

        def value(b, c, g):
            o = ((b * CH + c) * G + g) * VW
            return vext[:, o:o + 32]

        block = ctx.enter_context(nc.Block())

        @block.sync
        def _(sp):
            sp.dma_start(X[0][:, :, :], A["x"].rearrange("b s d -> s b d")).then_inc(sem("ld_x"), 16)
            sp.dma_start(packs["cst"][:, :], A["cst"]).then_inc(sem("ld_cst"), 16)
            for i in range(4):
                b, k = i // 2, (i % 2) * 1024
                sp.dma_start(ctxT[:, b, k:k + 1024], A["ctxT"][b, :, k:k + 1024]).then_inc(sem(f"ld_ctxT{i}"), 16)
                if i == 0:
                    sp.dma_start(packs["wB"][:, :], A["wB"]).then_inc(sem("ld_wB"), 16)
            for b in range(B):
                sp.dma_start(ctxN[:, b, :, :], A["ctx"][b].rearrange("(c k) d -> k c d", k=128)).then_inc(
                    sem(f"ld_ctxN{b}"), 16)
            for name in ("wC", "wD", "wE"):
                sp.dma_start(packs[name][:, :], A[name]).then_inc(sem("ld_" + name), 16)
            sp.dma_start(sel[:, :, :, :].rearrange("p g a r -> p (g a r)"), A["sel"]).then_inc(sem("ld_sel"), 16)
            for b in range(B):
                sp.wait_ge(sem("k_hi"), 4 * b + 4)
                sp.wait_ge(sem("k_mid"), 4 * b + 4)
                sp.wait_ge(sem("k_lo"), 4 * b + 4)
                for a in range(3):
                    sp.dma_start(kdram[a, :, b, :], kparts[:, a, b, :]).then_inc(sem(f"k_out{b}"), 16)
            for e in range(2):
                for r in range(RING):
                    sp.dma_start(kst[64 * e + MAX_ROW:64 * e + 64, r, :, :].rearrange("p b k -> p (b k)"),
                                 A["tail"]).then_inc(sem("ld_tail"), 16)

            def stack(g0_, n, b, to):
                for blk in range(NBLK):
                    for e in range(2):
                        src = kdram[K_PARTS[blk], :, b, :].rearrange("(g e d) k -> e d g k", e=2, d=DH)[
                            e, :, g0_:g0_ + n, :]
                        r = g0_ % RING
                        dst = kst[64 * e + DH * blk:64 * e + DH * (blk + 1), r:r + n, b, :]
                        sp.dma_start(dst, src).then_inc(to, 16)

            for b in range(B):
                sp.wait_ge(sem(f"k_out{b}"), 48)
                stack(0, RING, b, sem(f"k_in{b}"))
            for name in ("wF", "wG"):
                sp.dma_start(packs[name][:, :], A[name]).then_inc(sem("ld_" + name), 16)
            sp.dma_start(E8[:, :], A["E8"]).then_inc(sem("ld_b2e"), 16)
            sp.dma_start(b2e[:, :], A["b2e"]).then_inc(sem("ld_b2e"), 16)
            for g in range(RING, G):
                sp.wait_ge(sem("st_done"), 8 * (g - RING + 1))
                for b in range(B):
                    stack(g, 1, b, sem(f"k_in{2 + (g - RING) * 2 + b}"))
            sp.wait_ge(sem("out_ready"), 2)
            sp.dma_start(out.rearrange("b s d -> s b d"), X[6][:, :, :]).then_inc(sem("stored"), 16)
            sp.wait_ge(sem("stored"), 16)

        @block.gpsimd
        def _(pool):
            pool.memset(half[:, :], -0.5).then_inc(sem("half"), 1)

            def ln_power(i):
                pool.wait_ge(sem("ln_mv"), 2 * (i + 1))
                pool.tensor_scalar(veps[:, i, :], mv[:, i, :, 1], EPS, None, ALU.add).then_inc(sem("ln_veps"), 1)
                pool.wait_ge(sem("ln_veps"), i + 1)
                pool.wait_ge(sem("half"), 1)
                pool.tensor_tensor(rstd[:, i, :], veps[:, i, :], half[:, :], ALU.pow).then_inc(sem("ln_rstd"), 1)

            ln_power(0)
            pool.memset(onesb[:, :], 1.0).then_inc(sem("onesb"), 1)
            for i in range(8):
                b, k = i // 4, (i % 4) * 512
                pool.wait_ge(sem("k_mid"), i + 1)
                pool.tensor_tensor(kparts[:, 2, b, k:k + 512], kres[:, i % 2, :], kparts[:, 1, b, k:k + 512],
                                   ALU.subtract).then_inc(sem("k_lo"), 1)
            pool.memset(vext[:, :], 1.0).then_inc(sem("v_ones"), 1)
            ln_power(1)
            pool.memset(mt[:, :, :, :], 0.0).then_inc(sem("zeros"), 1)
            pool.memset(qs[:, :, :, :, :], 0.0).then_inc(sem("zeros"), 1)
            pool.memset(qt[:, :, :, :, :], 0.0).then_inc(sem("zeros"), 1)
            ln_power(2)
            ln_power(3)
            pool.memset(v4, 0.0).then_inc(sem("v4_set"), 1)
            pool.wait_ge(sem("v4_set"), 1)
            pool.memset(v4[:, :, :, DH:DH + 1], 1.0).then_inc(sem("v4_set"), 1)
            ln_power(4)
            pool.wait_ge(sem("rotated"), 3)
            pool.wait_ge(sem("x_ready"), 6)
            pool.tensor_tensor(kbd[:, 1, :, :], kr4[:, 128:256].unsqueeze(1).to_broadcast([128, H, 128]),
                               w("cst", "hm").unsqueeze(2).to_broadcast([128, H, 128]), ALU.mult).then_inc(
                sem("kbd1"), 1)
            ln_power(5)

        @block.scalar
        def _(act):
            act.dma_start(packs["wA"][:, :], A["wA"]).then_inc(sem("ld_wA"), 16)
            act.dma_start(rows[:, :], A["rows"].to_broadcast([128, n_rows])).then_inc(sem("ld_rows"), 16)
            act.dma_start(identb[:, :], A["identb"]).then_inc(sem("ld_identb"), 16)
            act.preload_act_table(ACT.Exp)

            def ln_turned(i, src):
                act.wait_ge(sem("ln_hT_ps"), i + 1)
                act.activation(hT[i][:, :], src, ACT.Copy).then_inc(sem("ln_hT"), 1)

            ln_turned(0, bank(4)[:, 0:256])

            def key_hi(i):
                b, k = i // 4, (i % 4) * 512
                act.wait_ge(sem("k_ps"), i + 1)
                if i == 0:
                    act.wait_ge(sem("ld_wB"), 16)
                act.activation(kparts[:, 0, b, k:k + 512], bank(5 + i % 2), ACT.Identity,
                               bias=w("wB", "bk")).then_inc(sem("k_hi"), 1)

            for b in range(B):
                for i in range(4):
                    key_hi(4 * b + i)
                act.wait_ge(sem("mx0"), b + 1)
                act.activation(P0[:, b, :], bank(0, 4), ACT.Exp, bias=mx0[:, b:b + 1],
                               accum_out=den0[:, b:b + 1]).then_inc(sem("probs"), 1)
            act.wait_ge(sem("rm_max"), 1)
            act.activation(erow[:, :], rmT[:, :], ACT.Exp, bias=rsm[:, 0:1], accum_out=rsm[:, 1:2]).then_inc(
                sem("erow"), 1)
            for b in range(B):
                for j in (1, 3):
                    act.wait_ge(sem("pT_ps"), 4 * b + j + 1)
                    act.activation(PT0[:, b, 512 * j:512 * (j + 1)], bank(5), ACT.Copy).then_inc(sem("pT_act"), 1)
            act.wait_ge(sem("turn_ps"), 1)
            act.activation(c2qT, bank(0)[:, 0:256], ACT.Copy).then_inc(sem("turned"), 1)
            act.wait_ge(sem("c2q_ps"), 2)
            for b in range(B):
                act.dma_start(mask_q.rearrange("p (b k) -> p b k", b=B)[:, b],
                              A["mask"][b]).then_inc(sem("ld_mask"), 16)
            for b in range(B):
                act.dma_start(mask_k.rearrange("p (b c q) -> p b c q", b=B, c=CH)[:, b],
                              A["maskT"][b].rearrange("(c k) q -> k c q", k=128)).then_inc(sem("ld_maskT"), 16)

            ln_turned(1, bank(4)[:, 0:256])
            act.wait_ge(sem("k_out0"), 48)
            act.wait_ge(sem("k_out1"), 48)
            act.wait_ge(sem("iq_ps"), 1)
            for j in range(2):
                act.activation(iqT[:, 256 * j:256 * (j + 1)], bank(2)[:, 256 * j:256 * (j + 1)], ACT.Identity,
                               bias=w("wC", "biq")[:, j:j + 1]).then_inc(sem("index_T"), 1)
            act.activation(ikT, bank(3)[:, 0:256], ACT.Identity, bias=w("wC", "bik")).then_inc(sem("index_T"), 1)
            for r in range(2):
                act.wait_ge(sem("hs_ps"), r + 1)
                act.activation(relu_region[:, 512 * r:512 * r + 512], bank(5 + r), ACT.Relu).then_inc(
                    sem("relu"), 1)
            act.wait_ge(sem("v_ones"), 1)
            for i in range(8):
                act.wait_ge(sem("v_ps"), i + 1)
                o = (4 * i) * G * VW
                act.activation(
                    vext[:, o:o + 4 * G * VW].rearrange("p (m n) -> p m n", n=DH + 1)[:, :, 0:DH],
                    bank(2 + i % 2).rearrange("p (m n) -> p m n", n=DH), ACT.Copy).then_inc(sem("v_set"), 1)
            for b in range(B):
                act.wait_ge(sem("nmx1"), b + 1)
                act.activation(Pm[:, b, :], lg[:, b, :], ACT.Exp, bias=nmx1[:, b:b + 1],
                               accum_out=den1[:, b:b + 1]).then_inc(sem("probs"), 1)
            act.preload_act_table(ACT.Gelu_apprx_tanh)
            act.wait_ge(sem("turn_ps"), 2)
            act.activation(PmT, bank(0)[:, 0:256], ACT.Copy).then_inc(sem("turned"), 1)
            act.wait_ge(sem("turn_ps"), 3)
            act.activation(aT, bank(1)[:, 0:256], ACT.Copy).then_inc(sem("turned"), 1)

            ln_turned(2, bank(4)[:, 0:256])
            for c in range(FC):
                act.wait_ge(sem("hidden_ps"), c + 1)
                act.activation(g0[:, c, :], bank(5 + c % 2)[:, 0:256], ACT.Gelu_apprx_tanh,
                               bias=w("wD", "b1")[:, c:c + 1]).then_inc(sem("gelu"), 1)
            act.preload_act_table(ACT.Exp)

            def router_exp(i):
                act.wait_ge(sem("rt_max"), i + 1)
                for b in range(B):
                    act.activation(rt[:, i, 8 * b:8 * b + 8], rt[:, i, 16 + 8 * b:24 + 8 * b], ACT.Exp,
                                   bias=rt[:, i, 32 + b:33 + b],
                                   accum_out=rt[:, i, 34 + b:35 + b]).then_inc(sem("rt_exp"), 1)

            router_exp(0)

            ln_turned(3, bank(4)[:, 0:256])
            act.wait_ge(sem("q3_ps"), 1)
            act.activation(qp[:, 0, :], bank(5)[:, 0:256], ACT.Identity, bias=w("wE", "bq")).then_inc(
                sem("q3_hi"), 1)

            def query_stack(g):
                act.wait_ge(sem("stack_ps"), g + 1)
                if g == 0:
                    act.wait_ge(sem("zeros"), 3)
                if g >= 2:
                    act.wait_ge(sem("s_done"), 16 * (g - 1))
                for e in range(2):
                    p = slice(64 * e, 64 * e + 64)
                    act.activation(qs[p, g % 2, e, :, :].rearrange("p b q -> p (b q)"), bank(7)[p, 0:256],
                                   ACT.Copy).then_inc(sem("qs"), 1)

            def query_stack_max(g):
                act.wait_ge(sem("stackm_ps"), g + 1)
                if g >= 2:
                    act.wait_ge(sem("st_done"), 8 * (g - 1))
                for e in range(2):
                    p = slice(64 * e, 64 * e + 64)
                    act.activation(qt[p, g % 2, :, e, :], bank(7)[p, 0:256].rearrange("p (b q) -> p b q", b=B),
                                   ACT.Copy).then_inc(sem("qt"), 1)

            def out_rows(g, b):
                act.wait_ge(sem("pv_done"), 8 * g + 4 * b + 4)
                if g >= 1:
                    act.wait_ge(sem("oq_ps"), 2 * g - 1 + b)
                act.activation(O[:, b, :], bank(6)[:, 0:256], ACT.Copy).then_inc(sem("o_rows"), 1)

            query_stack(0)
            query_stack(1)
            query_stack_max(0)
            for n in range(8 * G):
                g, j = n // 8, n % 8
                if j == 4 and g + 2 < G:
                    query_stack(g + 2)
                if j == 7 and g + 1 < G:
                    query_stack_max(g + 1)
                act.wait_ge(sem("st_done"), n + 1)
                if n == 0:
                    act.wait_ge(sem("mask_bias"), 4)
                if n >= 4:
                    act.wait_ge(sem("pv_done"), n - 3)
                act.activation(pt_ring[:, n % 4, :], bank(2 + 2 * (n % 2), 2), ACT.Exp, scale=DH ** -0.5).then_inc(
                    sem("p3"), 1)
                if j == 4:
                    out_rows(g, 0)
                if j == 0 and g:
                    out_rows(g - 1, 1)
            out_rows(G - 1, 1)
            act.wait_ge(sem("turn_ps"), 4)
            act.activation(att3T[:, :], bank(0)[:, 0:256], ACT.Copy).then_inc(sem("turned"), 1)

            ln_turned(4, bank(4)[:, 0:256])
            for b in range(B):
                act.wait_ge(sem("sub4"), b + 1)
                act.activation(sc4[:, b, :, :], sc4[:, b, :, :], ACT.Exp, scale=DH ** -0.5).then_inc(sem("probs"), 1)
            for j in (1, 3, 5, 7):
                act.wait_ge(sem("p4T_ps"), j + 1)
                b, q = j // 4, j % 4
                act.activation(pT4[:, b, 4 * q:4 * q + 4, :].rearrange("p h q -> p (h q)"), bank(1),
                               ACT.Copy).then_inc(sem("p4T_act"), 1)
            for b in range(B):
                act.wait_ge(sem("o4_ps"), b + 1)
                act.activation(o4[:, b, 0:512], bank(2 + b), ACT.Copy).then_inc(sem("o4"), 1)
            act.wait_ge(sem("turn_ps"), 5)
            act.activation(r4T[:, :], bank(6)[:, 0:256], ACT.Copy).then_inc(sem("turned"), 1)

            ln_turned(5, bank(4)[:, 0:256])
            router_exp(1)
            act.preload_act_table(ACT.Gelu)
            for c in range(FC):
                act.wait_ge(sem("hidden_ps"), c + 1 + 4)
                act.activation(g5[:, c, :], bank(c)[:, 0:256], ACT.Gelu, bias=w("wG", "b1")[:, c:c + 1]).then_inc(sem("gelu"), 1)

        @block.vector
        def _(v):
            links = [0]

            def link(ins):
                links[0] += 1
                ins.then_inc(sem("dve_link"), 1)
                v.wait_ge(sem("dve_link"), links[0])

            def ln_stats(i):
                for b in range(B):
                    v.bn_stats(stats[:, i, b, :], X[i][:, b, :]).then_inc(sem("ln_stats"), 1)
                for b in range(B):
                    v.wait_ge(sem("ln_stats"), 2 * i + b + 1)
                    v.bn_aggr(mv[:, i, b, :], stats[:, i, b, :]).then_inc(sem("ln_mv"), 1)

            def ln_apply(i):
                v.wait_ge(sem("ln_mv"), 2 * i + 2)
                v.wait_ge(sem("ln_rstd"), i + 1)
                for b in range(B):
                    v.tensor_scalar(h[i][:, b, :], X[i][:, b, :], mv[:, i, b, 0:1], rstd[:, i, b:b + 1],
                                    ALU.subtract, ALU.mult).then_inc(sem("ln_h"), 1)

            def with_bias(i, name):
                v.tensor_tensor(XB[i][:, :, :], X[i][:, :, :], row(name).unsqueeze(1).to_broadcast([128, B, D]),
                                ALU.add).then_inc(sem("xb"), 1)

            v.wait_ge(sem("ld_x"), 16)
            ln_stats(0)
            v.wait_ge(sem("ld_rows"), 16)
            with_bias(0, "b_l")
            v.tensor_reduce(b3[:, :], row("b3"), AX.X, ALU.add).then_inc(sem("b3"), 1)
            ln_apply(0)
            v.wait_ge(sem("ln_hT"), 1)
            v.wait_ge(sem("ld_wA"), 16)
            v.tensor_scalar(cm[:, :], hT[0][:, :], w("wA", "w_cq"), w("wA", "w_q"), ALU.mult, ALU.add).then_inc(
                sem("cm"), 1)

            def key_rest(i):
                b, k = i // 4, (i % 4) * 512
                v.wait_ge(sem("k_hi"), i + 1)
                if i >= 2:
                    v.wait_ge(sem("k_lo"), i - 1)
                v.scalar_tensor_tensor(kres[:, i % 2, :], bank(5 + i % 2), w("wB", "bk"), kparts[:, 0, b, k:k + 512],
                                       ALU.add, ALU.subtract).then_inc(sem("k_res"), 1)
                v.wait_ge(sem("k_res"), i + 1)
                v.tensor_copy(kparts[:, 1, b, k:k + 512], kres[:, i % 2, :]).then_inc(sem("k_mid"), 1)

            v.wait_ge(sem("ld_wB"), 16)
            for b in range(B):
                for i in range(4):
                    key_rest(4 * b + i)
                v.wait_ge(sem("s0_ps"), 4 * b + 4)
                v.tensor_reduce(mx0[:, b:b + 1], bank(0, 4), AX.X, ALU.max, negate=True).then_inc(sem("mx0"), 1)
            v.wait_ge(sem("cwc_ps"), 1)
            v.wait_ge(sem("b3"), 1)
            v.wait_ge(sem("mx0"), 2)
            v.scalar_tensor_tensor(rowmax[:, :], bank(7)[:, 256:256 + B], b3[:, 0:1], mx0[:, :], ALU.add,
                                   ALU.subtract).then_inc(sem("rowmax"), 1)
            v.wait_ge(sem("rm_ps"), 1)
            link(v.tensor_copy(rmT[:, :], bank(1)[0:B, 0:128]))
            v.tensor_reduce(rsm[:, 0:1], rmT[:, :], AX.X, ALU.max, negate=True).then_inc(sem("rm_max"), 1)

            def turned(b, j):
                v.wait_ge(sem("pT_ps"), 4 * b + j + 1)
                v.tensor_copy(PT0[:, b, 512 * j:512 * (j + 1)], bank(4)).then_inc(sem("pT_dve"), 1)

            turned(0, 0)
            v.wait_ge(sem("erow"), 1)
            link(v.reciprocal(rsm[:, 2:3], rsm[:, 1:2]))
            v.tensor_scalar(brow[:, :], erow[:, :], rsm[:, 2:3], None, ALU.mult).then_inc(sem("brow"), 1)
            turned(0, 2)
            v.wait_ge(sem("batt_ps"), 1)
            v.tensor_copy(batt[:, :], bank(1)[:, 128:128 + B]).then_inc(sem("batt"), 1)
            v.wait_ge(sem("probs"), 2)
            v.reciprocal(rden0[:, :], den0[:, :]).then_inc(sem("rden0"), 1)
            turned(1, 0)
            v.wait_ge(sem("q2c_ps"), 1)
            link(v.tensor_copy(q2c[:, :], bank(2)[:, 0:B]))
            v.wait_ge(sem("k_lo"), 8)
            v.tensor_scalar(x4T[:, 0:128], hT[0][:, 0:128], q2c[:, 0:1], None, ALU.mult).then_inc(sem("x4T"), 1)
            v.tensor_scalar(x4T[:, 128:256], hT[0][:, 128:256], q2c[:, 1:2], None, ALU.mult).then_inc(sem("x4T"), 1)
            turned(1, 2)
            v.wait_ge(sem("rden0"), 1)
            for b in range(B):
                v.wait_ge(sem("c2q_ps"), b + 1)
                v.tensor_scalar(c2q[:, b, :], bank(6 + b)[:, 0:128], rden0[:, b:b + 1], None, ALU.mult).then_inc(
                    sem("c2q"), 1)
            v.wait_ge(sem("turned"), 1)
            v.tensor_tensor(x3T[:, :], hT[0][:, :], c2qT[:, :], ALU.mult).then_inc(sem("x3T"), 1)
            v.wait_ge(sem("xb"), 1)
            v.wait_ge(sem("part_ps"), 1)
            v.tensor_tensor(X[1][:, :, :], XB[0][:, :, :], bank(3)[:, 0:256].rearrange("p (b d) -> p b d", b=B),
                            ALU.add).then_inc(sem("x_ready"), 1)

            v.wait_ge(sem("x_ready"), 1)
            ln_stats(1)
            with_bias(1, "a0_bo")
            ln_apply(1)
            v.wait_ge(sem("k_out0"), 48)
            v.wait_ge(sem("k_out1"), 48)
            v.wait_ge(sem("ld_wC"), 16)

            def over_b(ap):
                return ap.unsqueeze(1).to_broadcast([128, B, S])

            def by_b(ap):
                return ap.rearrange("p (b s) -> p b s", b=B)

            v.wait_ge(sem("iw_ps"), 1)
            v.tensor_tensor(iw[:, :, :], bank(7)[:, 256:256 + B * IH].rearrange("p (b h) -> p b h", b=B),
                            row("b_iw").unsqueeze(1).to_broadcast([128, B, IH]), ALU.add).then_inc(sem("iw"), 1)
            v.tensor_tensor(V, bank(7)[:, 0:256].rearrange("p (b d) -> p b d", b=B),
                            row("a0_bv").unsqueeze(1).to_broadcast([128, B, D]), ALU.add).then_inc(sem("V"), 1)

            def rotate(dst, ps, bias, bias_s, ta, tb, cos, sin, name):
                v.scalar_tensor_tensor(by_b(ta), by_b(ps[:, 0:256]), bias, over_b(cos), ALU.add,
                                       ALU.mult).then_inc(sem("rot"), 1)
                v.scalar_tensor_tensor(by_b(tb), by_b(ps[:, 256:512]), bias_s, over_b(sin), ALU.add,
                                       ALU.mult).then_inc(sem("rot"), 1)
                rots[0] += 2
                v.wait_ge(sem("rot"), rots[0])
                v.tensor_tensor(dst, ta, tb, ALU.add).then_inc(sem(name), 1)

            rots = [0]
            v.wait_ge(sem("qk_ps"), 1)
            rotate(qr, bank(0), w("wC", "bq"), w("wC", "bqs"), t1, t2, w("cst", "cos"), w("cst", "sin"), "rotated")
            rotate(kr, bank(1), w("wC", "bk"), w("wC", "bks"), t3, t4, w("cst", "cos"), w("cst", "sin"), "rotated")
            v.wait_ge(sem("iw"), 1)
            for i in range(IH):
                for b in range(B):
                    v.wait_ge(sem("relu"), i % 2 + 1)
                    if i == 0:
                        v.tensor_scalar(idx[0][:, b, :], relu[:, 0, b, 0, :], iw[:, b, 0:1], None, ALU.mult).then_inc(
                            sem("idx"), 1)
                    else:
                        v.wait_ge(sem("idx"), 2 * (i - 1) + b + 1)
                        v.scalar_tensor_tensor(idx[i % 2][:, b, :], relu[:, i % 2, b, i // 2, :], iw[:, b, i:i + 1],
                                               idx[(i - 1) % 2][:, b, :], ALU.mult, ALU.add).then_inc(sem("idx"), 1)
            for r in range(TOPK // 8):
                src, dst = idx[(IH - 1 + r) % 2], idx[(IH + r) % 2]
                for b in range(B):
                    if r == 0:
                        v.wait_ge(sem("idx"), 2 * (IH - 1) + b + 1)
                    else:
                        v.wait_ge(sem("taken"), 2 * (r - 1) + b + 1)
                    v.max(m8[:, b, r, :], src[:, b, :]).then_inc(sem("m8"), 1)
                for b in range(B):
                    v.wait_ge(sem("m8"), 2 * r + b + 1)
                    v.match_replace(dst[:, b, :], m8[:, b, r, :], src[:, b, :], GONE).then_inc(sem("taken"), 1)
            last = idx[(IH + TOPK // 8 - 1) % 2]
            v.wait_ge(sem("lg_ps"), 1)
            for b in range(B):
                v.wait_ge(sem("taken"), 2 * (TOPK // 8 - 1) + b + 1)
                link(v.tensor_scalar(keep[:, b, :], last[:, b, :], GONE * 0.99, -1.0e30, ALU.is_gt, ALU.mult))
                link(v.scalar_tensor_tensor(lg[:, b, :], bank(7)[:, 128 * b:128 * b + 128], float(D) ** -0.5,
                                            keep[:, b, :], ALU.mult, ALU.add))
                v.tensor_reduce(nmx1[:, b:b + 1], lg[:, b, :], AX.X, ALU.max, negate=True).then_inc(sem("nmx1"), 1)
            v.wait_ge(sem("probs"), 4)
            v.reciprocal(rden1[:, :], den1[:, :]).then_inc(sem("rden1"), 1)
            v.wait_ge(sem("rden1"), 1)
            v.wait_ge(sem("xb"), 2)
            v.wait_ge(sem("part_ps"), 2)
            for b in range(B):
                v.scalar_tensor_tensor(X[2][:, b, :], bank(3)[:, 128 * b:128 * b + 128], rden1[:, b:b + 1],
                                       XB[1][:, b, :], ALU.mult, ALU.add).then_inc(sem("x_ready"), 1)

            v.wait_ge(sem("x_ready"), 3)
            ln_stats(2)
            ln_apply(2)

            def router(i, ps):
                lgt = rt[:, i, 16:32].rearrange("p (b n) -> p b n", b=B)
                if i == 0:
                    link(v.tensor_copy(lgt, ps))
                else:
                    link(v.tensor_tensor(lgt, ps, row("f1_rb").unsqueeze(1).to_broadcast([128, B, NE]), ALU.add))
                v.tensor_reduce(rt[:, i, 32:34], lgt, AX.X, ALU.max, negate=True).then_inc(sem("rt_max"), 1)

            def router_top(i):
                v.wait_ge(sem("rt_exp"), 2 * i + 2)
                link(v.reciprocal(rt[:, i, 68:70], rt[:, i, 34:36]))
                for b in range(B):
                    ins = v.tensor_scalar(rt[:, i, 36 + 8 * b:44 + 8 * b], rt[:, i, 8 * b:8 * b + 8],
                                          rt[:, i, 68 + b:69 + b], None, ALU.mult)
                    ins.then_inc(sem("rt_p"), 1)
                for b in range(B):
                    v.wait_ge(sem("rt_p"), 2 * i + b + 1)
                    v.max(rt[:, i, 52 + 8 * b:60 + 8 * b], rt[:, i, 36 + 8 * b:44 + 8 * b]).then_inc(sem("rt_m8"), 1)
                v.wait_ge(sem("rt_m8"), 2 * i + 2)
                top = rt[:, i, 52:68].rearrange("p (b n) -> p b n", b=B)
                link(v.tensor_tensor(rt[:, i, 70:72], top[:, :, 0], top[:, :, 1], ALU.add))
                link(v.reciprocal(rt[:, i, 72:74], rt[:, i, 70:72]))
                return top

            for to, of, name in ((mb.rearrange("p b k -> p (b k)"), mask_q, "ld_mask"),
                                 (mbT.rearrange("p b c q -> p (b c q)"), mask_k, "ld_maskT")):
                v.wait_ge(sem(name), 16 * B)
                v.wait_ge(sem("c2q_ps"), 2)
                for i in range(2):
                    part = slice(i * SK, (i + 1) * SK)
                    v.tensor_scalar(to[:, part], of[:, part], 0.0, -MASK_BIG, ALU.is_equal, ALU.mult).then_inc(
                        sem("mask_bias"), 1)
            v.wait_ge(sem("router_ps"), 1)
            router(0, bank(7)[:, 0:16].rearrange("p (b n) -> p b n", b=B))
            with_bias_row = row("f0_b2").unsqueeze(1).to_broadcast([128, B, D])
            top = router_top(0)
            link(v.tensor_tensor(rt[:, 0, 74:78].rearrange("p (b n) -> p b n", b=B), top[:, :, 0:2],
                                 rt[:, 0, 72:74].unsqueeze(2).to_broadcast([128, B, 2]), ALU.mult))
            link(v.tensor_reduce(rt[:, 0, 78:80], rt[:, 0, 74:78].rearrange("p (b n) -> p b n", b=B), AX.X, ALU.add))
            v.wait_ge(sem("part_ps"), 3)
            link(v.tensor_tensor(ob[:, :, :], bank(3)[:, 0:256].rearrange("p (b d) -> p b d", b=B), with_bias_row,
                                 ALU.add))
            for b in range(B):
                v.scalar_tensor_tensor(X[3][:, b, :], ob[:, b, :], rt[:, 0, 78 + b:79 + b], X[2][:, b, :], ALU.mult,
                                       ALU.add).then_inc(sem("x_ready"), 1)

            v.wait_ge(sem("x_ready"), 5)
            ln_stats(3)
            with_bias(3, "x1_bo")
            ln_apply(3)
            v.wait_ge(sem("ld_wE"), 16)
            v.wait_ge(sem("q3_hi"), 1)
            link(v.scalar_tensor_tensor(qres[:, :], bank(5)[:, 0:256], w("wE", "bq"), qp[:, 0, :], ALU.add,
                                        ALU.subtract))
            v.tensor_copy(qp[:, 1, :], qres[:, :]).then_inc(sem("q3_mid"), 1)
            v.wait_ge(sem("q3_mid"), 1)
            v.tensor_tensor(qp[:, 2, :], qres[:, :], qp[:, 1, :], ALU.subtract).then_inc(sem("q3_lo"), 1)
            v.wait_ge(sem("flag_ps"), 1)
            link(v.tensor_reduce(flagf[:, :], bank(6)[0:1, :], AX.X, ALU.min))
            v.tensor_scalar(flag[:, :], flagf[:, :], 0.0, None, ALU.is_lt).then_inc(sem("flag"), 1)

            def max_parts(g):
                r = g % 2
                v.wait_ge(sem("s_red"), 16 * g + 16)
                link(v.tensor_reduce(nmx3[:, r, :], pmx[:, r, :, :], AX.X, ALU.max, negate=True))
                if g == 0:
                    v.wait_ge(sem("zeros"), 1)
                if g >= 2:
                    v.wait_ge(sem("stackm_ps"), g - 1)
                at_part = [mt[:, r, :, :].rearrange("p b (e m) -> p b e m", e=2)[:, :, :, MAX_ROW + a]
                           for a in range(3)]
                nm = nmx3[:, r, :].rearrange("p (b e) -> p b e", b=B)
                mr = mres[:, r, :].rearrange("p (b e) -> p b e", b=B)
                link(v.tensor_copy(at_part[0], nm))
                link(v.tensor_tensor(mr, nm, at_part[0], ALU.subtract))
                link(v.tensor_copy(at_part[1], mr))
                v.tensor_tensor(at_part[2], mr, at_part[1], ALU.subtract).then_inc(sem("mt"), 1)

            def pair_out(g):
                v.wait_ge(sem("oq_ps"), 2 * g + 2)
                v.tensor_copy(oq[:, :, g, :, :].rearrange("p b e n -> p b (e n)"),
                              bank(7)[:, 0:2 * VW].rearrange("p (b m) -> p b m", b=B)).then_inc(sem("oq"), 1)

            for m in range(16 * G):
                g, i = m // 16, m % 16
                v.wait_ge(sem("s_done"), m + 1)
                v.tensor_reduce(pmx[:, g % 2, i // 4, i % 4:i % 4 + 1], bank(m % 2), AX.X, ALU.max).then_inc(
                    sem("s_red"), 1)
                if i == 15:
                    max_parts(g)
                if i == 9 and g >= 2:
                    pair_out(g - 2)
            pair_out(G - 2)
            pair_out(G - 1)
            v.wait_ge(sem("oq"), G)
            heads = oq[:, :, :, :, :].rearrange("p b g e n -> p b (g e) n")
            link(v.reciprocal(rd3[:, :, :], heads[:, :, :, DH]))
            link(v.tensor_tensor(att3[:, :, :, :], heads[:, :, :, 0:DH],
                                 rd3[:, :, :].unsqueeze(3).to_broadcast([128, B, H, DH]), ALU.mult))
            v.tensor_tensor(ob[:, :, :], att3[:, :, :, :].rearrange("p b h n -> p b (h n)"),
                            row("x1_bv").unsqueeze(1).to_broadcast([128, B, D]), ALU.add).then_inc(sem("att3"), 1)
            v.wait_ge(sem("xb"), 3)
            v.wait_ge(sem("part_ps"), 4)
            v.tensor_tensor(X[4][:, :, :], XB[3][:, :, :], bank(1)[:, 0:256].rearrange("p (b d) -> p b d", b=B),
                            ALU.add).then_inc(sem("x_ready"), 1)

            v.wait_ge(sem("x_ready"), 6)
            ln_stats(4)
            with_bias(4, "a1_bo")
            ln_apply(4)
            v.wait_ge(sem("qk4_ps"), 1)
            v.wait_ge(sem("ld_wF"), 16)
            a4 = [r4[:, i, :, :].rearrange("p b d -> p (b d)") for i in range(2)]
            b4 = [n4[:, :, :].rearrange("p b d -> p (b d)"), r4[:, 2, :, :].rearrange("p b d -> p (b d)")]
            rotate(kr4[:, :], bank(1), w("wF", "bka"), w("wF", "bkb"), b4[0], b4[1], w("cst", "A"), w("cst", "B"),
                   "rotated")
            rotate(qr4[:, :], bank(0), w("wF", "bqa"), w("wF", "bqb"), a4[0], a4[1], w("cst", "A"), w("cst", "B"),
                   "rotated")
            v.wait_ge(sem("rotated"), 3)
            v.tensor_tensor(kbd[:, 0, :, :], kr4[:, 0:128].unsqueeze(1).to_broadcast([128, H, 128]),
                            w("cst", "hm").unsqueeze(2).to_broadcast([128, H, 128]), ALU.mult).then_inc(
                sem("kbd0"), 1)
            v.wait_ge(sem("v4_ps"), 1)
            link(v.tensor_tensor(va4[:, :, 0:256], bank(2).rearrange("p (b n) -> p b n", b=B),
                                 row("a1_bv").unsqueeze(1).to_broadcast([128, B, 2 * D]), ALU.add))

            def per_head(ap):
                return ap.unsqueeze(1).to_broadcast([128, H, DH])

            for b in range(B):
                for u, tab in ((0, "va"), (1, "vb")):
                    v.tensor_tensor(vt4[:, u, b, :].rearrange("p (h n) -> p h n", h=H),
                                    va4[:, b, D * u:D * (u + 1)].rearrange("p (h n) -> p h n", h=H),
                                    per_head(w("cst", tab)), ALU.mult).then_inc(sem("vt4"), 1)
            v.wait_ge(sem("vt4"), 4)
            v.wait_ge(sem("v4_set"), 2)
            for b in range(B):
                v.tensor_tensor(v4[:, b, :, 0:DH], vt4[:, 0, b, :].rearrange("p (h n) -> p h n", h=H),
                                vt4[:, 1, b, :].rearrange("p (h n) -> p h n", h=H), ALU.add).then_inc(sem("v4"), 1)
            for b in range(B):
                sc = bank(4 * b, 4).rearrange("p (h k) -> p h k", h=H)
                v.wait_ge(sem("s4_ps"), b + 1)
                v.tensor_reduce(mx4[:, b, :], sc, AX.X, ALU.max).then_inc(sem("mx4"), 1)
                v.wait_ge(sem("mx4"), b + 1)
                v.tensor_tensor(sc4[:, b, :, :], sc, mx4[:, b, :].unsqueeze(2).to_broadcast([128, H, S]),
                                ALU.subtract).then_inc(sem("sub4"), 1)
            for j in (0, 2, 4, 6):
                v.wait_ge(sem("p4T_ps"), j + 1)
                b, q = j // 4, j % 4
                v.tensor_copy(pT4[:, b, 4 * q:4 * q + 4, :].rearrange("p h q -> p (h q)"), bank(0)).then_inc(
                    sem("p4T_dve"), 1)
            for b in range(B):
                o = bank(4 + b).rearrange("p (h n) -> p h n", h=H)
                v.wait_ge(sem("o4T_ps"), b + 1)
                v.reciprocal(rd4[:, b, :], o[:, :, DH]).then_inc(sem("rd4"), 1)
                v.wait_ge(sem("rd4"), b + 1)
                v.tensor_tensor(n4[:, b, :].rearrange("p (h n) -> p h n", h=H), o[:, :, 0:DH],
                                rd4[:, b, :].unsqueeze(2).to_broadcast([128, H, DH]), ALU.mult).then_inc(
                    sem("n4"), 1)
            for b in range(B):
                v.wait_ge(sem("n4"), b + 1)
                pairs = n4[:, b, :].rearrange("p (h m t) -> p h m t", m=4, t=2)
                for u, tab in ((0, "na"), (1, "nb")):
                    v.tensor_tensor(r4[:, u, b, :].rearrange("p (h f m) -> p h f m", h=H, f=2),
                                    pairs[:, :, :, u].unsqueeze(2).to_broadcast([128, H, 2, 4]),
                                    w("cst", tab).rearrange("p (f m) -> p f m", f=2).unsqueeze(1).to_broadcast(
                                        [128, H, 2, 4]), ALU.mult).then_inc(sem("rot4"), 1)
            v.wait_ge(sem("rot4"), 4)
            v.tensor_tensor(r4[:, 2, :, :], r4[:, 0, :, :], r4[:, 1, :, :], ALU.add).then_inc(sem("r4"), 1)
            v.wait_ge(sem("xb"), 4)
            v.wait_ge(sem("part_ps"), 5)
            v.tensor_tensor(X[5][:, :, :], XB[4][:, :, :], bank(7)[:, 0:256].rearrange("p (b d) -> p b d", b=B),
                            ALU.add).then_inc(sem("x_ready"), 1)

            v.wait_ge(sem("x_ready"), 7)
            ln_stats(5)
            ln_apply(5)
            v.wait_ge(sem("router_ps"), 2)
            router(1, bank(7)[:, 256:272].rearrange("p (b n) -> p b n", b=B))
            top = router_top(1)
            link(v.memset(top[:, :, 2:8], -1.0))
            for b in range(B):
                v.match_replace(rt[:, 1, 80 + 8 * b:88 + 8 * b], top[:, b, :], rt[:, 1, 36 + 8 * b:44 + 8 * b],
                                -2.0).then_inc(sem("rt_mr"), 1)
            v.wait_ge(sem("rt_mr"), 2)
            link(v.scalar_tensor_tensor(rt[:, 1, 96:112], rt[:, 1, 80:96], 0.0, rt[:, 1, 36:52], ALU.is_lt,
                                        ALU.mult))
            v.tensor_tensor(rt[:, 1, 112:128].rearrange("p (b n) -> p b n", b=B),
                            rt[:, 1, 96:112].rearrange("p (b n) -> p b n", b=B),
                            rt[:, 1, 72:74].unsqueeze(2).to_broadcast([128, B, NE]), ALU.mult).then_inc(
                sem("rw"), 1)
            v.wait_ge(sem("rwT_ps"), 1)
            v.tensor_copy(rsel[:, :], bank(5)[0:NE, 0:256]).then_inc(sem("rsel"), 1)
            for c in range(FC):
                v.wait_ge(sem("gelu"), c + 1 + 4)
                v.wait_ge(sem("rx_ps"), c // 2 + 1)
                v.tensor_tensor(gw[:, c, :], g5[:, c, :], bank(6 if c < 2 else 4)[:, 256 * (c % 2):256 * (c % 2) + 256],
                                ALU.mult).then_inc(sem("gw"), 1)
            for b in range(B):
                v.wait_ge(sem("part_ps"), b + 1 + 5)
                v.tensor_tensor(X[6][:, b, :], X[5][:, b, :], bank(2 + b)[:, 256:384], ALU.add).then_inc(
                    sem("out_ready"), 1)

        @block.tensor
        def _(pe):
            def mm(o, lhsT, rhs, start=True, stop=True, **kw):
                return pe.matmul(o, lhsT, rhs, start=start, stop=stop, **kw)

            def ln_turn(i):
                for b in range(B):
                    pe.wait_ge(sem("ln_h"), 2 * i + b + 1)
                    ins = pe.transpose(bank(4)[:, 128 * b:128 * b + 128], h[i][:, b, :], ident)
                ins.then_inc(sem("ln_hT_ps"), 1)

            pe.wait_ge(sem("ld_cst"), 16)
            ln_turn(0)
            pe.wait_ge(sem("ld_wB"), 16)

            def keys(i):
                b, k = i // 4, (i % 4) * 512
                pe.wait_ge(sem(f"ld_ctxT{i // 2}"), 16)
                if i >= 2:
                    pe.wait_ge(sem("k_res"), i - 1)
                mm(bank(5 + i % 2), w("wB", "wk"), ctxT[:, b, k:k + 512]).then_inc(sem("k_ps"), 1)

            def scores0(b, j):
                if b == 1 and j == 0:
                    pe.wait_ge(sem("probs"), 1)
                mm(bank(j), cm[:, 128 * b:128 * b + 128], ctxT[:, b, 512 * j:512 * j + 512]).then_inc(sem("s0_ps"), 1)

            for b in range(B):
                for j in range(4):
                    keys(4 * b + j)
                    if b == 0:
                        pe.wait_ge(sem("cm"), 1)
                        scores0(0, j)
                if b == 1:
                    for j in range(4):
                        scores0(1, j)
            pe.wait_ge(sem("ld_wA"), 16)
            for b in range(B):
                ins = mm(bank(7)[:, 256 + b:257 + b], hT[0][:, 128 * b:128 * b + 128], w("wA", "w_c"))
            ins.then_inc(sem("cwc_ps"), 1)

            def turn_p(b, j):
                if b == 0 and j == 0:
                    pe.wait_ge(sem("ln_hT"), 1)
                    pe.wait_ge(sem("probs"), 1)
                if b == 1 and j == 0:
                    pe.wait_ge(sem("probs"), 2)
                if b == 0 and j == 1:
                    pe.wait_ge(sem("k_res"), 8)
                n = 4 * b + j
                if n >= 2:
                    pe.wait_ge(sem("pT_dve") if j % 2 == 0 else sem("pT_act"), n // 2)
                for c in range(4):
                    ins = pe.transpose(bank(4 + j % 2)[:, 128 * c:128 * c + 128],
                                       P0[:, b, 512 * j + 128 * c:512 * j + 128 * c + 128], ident)
                ins.then_inc(sem("pT_ps"), 1)

            def weigh(b, j):
                n = 4 * b + j
                pe.wait_ge(sem("pT_dve") if j % 2 == 0 else sem("pT_act"), n // 2 + 1)
                if j == 0:
                    pe.wait_ge(sem(f"ld_ctxN{b}"), 16)
                    if b == 0:
                        pe.wait_ge(sem("k_res"), 8)
                    else:
                        pe.wait_ge(sem("rowmax"), 1)
                for c in range(4):
                    ins = mm(bank(6 + b)[:, 0:128], PT0[:, b, 512 * j + 128 * c:512 * j + 128 * c + 128],
                             ctxN[:, b, 4 * j + c, :], start=(j == 0 and c == 0), stop=(j == 3 and c == 3))
                if j == 3:
                    ins.then_inc(sem("c2q_ps"), 1)

            turn_p(0, 0)
            pe.wait_ge(sem("rowmax"), 1)
            pe.wait_ge(sem("probs"), 2)
            pe.transpose(bank(1)[0:B, 0:128], rowmax[:, :], ident).then_inc(sem("rm_ps"), 1)
            turn_p(0, 1)
            weigh(0, 0)
            turn_p(0, 2)
            weigh(0, 1)
            turn_p(0, 3)
            pe.wait_ge(sem("brow"), 1)
            pe.transpose(bank(1)[:, 128:128 + B], brow[:, :], ident[0:B, 0:B]).then_inc(sem("batt_ps"), 1)
            weigh(0, 2)
            turn_p(1, 0)
            weigh(0, 3)
            pe.wait_ge(sem("batt"), 1)
            for b in range(B):
                ins = mm(bank(2)[:, b:b + 1], h[0][:, b, :], batt[:, b:b + 1])
            ins.then_inc(sem("q2c_ps"), 1)
            turn_p(1, 1)
            weigh(1, 0)
            turn_p(1, 2)
            weigh(1, 1)
            turn_p(1, 3)
            weigh(1, 2)
            weigh(1, 3)
            for b in range(B):
                pe.wait_ge(sem("c2q"), b + 1)
                ins = pe.transpose(bank(0)[:, 128 * b:128 * b + 128], c2q[:, b, :], ident)
            ins.then_inc(sem("turn_ps"), 1)
            wl = w("wA", "wl")
            pe.wait_ge(sem("x4T"), 2)
            for b in range(B):
                q = slice(128 * b, 128 * b + 128)
                mm(bank(3)[:, q], hT[0][:, q], wl[:, 0:128], start=True, stop=False)
                mm(bank(3)[:, q], x4T[:, q], wl[:, 384:512], start=False, stop=False)
                pe.wait_ge(sem("turned"), 1)
                mm(bank(3)[:, q], c2qT[:, q], wl[:, 128:256], start=False, stop=False)
                pe.wait_ge(sem("x3T"), 1)
                ins = mm(bank(3)[:, q], x3T[:, q], wl[:, 256:384], start=False, stop=True)
            ins.then_inc(sem("part_ps"), 1)

            ln_turn(1)
            pe.wait_ge(sem("ld_wC"), 16)
            pe.wait_ge(sem("ln_hT"), 2)
            for j in range(2):
                mm(bank(2)[:, 256 * j:256 * j + 256], w("wC", "iq")[:, 128 * j:128 * j + 128], hT[1][:, :])
            mm(bank(3)[:, 0:256], w("wC", "ik"), hT[1][:, :]).then_inc(sem("iq_ps"), 1)
            for b in range(B):
                q = slice(128 * b, 128 * b + 128)
                mm(bank(7)[:, 256 + IH * b:256 + IH * b + IH], hT[1][:, q], w("wC", "iw"))
                ins = mm(bank(7)[:, q], hT[1][:, q], w("wC", "v"))
            ins.then_inc(sem("iw_ps"), 1)
            for j, name in enumerate(("q", "qs", "k", "ks")):
                ins = mm(bank(j // 2)[:, 256 * (j % 2):256 * (j % 2) + 256], w("wC", name), hT[1][:, :])
            ins.then_inc(sem("qk_ps"), 1)
            pe.wait_ge(sem("index_T"), 3)
            for r in range(2):
                p = slice(64 * r, 64 * r + 64)
                for b in range(B):
                    for i in range(IH // 2):
                        c = 256 * i + 128 * b
                        o = 128 * (2 * b + i)
                        ins = mm(bank(5 + r)[:, o:o + 128], iqT[p, c:c + 128], ikT[p, 128 * b:128 * b + 128])
                ins.then_inc(sem("hs_ps"), 1)
            pe.wait_ge(sem("rotated"), 1)
            pe.wait_ge(sem("rotated"), 2)
            pe.wait_ge(sem("V"), 1)
            for b in range(B):
                q = slice(128 * b, 128 * b + 128)
                ins = mm(bank(7)[:, q], qr[:, q], kr[:, q])
            ins.then_inc(sem("lg_ps"), 1)
            for i in range(8):
                if i >= 2:
                    pe.wait_ge(sem("v_set"), i - 1)
                for c in range(4):
                    k = 512 * (i % 4) + 128 * c
                    ins = mm(bank(2 + i % 2)[:, 128 * c:128 * c + 128], ctxT[:, i // 4, k:k + 128], w("wB", "wv"))
                ins.then_inc(sem("v_ps"), 1)
            for b in range(B):
                pe.wait_ge(sem("probs"), b + 1 + 2)
                ins = pe.transpose(bank(0)[:, 128 * b:128 * b + 128], Pm[:, b, :], ident)
            ins.then_inc(sem("turn_ps"), 1)
            pe.wait_ge(sem("turned"), 2)
            for b in range(B):
                q = slice(128 * b, 128 * b + 128)
                ins = mm(bank(1)[:, q], V[:, b, :], PmT[:, q])
            ins.then_inc(sem("turn_ps"), 1)
            pe.wait_ge(sem("turned"), 3)
            pe.wait_ge(sem("v_set"), 8)
            for b in range(B):
                q = slice(128 * b, 128 * b + 128)
                ins = mm(bank(3)[:, q], aT[:, q], w("wC", "o"))
            ins.then_inc(sem("part_ps"), 1)

            ln_turn(2)
            pe.wait_ge(sem("ld_wD"), 16)
            pe.wait_ge(sem("ln_hT"), 3)
            for c in range(FC):
                if c >= 2:
                    pe.wait_ge(sem("gelu"), c - 1)
                mm(bank(5 + c % 2)[:, 0:256], w("wD", "w1")[:, 128 * c:128 * c + 128], hT[2][:, :]).then_inc(sem("hidden_ps"), 1)
                if c == 1:
                    for b in range(B):
                        ins = mm(bank(7)[:, 8 * b:8 * b + 8], hT[2][:, 128 * b:128 * b + 128], w("wD", "r"))
                    ins.then_inc(sem("router_ps"), 1)
            for b in range(B):
                for c in range(FC):
                    pe.wait_ge(sem("gelu"), c + 1)
                    ins = mm(bank(3)[:, 128 * b:128 * b + 128], g0[:, c, 128 * b:128 * b + 128],
                             w("wD", "w2")[:, 128 * c:128 * c + 128], start=(c == 0), stop=(c == FC - 1))
            ins.then_inc(sem("part_ps"), 1)

            pe.wait_ge(sem("onesb"), 1)
            pe.wait_ge(sem("mask_bias"), 4)
            for i in range(8):
                ins = mm(bank(6)[0:1, :], onesb[:, :], mb[:, i // 4, 512 * (i % 4):512 * (i % 4) + 512],
                         start=(i == 0), stop=(i == 7))
            ins.then_inc(sem("flag_ps"), 1)
            ln_turn(3)
            pe.wait_ge(sem("ld_wE"), 16)
            pe.wait_ge(sem("ln_hT"), 4)
            mm(bank(5)[:, 0:256], w("wE", "q"), hT[3][:, :]).then_inc(sem("q3_ps"), 1)
            pe.wait_ge(sem("ld_sel"), 16)
            pe.wait_ge(sem("q3_hi"), 1)
            pe.wait_ge(sem("q3_lo"), 1)
            pe.wait_ge(sem("ld_identb"), 16)
            pe.wait_ge(sem("ld_tail"), 16 * 2 * RING)
            pe.wait_ge(sem("v_set"), 8)

            def stack_queries(g):
                if g == 0:
                    pe.wait_ge(sem("rt_max"), 1)
                elif g == 1:
                    pe.wait_ge(sem("qs"), 2)
                elif g >= 3:
                    pe.wait_ge(sem("oq"), g - 2)
                if g >= 2:
                    pe.wait_ge(sem("qt"), 2 * (g - 1))
                for a in range(3):
                    ins = mm(bank(7)[:, 0:256], sel[:, g, a, :], qp[:, a, :], start=(a == 0), stop=(a == 2))
                ins.then_inc(sem("stack_ps"), 1)

            def stack_queries_max(g):
                pe.wait_ge(sem("mt"), g + 1)
                pe.wait_ge(sem("qs"), min(2 * (g + 2), 2 * G))
                if g >= 2:
                    pe.wait_ge(sem("oq"), g - 1)
                for a in range(3):
                    mm(bank(7)[:, 0:256], sel[:, g, a, :], qp[:, a, :], start=(a == 0), stop=(a == 2))
                for b in range(B):
                    ins = mm(bank(7)[:, 128 * b:128 * b + 128], mt[:, g % 2, b, :], identb[:, :], start=False,
                             stop=True, skip_group_check=True)
                ins.then_inc(sem("stackm_ps"), 1)

            def pair_rows(g, b):
                pe.wait_ge(sem("o_rows"), 2 * g + b + 1)
                if b == 0:
                    if g + 1 < G:
                        pe.wait_ge(sem("qt"), 2 * (g + 2))
                    elif G >= 2:
                        pe.wait_ge(sem("oq"), G - 1)
                for e in range(2):
                    ins = mm(bank(7)[:, VW * b + (DH + 1) * e:VW * b + (DH + 1) * (e + 1)],
                             O[:, b, S * e:S * e + S], w("cst", "R")[:, (DH + 1) * e:(DH + 1) * (e + 1)])
                ins.then_inc(sem("oq_ps"), 1)

            def wide_attention(masked):
                def score(m):
                    g, b, e, c = m // 16, m // 8 % 2, m // 4 % 2, m % 4
                    if m % 16 == 0:
                        pe.wait_ge(sem("qs"), 2 * g + 2)
                        if g < RING:
                            if g == 0:
                                pe.wait_ge(sem("k_in0"), 16 * 2 * NBLK)
                                pe.wait_ge(sem("k_in1"), 16 * 2 * NBLK)
                        else:
                            for bb in range(B):
                                pe.wait_ge(sem(f"k_in{2 + (g - RING) * 2 + bb}"), 16 * 2 * NBLK)
                    if m >= 2:
                        pe.wait_ge(sem("s_red"), m - 1)
                    ins = mm(bank(m % 2), qs[:, g % 2, e, b, :], kst[:, g % RING, b, 512 * c:512 * c + 512],
                             stop=not masked)
                    if masked:
                        ins = mm(bank(m % 2), identb[:, :], mb[:, b, 512 * c:512 * c + 512], start=False)
                    ins.then_inc(sem("s_done"), 1)

                def score_t(n):
                    g, b, u = n // 8, n // 4 % 2, n % 4
                    if n >= 2:
                        pe.wait_ge(sem("p3"), n - 1)
                    if n % 8 == 0:
                        pe.wait_ge(sem("qt"), 2 * g + 2)
                    for c in range(4):
                        k = 128 * (4 * u + c)
                        to = bank(2 + 2 * (n % 2), 2)[:, 256 * c:256 * c + 256]
                        ins = mm(to, kst[:, g % RING, b, k:k + 128],
                                 qt[:, g % 2, b, :, :].rearrange("p e q -> p (e q)"), stop=not masked)
                        if masked:
                            ins = mm(to.rearrange("p (e q) -> p e q", e=2), identb[:, :],
                                     mbT[:, b, 4 * u + c, :].unsqueeze(1).to_broadcast([128, 2, S]), start=False)
                    ins.then_inc(sem("st_done"), 1)

                def weigh_values(n):
                    g, b, u = n // 8, n // 4 % 2, n % 4
                    pe.wait_ge(sem("p3"), n + 1)
                    if n == 0:
                        pe.wait_ge(sem("flag"), 1)
                    elif u == 0:
                        pe.wait_ge(sem("o_rows"), 2 * g + b)
                    for c in range(4):
                        ins = mm(bank(6)[32 * c:32 * c + 32, 0:256], value(b, 4 * u + c, g),
                                 pt_ring[:, n % 4, 256 * c:256 * c + 256], start=(u == 0), stop=(u == 3),
                                 tile_position=(0, 32 * c))
                    ins.then_inc(sem("pv_done"), 1)

                m = 0
                while m < 16:
                    score(m)
                    m += 1
                stack_queries(1)
                while m < 16 + S_LEAD:
                    score(m)
                    m += 1
                stack_queries_max(0)
                for n in range(8 * G):
                    g, j = n // 8, n % 8
                    if j == 2 and g:
                        pair_rows(g - 1, 0)
                        pair_rows(g - 1, 1)
                    if j == 4 and g + 2 < G:
                        stack_queries(g + 2)
                    if j == 7 and g + 1 < G:
                        stack_queries_max(g + 1)
                    score_t(n)
                    for _ in range(2):
                        if m < 16 * G:
                            score(m)
                            m += 1
                    if n:
                        weigh_values(n - 1)
                weigh_values(8 * G - 1)
                pair_rows(G - 1, 0)
                pair_rows(G - 1, 1)

            stack_queries(0)
            pe.wait_ge(sem("flag"), 1)
            any_masked = pe.value_load(flag[0:1, 0:1], min_val=0, max_val=1)
            with pe.If(any_masked != 0):
                wide_attention(True)
            with pe.Else():
                wide_attention(False)
            for b in range(B):
                pe.wait_ge(sem("att3"), 1)
                ins = pe.transpose(bank(0)[:, 128 * b:128 * b + 128], ob[:, b, :], ident)
            ins.then_inc(sem("turn_ps"), 1)
            pe.wait_ge(sem("turned"), 4)
            for b in range(B):
                q = slice(128 * b, 128 * b + 128)
                ins = mm(bank(1)[:, q], att3T[:, q], w("wE", "o"))
            ins.then_inc(sem("part_ps"), 1)

            ln_turn(4)
            pe.wait_ge(sem("ld_wF"), 16)
            pe.wait_ge(sem("ln_hT"), 5)
            for j, name in enumerate(("qa", "qb", "ka", "kb")):
                ins = mm(bank(j // 2)[:, 256 * (j % 2):256 * (j % 2) + 256], w("wF", name), hT[4][:, :])
            ins.then_inc(sem("qk4_ps"), 1)
            for b in range(B):
                ins = mm(bank(2)[:, 256 * b:256 * b + 256], hT[4][:, 128 * b:128 * b + 128], w("wF", "v"))
            ins.then_inc(sem("v4_ps"), 1)
            pe.wait_ge(sem("rotated"), 4)
            pe.wait_ge(sem("vt4"), 4)
            for b in range(B):
                pe.wait_ge(sem(f"kbd{b}"), 1)
                for j in range(4):
                    ins = mm(bank(4 * b + j), qr4[:, 128 * b:128 * b + 128],
                             kbd[:, b, 4 * j:4 * j + 4, :].rearrange("p h k -> p (h k)"))
                ins.then_inc(sem("s4_ps"), 1)
            for n in range(8):
                b, j = n // 4, n % 4
                if j == 0:
                    pe.wait_ge(sem("probs"), b + 1 + 4)
                if n >= 2:
                    pe.wait_ge(sem("p4T_dve") if n % 2 == 0 else sem("p4T_act"), n // 2)
                for i in range(4):
                    ins = pe.transpose(bank(n % 2)[:, 128 * i:128 * i + 128], sc4[:, b, 4 * j + i, :], ident)
                ins.then_inc(sem("p4T_ps"), 1)
            pe.wait_ge(sem("v4"), 2)
            pe.wait_ge(sem("p4T_dve"), 4)
            pe.wait_ge(sem("p4T_act"), 4)
            for b in range(B):
                for quad in range(4):
                    for j in range(4):
                        hd = 4 * quad + j
                        ins = mm(bank(2 + b)[32 * j:32 * j + 32, 128 * quad:128 * quad + 128], v4[:, b, hd, :],
                                 pT4[:, b, hd, :], tile_position=(0, 32 * j))
                ins.then_inc(sem("o4_ps"), 1)
            for b in range(B):
                pe.wait_ge(sem("o4"), b + 1)
                if b == 0:
                    pe.wait_ge(sem("sub4"), 2)
                for quad in range(4):
                    ins = pe.transpose(bank(4 + b)[:, 128 * quad:128 * quad + 128],
                                       o4[:, b, 128 * quad:128 * quad + 128], ident)
                ins.then_inc(sem("o4T_ps"), 1)
            pe.wait_ge(sem("r4"), 1)
            for b in range(B):
                ins = pe.transpose(bank(6)[:, 128 * b:128 * b + 128], r4[:, 2, b, :], ident)
            ins.then_inc(sem("turn_ps"), 1)
            pe.wait_ge(sem("turned"), 5)
            for b in range(B):
                q = slice(128 * b, 128 * b + 128)
                ins = mm(bank(7)[:, q], r4T[:, q], w("wF", "o"))
            ins.then_inc(sem("part_ps"), 1)

            ln_turn(5)
            pe.wait_ge(sem("ld_wG"), 16)
            pe.wait_ge(sem("ln_hT"), 6)
            pe.wait_ge(sem("x_ready"), 7)
            for b in range(B):
                ins = mm(bank(7)[:, 256 + 8 * b:264 + 8 * b], hT[5][:, 128 * b:128 * b + 128], w("wG", "r"))
            ins.then_inc(sem("router_ps"), 1)
            pe.wait_ge(sem("o4"), 2)
            for c in range(FC):
                mm(bank(c)[:, 0:256], w("wG", "w1")[:, 128 * c:128 * c + 128], hT[5][:, :]).then_inc(sem("hidden_ps"), 1)
            pe.wait_ge(sem("rw"), 1)
            for b in range(B):
                ins = pe.transpose(bank(5)[0:NE, 128 * b:128 * b + 128], rt[:, 1, 112 + 8 * b:120 + 8 * b], ident)
            ins.then_inc(sem("rwT_ps"), 1)
            pe.wait_ge(sem("rsel"), 1)
            pe.wait_ge(sem("ld_b2e"), 32)
            for c in range(FC):
                ins = mm(bank(6 if c < 2 else 4)[:, 256 * (c % 2):256 * (c % 2) + 256], E8[:, 128 * c:128 * c + 128],
                         rsel[:, :])
                if c % 2:
                    ins.then_inc(sem("rx_ps"), 1)
            pe.wait_ge(sem("gelu"), FC + 4)
            for b in range(B):
                q = slice(128 * b, 128 * b + 128)
                o = bank(2 + b)[:, 256:384]
                mm(o, rsel[:, q], b2e[:, :], start=True, stop=False)
                for c in range(FC):
                    pe.wait_ge(sem("gw"), c + 1)
                    ins = mm(o, gw[:, c, q], w("wG", "w2")[:, 128 * c:128 * c + 128], start=False, stop=(c == FC - 1))
                ins.then_inc(sem("part_ps"), 1)


def constants():
    f = np.float32
    cst = {"ident": np.eye(128, dtype=f)}
    half = D // 2
    inv = f(1.0) / f(10000.0) ** (np.arange(half, dtype=f) / f(half))
    ang = np.arange(S, dtype=f)[:, None] * inv[None, :].astype(f)
    cos, sin = np.cos(ang).astype(f).T, np.sin(ang).astype(f).T
    cst["cos"] = np.concatenate([cos, cos])
    cst["sin"] = np.concatenate([-sin, sin])
    theta = f(10000.0) ** (-np.arange(0, DH, 2, dtype=f) / f(DH))
    fr = np.arange(S, dtype=f)[:, None] * theta[None, :].astype(f)
    rope = np.concatenate([np.cos(fr), np.sin(fr)], axis=1).astype(f)
    c, s = rope[:, ::2], rope[:, 1::2]
    va, vb = np.concatenate([c, s], 1), np.concatenate([-s, c], 1)
    cst["va"], cst["vb"], cst["na"], cst["nb"] = va, vb, -va, -vb
    cst["A"], cst["B"] = np.tile(va.T, (H, 1)), np.tile(vb.T, (H, 1))
    feat = np.arange(128)
    cst["hm"] = (feat[:, None] // DH == np.arange(H)[None, :]).astype(f)
    R = np.zeros((128, VW), f)
    for j in range(4):
        for i in range(VW):
            R[32 * j + i, i] = 1.0
    cst["R"] = R
    sel = np.zeros((128, G, 3, 128), f)
    for g in range(G):
        for e in range(2):
            for blk, a in enumerate(Q_PARTS):
                for d in range(DH):
                    sel[(2 * g + e) * DH + d, g, a, 64 * e + DH * blk + d] = 1.0
    tail = np.zeros((64 - MAX_ROW, B * SK), f)
    tail[0:3] = 1.0
    E8 = np.repeat(np.eye(NE, dtype=f), FC * D // NE, axis=1)
    return cst, sel.reshape(128, -1), tail, E8


def kernel(**inp):
    import ml_dtypes
    import concourse.bacc as bacc
    from concourse.bass_utils import run_bass_kernel_spmd

    a = {k: np.asarray(v) for k, v in inp.items()}
    bf = ml_dtypes.bfloat16
    cst, sel, tail, E8 = constants()

    def blocks(m):
        return np.concatenate([m[128 * i:128 * (i + 1)] for i in range(m.shape[0] // 128)], axis=1)

    def col(x):
        return x.reshape(-1, 1)

    wq, wk, wv = (a["L0_attn_w_qkv"][i * D:(i + 1) * D] for i in range(3))
    bq, bk, bv = (a["L0_attn_b_qkv"][i * D:(i + 1) * D] for i in range(3))
    swap = (np.arange(D) + D // 2) % D
    hj = np.arange(D)
    pa = (hj // DH) * DH + 2 * (hj % (DH // 2))
    pb = pa + 1
    w1e = np.concatenate(list(a["L1_ffn_W1"]), axis=1)
    w2e = np.concatenate(list(a["L1_ffn_W2"]), axis=0)
    fields = {
        "wA": dict(wl=blocks(a["L0_xattn_W_l"].T), w_cq=col(a["L0_xattn_w_cq"]), w_q=col(a["L0_xattn_w_q"]),
                   w_c=col(a["L0_xattn_w_c"])),
        "wB": dict(wk=a["L1_xattn_Wk"].T, wv=a["L1_xattn_Wv"].T, bk=col(a["L1_xattn_bk"])),
        "wC": dict(q=wq.T, qs=wq[swap].T, k=wk.T, ks=wk[swap].T, v=wv.T, iq=a["L0_attn_w_iq"].T,
                   ik=np.concatenate([a["L0_attn_w_ik"].T] * 2, axis=1), iw=a["L0_attn_w_iw"].T,
                   o=a["L0_attn_w_o"].T, bq=col(bq), bqs=col(bq[swap]), bk=col(bk), bks=col(bk[swap]),
                   biq=a["L0_attn_b_iq"].reshape(2, D).T, bik=col(np.concatenate([a["L0_attn_b_ik"]] * 2))),
        "wD": dict(r=a["L0_ffn_router_w"], w1=a["L0_ffn_w1"], w2=blocks(a["L0_ffn_w2"]),
                   b1=a["L0_ffn_b1"].reshape(FC, D).T),
        "wE": dict(q=a["L1_xattn_Wq"].T, o=a["L1_xattn_Wo"].T, bq=col(a["L1_xattn_bq"])),
        "wF": dict(qa=a["L1_attn_Wq"][pa].T, qb=a["L1_attn_Wq"][pb].T, ka=a["L1_attn_Wk"][pa].T,
                   kb=a["L1_attn_Wk"][pb].T,
                   v=np.concatenate([a["L1_attn_Wv"][pa].T, a["L1_attn_Wv"][pb].T], axis=1),
                   o=a["L1_attn_Wo"].T, bqa=col(a["L1_attn_bq"][pa]), bqb=col(a["L1_attn_bq"][pb]),
                   bka=col(a["L1_attn_bk"][pa]), bkb=col(a["L1_attn_bk"][pb])),
        "wG": dict(r=a["L1_ffn_router_w"], w1=w1e, w2=blocks(w2e), b1=a["L1_ffn_b1"].reshape(FC, D).T),
        "cst": cst,
    }
    arrays = {}
    for name, order in PACKS.items():
        arrays[name] = np.concatenate([fields[name][f] for f, _ in order], axis=1)
    rows = dict(b3=np.concatenate([a[f"L0_xattn_b_{k}"].reshape(1) for k in ("c", "q", "cq")]),
                b_l=a["L0_xattn_b_l"], a0_bv=bv, b_iw=a["L0_attn_b_iw"], a0_bo=a["L0_attn_b_o"],
                f0_b2=a["L0_ffn_b2"], x1_bv=a["L1_xattn_bv"], x1_bo=a["L1_xattn_bo"],
                a1_bv=np.concatenate([a["L1_attn_bv"][pa], a["L1_attn_bv"][pb]]), a1_bo=a["L1_attn_bo"],
                f1_rb=a["L1_ffn_router_b"])
    arrays["rows"] = np.concatenate([rows[f] for f, _ in ROWS]).reshape(1, -1)
    arrays["x"] = a["x"]
    arrays["ctx"] = a["ctx_1024"]
    arrays["ctxT"] = a["ctx_1024"].transpose(0, 2, 1)
    arrays["mask"] = a["mask_BxSxS2_if1"]
    arrays["maskT"] = a["mask_BxSxS2_if1"].transpose(0, 2, 1)
    arrays["b2e"] = a["L1_ffn_b2"]
    arrays["E8"] = E8
    arrays["identb"] = np.eye(128, dtype=bf)
    arrays["sel"] = sel.astype(bf)
    arrays["tail"] = tail.astype(bf)
    arrays = {f"in_{k}": np.ascontiguousarray(x) for k, x in arrays.items()}

    nc = bacc.Bacc("TRN2", target_bir_lowering=False, num_devices=1)
    A = {k[3:]: nc.dram_tensor(k, x.shape, mybir.dt.from_np(x.dtype), kind="ExternalInput").ap()
         for k, x in arrays.items()}
    out = nc.dram_tensor("out_dram", (B, S, D), F32, kind="ExternalOutput").ap()
    build(nc, A, out)
    r = run_bass_kernel_spmd(nc, [arrays], core_ids=[0])
    return r.results[0]["out_dram"]
```

```python
from contextlib import ExitStack

import numpy as np

import concourse.bass as bass
from concourse import mybir

F32 = mybir.dt.float32
BF16 = mybir.dt.bfloat16
I32 = mybir.dt.int32
ALU = mybir.AluOpType
ACT = mybir.ActivationFunctionType
AX = mybir.AxisListType

B, S, D, SK = 2, 128, 128, 2048
H, DH = 16, 8
G = H // 2
CH = SK // 128
IH, TOPK = 4, 32
NE = 8
FC = 4
EPS = 1e-5
MASK_BIG = float(2.0 ** 100)
GONE = -3.0e38
VW = 2 * (DH + 1)
RING = 4
UNITS = B * G
KEY_BANK = (5, 6) + (6, 7) * 3
S_LEAD = 6

K_PARTS = (0, 1, 2, 0, 1, 0)
Q_PARTS = (0, 0, 0, 1, 1, 2)
NBLK = len(K_PARTS)
MAX_ROW = NBLK * DH

ROWS = (("b3", 3), ("b_l", D), ("a0_bv", D), ("b_iw", IH), ("a0_bo", D), ("f0_b2", D), ("x1_bv", D), ("x1_bo", D),
        ("a1_bv", 2 * D), ("a1_bo", D), ("f1_rb", NE))
PACKS = {
    "wA": (("wl", 4 * D), ("w_cq", 1), ("w_q", 1), ("w_c", 1)),
    "wB": (("wk", D), ("wv", D), ("bk", 1)),
    "wC": (("q", D), ("qs", D), ("k", D), ("ks", D), ("v", D), ("iq", 2 * D), ("ik", D), ("iw", IH), ("o", D),
           ("bq", 1), ("bqs", 1), ("bk", 1), ("bks", 1), ("biq", 2), ("bik", 1)),
    "wD": (("r", NE), ("w1", FC * D), ("w2", FC * D), ("b1", FC)),
    "wE": (("q", D), ("o", D), ("bq", 1)),
    "wF": (("qa", D), ("qb", D), ("ka", D), ("kb", D), ("v", 2 * D), ("o", D),
           ("bqa", 1), ("bqb", 1), ("bka", 1), ("bkb", 1)),
    "wG": (("r", NE), ("w1", FC * D), ("w2", FC * D), ("b1", FC)),
    "cst": (("ident", D), ("cos", S), ("sin", S), ("A", S), ("B", S), ("va", DH), ("vb", DH), ("na", DH), ("nb", DH),
            ("hm", H), ("R", VW)),
}


def offsets(fields):
    at, out = 0, {}
    for name, n in fields:
        out[name] = (at, at + n)
        at += n
    return out, at


def build(nc, A, out):
    rows_at, n_rows = offsets(ROWS)
    with ExitStack() as ctx:
        def sb(name, shape, dt=F32):
            return ctx.enter_context(nc.sbuf_tensor(name, shape, dt))

        names = {}

        def sem(name):
            if name not in names:
                names[name] = ctx.enter_context(nc.semaphore(name))
            return names[name]

        packs, at = {}, {}
        for name, fields in PACKS.items():
            at[name], n = offsets(fields)
            packs[name] = sb(name, [128, n])

        def w(pack, field):
            a, b = at[pack][field]
            return packs[pack][:, a:b]

        rows = sb("rows", [128, n_rows])

        def row(field):
            a, b = rows_at[field]
            return rows[:, a:b]

        X = [sb(f"x{i}", [128, B, D]) for i in range(7)]
        XB = [sb(f"xb{i}", [128, B, D]) for i in range(2)] * 3
        h = [sb(f"h{i}", [128, B, D]) for i in range(2)] * 3
        hT = [sb(f"hT{i}", [128, B * S]) for i in range(2)] * 3
        stats = sb("stats", [128, 6, B, 6])
        mv = sb("mv", [128, 6, B, 2])
        veps = sb("veps", [128, 6, B])
        rstd = sb("rstd", [128, 6, B])
        half = sb("half", [128, B])
        identb = sb("identb", [128, 128], BF16)
        sel = sb("sel", [128, G, 3, 128], BF16)
        ctxT = sb("ctxT", [128, B, SK])
        ctxN = sb("ctxN", [128, B, CH, D])
        kparts = sb("kparts", [128, 3, B, SK], BF16)
        kst = sb("kst", [128, RING, B, SK], BF16)
        kres = sb("kres", [128, 2, 512])
        vext = sb("vext", [128, B * CH * G * VW + 32 - VW])
        P0 = sb("P0", [128, B, SK])
        PT0 = sb("PT0", [128, B, SK])
        ident = w("cst", "ident")

        mask_q = P0[:, :, :].rearrange("p b k -> p (b k)").bitcast(I32)
        mask_k = PT0[:, :, :].rearrange("p b k -> p (b k)").bitcast(I32)
        mb = ctxN[:, 0, :, :].rearrange("p c d -> p (c d)").bitcast(BF16).rearrange("p (b k) -> p b k", b=B)
        mbT = ctxN[:, 1, :, :].rearrange("p c d -> p (c d)").bitcast(BF16).rearrange(
            "p (b c q) -> p b c q", b=B, c=CH)
        pt_ring = PT0[:, :, :].rearrange("p b k -> p (b k)").rearrange("p (r n) -> p r n", r=4)
        late = kparts[:, :, :, :].rearrange("p a b k -> p (a b k)").bitcast(F32)
        cut = [0]

        def lt(n):
            cut[0] += n
            return late[:, cut[0] - n:cut[0]]

        cm = sb("cm", [128, B * S])
        mx0 = sb("mx0", [128, B])
        den0 = sb("den0", [128, B])
        rden0 = sb("rden0", [128, B])
        pm0 = sb("pm0", [128, B, 4])
        cwc = sb("cwc", [128, B])
        after_keys = P0[:, 0, 0:1024]
        c2q = after_keys[:, 0:256].rearrange("p (b d) -> p b d", b=B)
        c2qT, x3T, x4T = (after_keys[:, 256 * i:256 * (i + 1)] for i in range(1, 4))
        b3 = sb("b3", [128, 1])
        rowmax = sb("rowmax", [128, B])
        rmT = sb("rmT", [B, 128])
        rsm = sb("rsm", [B, 4])
        erow = sb("erow", [B, 128])
        brow = sb("brow", [B, 128])
        batt = sb("batt", [128, B])
        q2c = sb("q2c", [128, B])
        t_region = lt(1024)
        t1, t2, t3, t4 = (t_region[:, 256 * i:256 * (i + 1)] for i in range(4))
        qr, kr = lt(256), lt(256)
        iqT, ikT = lt(512), lt(256)
        V = lt(256).rearrange("p (b d) -> p b d", b=B)
        relu_region = lt(1024)
        relu = relu_region.rearrange("p (r b i k) -> p r b i k", r=2, b=B, i=IH // 2)
        idx = [lt(256).rearrange("p (b k) -> p b k", b=B) for _ in range(2)]
        keep = lt(256).rearrange("p (b k) -> p b k", b=B)
        lg = lt(256).rearrange("p (b k) -> p b k", b=B)
        Pm = lt(256).rearrange("p (b k) -> p b k", b=B)
        PmT, aT = lt(256), lt(256)
        iw = sb("iw", [128, B, IH])
        m8 = sb("m8", [128, B, TOPK // 8, 8])
        nmx1 = sb("nmx1", [128, B])
        den1 = sb("den1", [128, B])
        rden1 = sb("rden1", [128, B])
        g0 = relu_region.rearrange("p (c t) -> p c t", c=FC)
        g5 = g0
        gw = t_region.rearrange("p (c t) -> p c t", c=FC)
        rt = sb("rt", [128, 2, 160])
        rsel = sb("rsel", [8, 256])
        E8 = sb("E8", [NE, FC * D])
        b2e = sb("b2e", [NE, D])
        ob = sb("ob", [128, B, D])
        qp = sb("qp", [128, 3, B * S], BF16)
        cut[0] = 4 * 256
        O = lt(512).rearrange("p (b n) -> p b n", b=B)
        qres, att3T, r4T = lt(256), lt(256), lt(256)
        att3 = lt(256).rearrange("p (b h n) -> p b h n", b=B, h=H)
        assert cut[0] == 4 * 256 + 6 * 256
        cut[0] += 4 * 256
        v4 = lt(1024).rearrange("p (b h n) -> p b h n", b=B, h=H)
        qr4, kr4 = lt(256), lt(256)
        n4 = lt(256).rearrange("p (b d) -> p b d", b=B)
        r4 = lt(768).rearrange("p (u b d) -> p u b d", u=3, b=B)
        qs = sb("qs", [128, 2, 2, B, S], BF16)
        qt = sb("qt", [128, 2, B, 2, S], BF16)
        mt = sb("mt", [128, 2, B, 128], BF16)
        pmx = sb("pmx", [128, 2, 4, 4])
        nmx3 = sb("nmx3", [128, 2, 4])
        mres = sb("mres", [128, 2, 4])
        oq = sb("oq", [128, B, G, 2, DH + 1])
        rd3 = sb("rd3", [128, B, H])
        flagf = sb("flagf", [1, 1])
        flag = sb("flag", [1, 1], I32)
        onesb = sb("onesb", [128, 1], BF16)
        kbd = ctxT[:, :, :].rearrange("p b (h k) -> p b h k", h=H)
        sc4 = P0[:, :, :].rearrange("p b (h k) -> p b h k", h=H)
        pT4 = PT0[:, :, :].rearrange("p b (h q) -> p b h q", h=H)
        va4 = kst[:, 0, 0, :].bitcast(F32).rearrange("p (b n) -> p b n", b=B)
        vt4 = kst[:, 0, 1, :].bitcast(F32).rearrange("p (u b n) -> p u b n", u=4, b=B)
        mx4 = sb("mx4", [128, B, H])
        o4 = kst[:, 1, :, :].bitcast(F32)
        rd4 = rd3

        PS = ctx.enter_context(nc.psum_tensor("psum", [128, 8 * 512], F32))

        def bank(i, n=1):
            return PS[:, 512 * i:512 * (i + n)]

        kdram = nc.dram_tensor("k_parts_dram", [3, 128, B, SK], BF16, kind="Internal").ap()

        def value(b, c, g):
            o = ((b * CH + c) * G + g) * VW
            return vext[:, o:o + 32]

        block = ctx.enter_context(nc.Block())

        @block.sync
        def _(sp):
            sp.dma_start(X[0][:, :, :], A["x"].rearrange("b s d -> s b d")).then_inc(sem("ld_x"), 16)
            sp.dma_start(packs["cst"][:, :], A["cst"]).then_inc(sem("ld_cst"), 16)
            for i in range(4):
                b, k = i // 2, (i % 2) * 1024
                sp.dma_start(ctxT[:, b, k:k + 1024], A["ctxT"][b, :, k:k + 1024]).then_inc(sem(f"ld_ctxT{i}"), 16)
                if i == 0:
                    sp.dma_start(packs["wB"][:, :], A["wB"]).then_inc(sem("ld_wB"), 16)
            for b in range(B):
                sp.dma_start(ctxN[:, b, :, :], A["ctx"][b].rearrange("(c k) d -> k c d", k=128)).then_inc(
                    sem(f"ld_ctxN{b}"), 16)
            for name in ("wC", "wD", "wE"):
                sp.dma_start(packs[name][:, :], A[name]).then_inc(sem("ld_" + name), 16)
            sp.dma_start(sel[:, :, :, :].rearrange("p g a r -> p (g a r)"), A["sel"]).then_inc(sem("ld_sel"), 16)
            for b in range(B):
                sp.wait_ge(sem("k_hi"), 4 * b + 4)
                sp.wait_ge(sem("k_mid"), 4 * b + 4)
                sp.wait_ge(sem("k_lo"), 4 * b + 4)
                for a in range(3):
                    sp.dma_start(kdram[a, :, b, :], kparts[:, a, b, :]).then_inc(sem(f"k_out{b}"), 16)
            for e in range(2):
                for r in range(RING):
                    sp.dma_start(kst[64 * e + MAX_ROW:64 * e + 64, r, :, :].rearrange("p b k -> p (b k)"),
                                 A["tail"]).then_inc(sem("ld_tail"), 16)

            def stack(g0_, n, b, to):
                for blk in range(NBLK):
                    for e in range(2):
                        src = kdram[K_PARTS[blk], :, b, :].rearrange("(g e d) k -> e d g k", e=2, d=DH)[
                            e, :, g0_:g0_ + n, :]
                        r = g0_ % RING
                        dst = kst[64 * e + DH * blk:64 * e + DH * (blk + 1), r:r + n, b, :]
                        sp.dma_start(dst, src).then_inc(to, 16)

            for b in range(B):
                sp.wait_ge(sem(f"k_out{b}"), 48)
                stack(0, RING, b, sem(f"k_in{b}"))
            for name in ("wF", "wG"):
                sp.dma_start(packs[name][:, :], A[name]).then_inc(sem("ld_" + name), 16)
            sp.dma_start(E8[:, :], A["E8"]).then_inc(sem("ld_b2e"), 16)
            sp.dma_start(b2e[:, :], A["b2e"]).then_inc(sem("ld_b2e"), 16)
            for g in range(RING, G):
                sp.wait_ge(sem("st_done"), 8 * (g - RING + 1))
                for b in range(B):
                    stack(g, 1, b, sem(f"k_in{2 + (g - RING) * 2 + b}"))
            sp.wait_ge(sem("out_ready"), 2)
            sp.dma_start(out.rearrange("b s d -> s b d"), X[6][:, :, :]).then_inc(sem("stored"), 16)
            sp.wait_ge(sem("stored"), 16)

        @block.gpsimd
        def _(pool):
            pool.memset(half[:, :], -0.5).then_inc(sem("half"), 1)

            def ln_power(i):
                pool.wait_ge(sem("ln_mv"), 2 * (i + 1))
                pool.tensor_scalar(veps[:, i, :], mv[:, i, :, 1], EPS, None, ALU.add).then_inc(sem("ln_veps"), 1)
                pool.wait_ge(sem("ln_veps"), i + 1)
                pool.wait_ge(sem("half"), 1)
                pool.tensor_tensor(rstd[:, i, :], veps[:, i, :], half[:, :], ALU.pow).then_inc(sem("ln_rstd"), 1)

            ln_power(0)
            pool.memset(onesb[:, :], 1.0).then_inc(sem("onesb"), 1)
            for i in range(8):
                b, k = i // 4, (i % 4) * 512
                pool.wait_ge(sem("k_mid"), i + 1)
                pool.tensor_tensor(kparts[:, 2, b, k:k + 512], kres[:, i % 2, :], kparts[:, 1, b, k:k + 512],
                                   ALU.subtract).then_inc(sem("k_lo"), 1)
            pool.memset(vext[:, :], 1.0).then_inc(sem("v_ones"), 1)
            ln_power(1)
            pool.memset(mt[:, :, :, :], 0.0).then_inc(sem("zeros"), 1)
            pool.memset(qs[:, :, :, :, :], 0.0).then_inc(sem("zeros"), 1)
            pool.memset(qt[:, :, :, :, :], 0.0).then_inc(sem("zeros"), 1)
            ln_power(2)
            ln_power(3)
            pool.memset(v4, 0.0).then_inc(sem("v4_set"), 1)
            pool.wait_ge(sem("v4_set"), 1)
            pool.memset(v4[:, :, :, DH:DH + 1], 1.0).then_inc(sem("v4_set"), 1)

            def max_parts(u):
                g, b = u // B, u % B
                pool.wait_ge(sem("nmx3"), u + 1)
                if u >= 2 * B:
                    pool.wait_ge(sem("stackm_ps"), u - 2 * B + 1)
                at_part = [mt[:, g % 2, b, :].rearrange("p (e m) -> p e m", e=2)[:, :, MAX_ROW + a]
                           for a in range(3)]
                nm, mr = nmx3[:, g % 2, 2 * b:2 * b + 2], mres[:, g % 2, 2 * b:2 * b + 2]
                pool.tensor_copy(at_part[0], nm).then_inc(sem("mt_part"), 1)
                pool.wait_ge(sem("mt_part"), 3 * u + 1)
                pool.tensor_tensor(mr, nm, at_part[0], ALU.subtract).then_inc(sem("mt_part"), 1)
                pool.wait_ge(sem("mt_part"), 3 * u + 2)
                pool.tensor_copy(at_part[1], mr).then_inc(sem("mt_part"), 1)
                pool.wait_ge(sem("mt_part"), 3 * u + 3)
                pool.tensor_tensor(at_part[2], mr, at_part[1], ALU.subtract).then_inc(sem("mt"), 1)

            pool.wait_ge(sem("zeros"), 3)
            for u in range(UNITS):
                max_parts(u)
            ln_power(4)
            pool.wait_ge(sem("rotated4"), 1)
            for n in range(2, 8):
                b, hs = n // 4, slice(4 * (n % 4), 4 * (n % 4) + 4)
                pool.tensor_tensor(kbd[:, b, hs, :],
                                   kr4[:, 128 * b:128 * b + 128].unsqueeze(1).to_broadcast([128, 4, 128]),
                                   w("cst", "hm")[:, hs].unsqueeze(2).to_broadcast([128, 4, 128]),
                                   ALU.mult).then_inc(sem("kbd_pool"), 1)
            pool.wait_ge(sem("va4"), 1)
            pool.wait_ge(sem("ld_rows"), 16)
            pool.tensor_tensor(va4[:, :, 0:256], va4[:, :, 0:256],
                               row("a1_bv").unsqueeze(1).to_broadcast([128, B, 2 * D]), ALU.add).then_inc(
                sem("vb4"), 1)
            pool.wait_ge(sem("vb4"), 1)

            def by_head(ap):
                return ap.rearrange("p b (h n) -> p b h n", h=H)

            for u, tab in ((0, "va"), (1, "vb")):
                pool.tensor_tensor(by_head(vt4[:, u, :, :]), by_head(va4[:, :, D * u:D * (u + 1)]),
                                   w("cst", tab).unsqueeze(1).unsqueeze(1).to_broadcast([128, B, H, DH]),
                                   ALU.mult).then_inc(sem("vt4"), 1)
            pool.wait_ge(sem("vt4"), 2)
            pool.wait_ge(sem("v4_set"), 2)
            pool.tensor_tensor(v4[:, :, :, 0:DH], by_head(vt4[:, 0, :, :]), by_head(vt4[:, 1, :, :]),
                               ALU.add).then_inc(sem("v4"), 1)
            ln_power(5)

        @block.scalar
        def _(act):
            act.dma_start(packs["wA"][:, :], A["wA"]).then_inc(sem("ld_wA"), 16)
            act.dma_start(rows[:, :], A["rows"].to_broadcast([128, n_rows])).then_inc(sem("ld_rows"), 16)
            act.dma_start(identb[:, :], A["identb"]).then_inc(sem("ld_identb"), 16)
            act.preload_act_table(ACT.Exp)

            def ln_turned(i, src):
                act.wait_ge(sem("ln_hT_ps"), i + 1)
                act.activation(hT[i][:, :], src, ACT.Copy).then_inc(sem("ln_hT"), 1)

            ln_turned(0, bank(4)[:, 0:256])

            def key_hi(i):
                b, k = i // 4, (i % 4) * 512
                act.wait_ge(sem("k_ps"), i + 1)
                if i == 0:
                    act.wait_ge(sem("ld_wB"), 16)
                act.activation(kparts[:, 0, b, k:k + 512], bank(KEY_BANK[i]), ACT.Identity,
                               bias=w("wB", "bk")).then_inc(sem("k_hi"), 1)

            def probs0(b):
                act.wait_ge(sem("mx0"), b + 1)
                act.activation(P0[:, b, :], bank(4 * b, 4), ACT.Exp, bias=mx0[:, b:b + 1],
                               accum_out=den0[:, b:b + 1]).then_inc(sem("probs"), 1)

            def turned0(b, j):
                act.wait_ge(sem("pT_ps"), 4 * b + j + 1)
                act.activation(PT0[:, b, 512 * j:512 * (j + 1)], bank(1), ACT.Copy).then_inc(sem("pT_act"), 1)

            key_hi(0)
            key_hi(1)
            probs0(0)
            probs0(1)
            turned0(0, 1)
            key_hi(2)
            act.wait_ge(sem("rm_max"), 1)
            act.activation(erow[:, :], rmT[:, :], ACT.Exp, bias=rsm[:, 0:1], accum_out=rsm[:, 1:2]).then_inc(
                sem("erow"), 1)
            key_hi(3)
            turned0(0, 3)
            key_hi(4)
            turned0(1, 1)
            key_hi(5)
            turned0(1, 3)
            key_hi(6)
            key_hi(7)
            act.wait_ge(sem("turn_ps"), 1)
            act.activation(c2qT, bank(5)[:, 256:512], ACT.Copy).then_inc(sem("turned"), 1)
            act.wait_ge(sem("part_ps"), 1)
            for b in range(B):
                act.dma_start(mask_q.rearrange("p (b k) -> p b k", b=B)[:, b],
                              A["mask"][b]).then_inc(sem("ld_mask"), 16)
            for b in range(B):
                act.dma_start(mask_k.rearrange("p (b c q) -> p b c q", b=B, c=CH)[:, b],
                              A["maskT"][b].rearrange("(c k) q -> k c q", k=128)).then_inc(sem("ld_maskT"), 16)

            ln_turned(1, bank(4)[:, 0:256])
            act.wait_ge(sem("k_out0"), 48)
            act.wait_ge(sem("k_out1"), 48)
            act.wait_ge(sem("iq_ps"), 1)
            for j in range(2):
                act.activation(iqT[:, 256 * j:256 * (j + 1)], bank(2)[:, 256 * j:256 * (j + 1)], ACT.Identity,
                               bias=w("wC", "biq")[:, j:j + 1]).then_inc(sem("index_T"), 1)
            act.activation(ikT, bank(3)[:, 0:256], ACT.Identity, bias=w("wC", "bik")).then_inc(sem("index_T"), 1)
            for r in range(2):
                act.wait_ge(sem("hs_ps"), r + 1)
                act.activation(relu_region[:, 512 * r:512 * r + 512], bank(5 + r), ACT.Relu).then_inc(
                    sem("relu"), 1)
            act.wait_ge(sem("v_ones"), 1)
            for i in range(8):
                act.wait_ge(sem("v_ps"), i + 1)
                o = (4 * i) * G * VW
                act.activation(
                    vext[:, o:o + 4 * G * VW].rearrange("p (m n) -> p m n", n=DH + 1)[:, :, 0:DH],
                    bank(2 + i % 2).rearrange("p (m n) -> p m n", n=DH), ACT.Copy).then_inc(sem("v_set"), 1)
            for b in range(B):
                act.wait_ge(sem("nmx1"), b + 1)
                act.activation(Pm[:, b, :], lg[:, b, :], ACT.Exp, bias=nmx1[:, b:b + 1],
                               accum_out=den1[:, b:b + 1]).then_inc(sem("probs"), 1)
            act.preload_act_table(ACT.Gelu_apprx_tanh)
            act.wait_ge(sem("turn_ps"), 2)
            act.activation(PmT, bank(0)[:, 0:256], ACT.Copy).then_inc(sem("turned"), 1)
            act.wait_ge(sem("turn_ps"), 3)
            act.activation(aT, bank(1)[:, 0:256], ACT.Copy).then_inc(sem("turned"), 1)

            ln_turned(2, bank(4)[:, 0:256])
            for c in range(FC):
                act.wait_ge(sem("hidden_ps"), c + 1)
                act.activation(g0[:, c, :], bank(5 + c % 2)[:, 0:256], ACT.Gelu_apprx_tanh,
                               bias=w("wD", "b1")[:, c:c + 1]).then_inc(sem("gelu"), 1)
            act.preload_act_table(ACT.Exp)

            def router_exp(i):
                act.wait_ge(sem("rt_max"), i + 1)
                for b in range(B):
                    act.activation(rt[:, i, 8 * b:8 * b + 8], rt[:, i, 16 + 8 * b:24 + 8 * b], ACT.Exp,
                                   bias=rt[:, i, 32 + b:33 + b],
                                   accum_out=rt[:, i, 34 + b:35 + b]).then_inc(sem("rt_exp"), 1)

            router_exp(0)

            ln_turned(3, bank(4)[:, 0:256])
            act.wait_ge(sem("q3_ps"), 1)
            act.activation(qp[:, 0, :], bank(5)[:, 0:256], ACT.Identity, bias=w("wE", "bq")).then_inc(
                sem("q3_hi"), 1)

            def query_stack(g):
                act.wait_ge(sem("stack_ps"), g + 1)
                if g == 0:
                    act.wait_ge(sem("zeros"), 3)
                if g >= 2:
                    act.wait_ge(sem("s_done"), 16 * (g - 1))
                for e in range(2):
                    p = slice(64 * e, 64 * e + 64)
                    act.activation(qs[p, g % 2, e, :, :].rearrange("p b q -> p (b q)"), bank(7)[p, 0:256],
                                   ACT.Copy).then_inc(sem("qs"), 1)

            def query_stack_max(u):
                g, b = u // B, u % B
                act.wait_ge(sem("stackm_ps"), u + 1)
                if u >= 2 * B:
                    act.wait_ge(sem("st_done"), 4 * (u - 2 * B + 1))
                for e in range(2):
                    p = slice(64 * e, 64 * e + 64)
                    act.activation(qt[p, g % 2, b, e, :], bank(7)[p, 0:128], ACT.Copy).then_inc(sem("qt"), 1)

            def out_rows(g, b):
                act.wait_ge(sem("pv_done"), 8 * g + 4 * b + 4)
                if g >= 1:
                    act.wait_ge(sem("oq_ps"), 2 * g - 1 + b)
                act.activation(O[:, b, :], bank(6)[:, 0:256], ACT.Copy).then_inc(sem("o_rows"), 1)

            query_stack(0)
            query_stack(1)
            query_stack_max(0)
            for n in range(8 * G):
                g, j = n // 8, n % 8
                if j == 5 and g + 2 < G:
                    query_stack(g + 2)
                if n % 4 == 3 and n // 4 + 1 < UNITS:
                    query_stack_max(n // 4 + 1)
                act.wait_ge(sem("st_done"), n + 1)
                if n == 0:
                    act.wait_ge(sem("mask_bias"), 4)
                if n >= 4:
                    act.wait_ge(sem("pv_done"), n - 3)
                act.activation(pt_ring[:, n % 4, :], bank(2 + 2 * (n % 2), 2), ACT.Exp, scale=DH ** -0.5).then_inc(
                    sem("p3"), 1)
                if j == 4:
                    out_rows(g, 0)
                if j == 0 and g:
                    out_rows(g - 1, 1)
            out_rows(G - 1, 1)
            act.wait_ge(sem("turn_ps"), 4)
            act.activation(att3T[:, :], bank(0)[:, 0:256], ACT.Copy).then_inc(sem("turned"), 1)

            ln_turned(4, bank(4)[:, 0:256])
            act.wait_ge(sem("v4_ps"), 1)
            act.activation(va4[:, :, 0:256], bank(2).rearrange("p (b n) -> p b n", b=B), ACT.Copy).then_inc(
                sem("va4"), 1)

            def probs4(n):
                act.wait_ge(sem("p4T_ps"), n + 1)
                act.activation(pT4[:, n // 4, 4 * (n % 4):4 * (n % 4) + 4, :].rearrange("p h q -> p (h q)"),
                               bank(3 if n % 2 else 7), ACT.Copy).then_inc(sem("p4T"), 1)

            def out4(b):
                act.wait_ge(sem("o4_ps"), b + 1)
                act.activation(o4[:, b, 0:512], bank(b), ACT.Copy).then_inc(sem("o4"), 1)

            for n in range(8):
                b, hs = n // 4, slice(4 * (n % 4), 4 * (n % 4) + 4)
                act.wait_ge(sem("sub4"), n + 1)
                act.activation(sc4[:, b, hs, :], sc4[:, b, hs, :], ACT.Exp, scale=DH ** -0.5).then_inc(
                    sem("exp4"), 1)
                if n:
                    probs4(n - 1)
            out4(0)
            probs4(7)
            out4(1)
            act.wait_ge(sem("turn_ps"), 5)
            act.activation(r4T[:, :], bank(7)[:, 0:256], ACT.Copy).then_inc(sem("turned"), 1)

            ln_turned(5, bank(4)[:, 0:256])
            router_exp(1)
            act.preload_act_table(ACT.Gelu)
            for c in range(FC):
                act.wait_ge(sem("hidden_ps"), c + 1 + 4)
                act.activation(g5[:, c, :], bank(c)[:, 0:256], ACT.Gelu, bias=w("wG", "b1")[:, c:c + 1]).then_inc(sem("gelu"), 1)

        @block.vector
        def _(v):
            links = [0]

            def link(ins):
                links[0] += 1
                ins.then_inc(sem("dve_link"), 1)
                v.wait_ge(sem("dve_link"), links[0])

            def ln_stats(i):
                for b in range(B):
                    v.bn_stats(stats[:, i, b, :], X[i][:, b, :]).then_inc(sem("ln_stats"), 1)
                for b in range(B):
                    v.wait_ge(sem("ln_stats"), 2 * i + b + 1)
                    v.bn_aggr(mv[:, i, b, :], stats[:, i, b, :]).then_inc(sem("ln_mv"), 1)

            def ln_apply(i):
                v.wait_ge(sem("ln_mv"), 2 * i + 2)
                v.wait_ge(sem("ln_rstd"), i + 1)
                for b in range(B):
                    v.tensor_scalar(h[i][:, b, :], X[i][:, b, :], mv[:, i, b, 0:1], rstd[:, i, b:b + 1],
                                    ALU.subtract, ALU.mult).then_inc(sem("ln_h"), 1)

            def with_bias(i, name):
                v.tensor_tensor(XB[i][:, :, :], X[i][:, :, :], row(name).unsqueeze(1).to_broadcast([128, B, D]),
                                ALU.add).then_inc(sem("xb"), 1)

            v.wait_ge(sem("ld_x"), 16)
            ln_stats(0)
            ln_apply(0)
            v.wait_ge(sem("ld_rows"), 16)
            link(v.tensor_reduce(b3[:, :], row("b3"), AX.X, ALU.add))
            v.wait_ge(sem("ln_hT"), 1)
            v.wait_ge(sem("ld_wA"), 16)
            v.tensor_scalar(cm[:, :], hT[0][:, :], w("wA", "w_cq"), w("wA", "w_q"), ALU.mult, ALU.add).then_inc(
                sem("cm"), 1)

            def key_rest(i):
                b, k = i // 4, (i % 4) * 512
                v.wait_ge(sem("k_hi"), i + 1)
                if i >= 2:
                    v.wait_ge(sem("k_lo"), i - 1)
                v.scalar_tensor_tensor(kres[:, i % 2, :], bank(KEY_BANK[i]), w("wB", "bk"), kparts[:, 0, b, k:k + 512],
                                       ALU.add, ALU.subtract).then_inc(sem("k_res"), 1)
                v.wait_ge(sem("k_res"), i + 1)
                v.tensor_copy(kparts[:, 1, b, k:k + 512], kres[:, i % 2, :]).then_inc(sem("k_mid"), 1)

            def chunk_max(b, j):
                v.wait_ge(sem("s0_ps"), 4 * b + j + 1)
                v.tensor_reduce(pm0[:, b, j:j + 1], bank(4 * b + j), AX.X, ALU.max).then_inc(sem("pm0"), 1)

            def row_max(b):
                v.wait_ge(sem("pm0"), 4 * b + 4)
                v.tensor_reduce(mx0[:, b:b + 1], pm0[:, b, :], AX.X, ALU.max, negate=True).then_inc(sem("mx0"), 1)

            def turned(b, j):
                v.wait_ge(sem("pT_ps"), 4 * b + j + 1)
                v.tensor_copy(PT0[:, b, 512 * j:512 * (j + 1)], bank(0)).then_inc(sem("pT_dve"), 1)

            v.wait_ge(sem("ld_wB"), 16)
            key_rest(0)
            chunk_max(0, 0)
            chunk_max(0, 1)
            key_rest(1)
            chunk_max(0, 2)
            chunk_max(0, 3)
            row_max(0)
            v.wait_ge(sem("cwc_ps"), 1)
            v.tensor_scalar(cwc[:, :], bank(4)[:, 256:256 + B], b3[:, 0:1], None, ALU.add).then_inc(sem("cwc"), 1)
            for j in range(4):
                chunk_max(1, j)
            row_max(1)
            v.wait_ge(sem("mx0"), 2)
            v.wait_ge(sem("cwc"), 1)
            v.tensor_tensor(rowmax[:, :], cwc[:, :], mx0[:, :], ALU.subtract).then_inc(sem("rowmax"), 1)
            turned(0, 0)
            key_rest(2)
            v.wait_ge(sem("rm_ps"), 1)
            link(v.tensor_copy(rmT[:, :], bank(4)[0:B, 0:128]))
            v.tensor_reduce(rsm[:, 0:1], rmT[:, :], AX.X, ALU.max, negate=True).then_inc(sem("rm_max"), 1)
            turned(0, 2)
            key_rest(3)
            v.wait_ge(sem("erow"), 1)
            link(v.reciprocal(rsm[:, 2:3], rsm[:, 1:2]))
            v.tensor_scalar(brow[:, :], erow[:, :], rsm[:, 2:3], None, ALU.mult).then_inc(sem("brow"), 1)
            turned(1, 0)
            key_rest(4)
            v.wait_ge(sem("batt_ps"), 1)
            v.tensor_copy(batt[:, :], bank(4)[:, 128:128 + B]).then_inc(sem("batt"), 1)
            v.wait_ge(sem("probs"), 2)
            link(v.reciprocal(rden0[:, :], den0[:, :]))
            turned(1, 2)
            key_rest(5)
            v.wait_ge(sem("q2c_ps"), 1)
            link(v.tensor_copy(q2c[:, :], bank(5)[:, 0:B]))
            v.wait_ge(sem("pT_ps"), 4)
            v.tensor_scalar(x4T[:, 0:128], hT[0][:, 0:128], q2c[:, 0:1], None, ALU.mult).then_inc(sem("x4T"), 1)
            v.tensor_scalar(x4T[:, 128:256], hT[0][:, 128:256], q2c[:, 1:2], None, ALU.mult).then_inc(sem("x4T"), 1)
            key_rest(6)
            for b in range(B):
                if b == 1:
                    key_rest(7)
                v.wait_ge(sem("c2q_ps"), b + 1)
                v.tensor_scalar(c2q[:, b, :], bank(2 + b)[:, 0:128], rden0[:, b:b + 1], None, ALU.mult).then_inc(
                    sem("c2q"), 1)
            with_bias(0, "b_l")
            v.wait_ge(sem("turned"), 1)
            v.tensor_tensor(x3T[:, :], hT[0][:, :], c2qT[:, :], ALU.mult).then_inc(sem("x3T"), 1)
            v.wait_ge(sem("xb"), 1)
            v.wait_ge(sem("part_ps"), 1)
            v.tensor_tensor(X[1][:, :, :], XB[0][:, :, :], bank(4)[:, 256:512].rearrange("p (b d) -> p b d", b=B),
                            ALU.add).then_inc(sem("x_ready"), 1)

            v.wait_ge(sem("x_ready"), 1)
            ln_stats(1)
            with_bias(1, "a0_bo")
            ln_apply(1)
            v.wait_ge(sem("k_out0"), 48)
            v.wait_ge(sem("k_out1"), 48)
            v.wait_ge(sem("ld_wC"), 16)

            def over_b(ap):
                return ap.unsqueeze(1).to_broadcast([128, B, S])

            def by_b(ap):
                return ap.rearrange("p (b s) -> p b s", b=B)

            v.wait_ge(sem("iw_ps"), 1)
            v.tensor_tensor(iw[:, :, :], bank(7)[:, 256:256 + B * IH].rearrange("p (b h) -> p b h", b=B),
                            row("b_iw").unsqueeze(1).to_broadcast([128, B, IH]), ALU.add).then_inc(sem("iw"), 1)
            v.tensor_tensor(V, bank(7)[:, 0:256].rearrange("p (b d) -> p b d", b=B),
                            row("a0_bv").unsqueeze(1).to_broadcast([128, B, D]), ALU.add).then_inc(sem("V"), 1)

            def rotate(dst, ps, bias, bias_s, ta, tb, cos, sin, name):
                v.scalar_tensor_tensor(by_b(ta), by_b(ps[:, 0:256]), bias, over_b(cos), ALU.add,
                                       ALU.mult).then_inc(sem("rot"), 1)
                v.scalar_tensor_tensor(by_b(tb), by_b(ps[:, 256:512]), bias_s, over_b(sin), ALU.add,
                                       ALU.mult).then_inc(sem("rot"), 1)
                rots[0] += 2
                v.wait_ge(sem("rot"), rots[0])
                v.tensor_tensor(dst, ta, tb, ALU.add).then_inc(sem(name), 1)

            rots = [0]
            v.wait_ge(sem("qk_ps"), 1)
            rotate(qr, bank(0), w("wC", "bq"), w("wC", "bqs"), t1, t2, w("cst", "cos"), w("cst", "sin"), "rotated")
            rotate(kr, bank(1), w("wC", "bk"), w("wC", "bks"), t3, t4, w("cst", "cos"), w("cst", "sin"), "rotated")
            v.wait_ge(sem("iw"), 1)
            for i in range(IH):
                for b in range(B):
                    v.wait_ge(sem("relu"), i % 2 + 1)
                    if i == 0:
                        v.tensor_scalar(idx[0][:, b, :], relu[:, 0, b, 0, :], iw[:, b, 0:1], None, ALU.mult).then_inc(
                            sem("idx"), 1)
                    else:
                        v.wait_ge(sem("idx"), 2 * (i - 1) + b + 1)
                        v.scalar_tensor_tensor(idx[i % 2][:, b, :], relu[:, i % 2, b, i // 2, :], iw[:, b, i:i + 1],
                                               idx[(i - 1) % 2][:, b, :], ALU.mult, ALU.add).then_inc(sem("idx"), 1)
            for r in range(TOPK // 8):
                src, dst = idx[(IH - 1 + r) % 2], idx[(IH + r) % 2]
                for b in range(B):
                    if r == 0:
                        v.wait_ge(sem("idx"), 2 * (IH - 1) + b + 1)
                    else:
                        v.wait_ge(sem("taken"), 2 * (r - 1) + b + 1)
                    v.max(m8[:, b, r, :], src[:, b, :]).then_inc(sem("m8"), 1)
                for b in range(B):
                    v.wait_ge(sem("m8"), 2 * r + b + 1)
                    v.match_replace(dst[:, b, :], m8[:, b, r, :], src[:, b, :], GONE).then_inc(sem("taken"), 1)
            last = idx[(IH + TOPK // 8 - 1) % 2]
            v.wait_ge(sem("lg_ps"), 1)
            for b in range(B):
                v.wait_ge(sem("taken"), 2 * (TOPK // 8 - 1) + b + 1)
                link(v.tensor_scalar(keep[:, b, :], last[:, b, :], GONE * 0.99, -1.0e30, ALU.is_gt, ALU.mult))
                link(v.scalar_tensor_tensor(lg[:, b, :], bank(7)[:, 128 * b:128 * b + 128], float(D) ** -0.5,
                                            keep[:, b, :], ALU.mult, ALU.add))
                v.tensor_reduce(nmx1[:, b:b + 1], lg[:, b, :], AX.X, ALU.max, negate=True).then_inc(sem("nmx1"), 1)
            v.wait_ge(sem("probs"), 4)
            link(v.reciprocal(rden1[:, :], den1[:, :]))
            v.wait_ge(sem("xb"), 2)
            v.wait_ge(sem("part_ps"), 2)
            for b in range(B):
                v.scalar_tensor_tensor(X[2][:, b, :], bank(3)[:, 128 * b:128 * b + 128], rden1[:, b:b + 1],
                                       XB[1][:, b, :], ALU.mult, ALU.add).then_inc(sem("x_ready"), 1)

            v.wait_ge(sem("x_ready"), 3)
            ln_stats(2)
            ln_apply(2)

            def router(i, ps):
                lgt = rt[:, i, 16:32].rearrange("p (b n) -> p b n", b=B)
                if i == 0:
                    link(v.tensor_copy(lgt, ps))
                else:
                    link(v.tensor_tensor(lgt, ps, row("f1_rb").unsqueeze(1).to_broadcast([128, B, NE]), ALU.add))
                v.tensor_reduce(rt[:, i, 32:34], lgt, AX.X, ALU.max, negate=True).then_inc(sem("rt_max"), 1)

            def router_top(i):
                v.wait_ge(sem("rt_exp"), 2 * i + 2)
                link(v.reciprocal(rt[:, i, 68:70], rt[:, i, 34:36]))
                for b in range(B):
                    ins = v.tensor_scalar(rt[:, i, 36 + 8 * b:44 + 8 * b], rt[:, i, 8 * b:8 * b + 8],
                                          rt[:, i, 68 + b:69 + b], None, ALU.mult)
                    ins.then_inc(sem("rt_p"), 1)
                for b in range(B):
                    v.wait_ge(sem("rt_p"), 2 * i + b + 1)
                    v.max(rt[:, i, 52 + 8 * b:60 + 8 * b], rt[:, i, 36 + 8 * b:44 + 8 * b]).then_inc(sem("rt_m8"), 1)
                v.wait_ge(sem("rt_m8"), 2 * i + 2)
                top = rt[:, i, 52:68].rearrange("p (b n) -> p b n", b=B)
                link(v.tensor_tensor(rt[:, i, 70:72], top[:, :, 0], top[:, :, 1], ALU.add))
                link(v.reciprocal(rt[:, i, 72:74], rt[:, i, 70:72]))
                return top

            for to, of, name in ((mb.rearrange("p b k -> p (b k)"), mask_q, "ld_mask"),
                                 (mbT.rearrange("p b c q -> p (b c q)"), mask_k, "ld_maskT")):
                v.wait_ge(sem(name), 16 * B)
                v.wait_ge(sem("c2q_ps"), 2)
                for i in range(2):
                    part = slice(i * SK, (i + 1) * SK)
                    v.tensor_scalar(to[:, part], of[:, part], 0.0, -MASK_BIG, ALU.is_equal, ALU.mult).then_inc(
                        sem("mask_bias"), 1)
            v.wait_ge(sem("router_ps"), 1)
            router(0, bank(7)[:, 0:16].rearrange("p (b n) -> p b n", b=B))
            with_bias_row = row("f0_b2").unsqueeze(1).to_broadcast([128, B, D])
            top = router_top(0)
            link(v.tensor_tensor(rt[:, 0, 74:78].rearrange("p (b n) -> p b n", b=B), top[:, :, 0:2],
                                 rt[:, 0, 72:74].unsqueeze(2).to_broadcast([128, B, 2]), ALU.mult))
            link(v.tensor_reduce(rt[:, 0, 78:80], rt[:, 0, 74:78].rearrange("p (b n) -> p b n", b=B), AX.X, ALU.add))
            v.wait_ge(sem("part_ps"), 3)
            link(v.tensor_tensor(ob[:, :, :], bank(3)[:, 0:256].rearrange("p (b d) -> p b d", b=B), with_bias_row,
                                 ALU.add))
            for b in range(B):
                v.scalar_tensor_tensor(X[3][:, b, :], ob[:, b, :], rt[:, 0, 78 + b:79 + b], X[2][:, b, :], ALU.mult,
                                       ALU.add).then_inc(sem("x_ready"), 1)

            v.wait_ge(sem("x_ready"), 5)
            ln_stats(3)
            with_bias(3, "x1_bo")
            ln_apply(3)
            v.wait_ge(sem("ld_wE"), 16)
            v.wait_ge(sem("q3_hi"), 1)
            link(v.scalar_tensor_tensor(qres[:, :], bank(5)[:, 0:256], w("wE", "bq"), qp[:, 0, :], ALU.add,
                                        ALU.subtract))
            v.tensor_copy(qp[:, 1, :], qres[:, :]).then_inc(sem("q3_mid"), 1)
            v.wait_ge(sem("q3_mid"), 1)
            v.tensor_tensor(qp[:, 2, :], qres[:, :], qp[:, 1, :], ALU.subtract).then_inc(sem("q3_lo"), 1)
            v.wait_ge(sem("flag_ps"), 1)
            link(v.tensor_reduce(flagf[:, :], bank(6)[0:1, :], AX.X, ALU.min))
            v.tensor_scalar(flag[:, :], flagf[:, :], 0.0, None, ALU.is_lt).then_inc(sem("flag"), 1)

            def unit_max(u):
                r, of = u // B % 2, slice(2 * (u % B), 2 * (u % B) + 2)
                v.wait_ge(sem("s_red"), 8 * u + 8)
                if u >= 2 * B:
                    v.wait_ge(sem("mt"), u - 2 * B + 1)
                v.tensor_reduce(nmx3[:, r, of], pmx[:, r, of, :], AX.X, ALU.max, negate=True).then_inc(
                    sem("nmx3"), 1)

            def pair_out(g):
                v.wait_ge(sem("oq_ps"), 2 * g + 2)
                v.tensor_copy(oq[:, :, g, :, :].rearrange("p b e n -> p b (e n)"),
                              bank(7)[:, 0:2 * VW].rearrange("p (b m) -> p b m", b=B)).then_inc(sem("oq"), 1)

            for m in range(16 * G):
                g, i = m // 16, m % 16
                v.wait_ge(sem("s_done"), m + 1)
                v.tensor_reduce(pmx[:, g % 2, i // 4, i % 4:i % 4 + 1], bank(m % 2), AX.X, ALU.max).then_inc(
                    sem("s_red"), 1)
                if m >= 8 and m % 8 == 0:
                    unit_max(m // 8 - 1)
                if i == 2 and g >= 2:
                    pair_out(g - 2)
            unit_max(UNITS - 1)
            pair_out(G - 2)
            pair_out(G - 1)
            v.wait_ge(sem("oq"), G)
            heads = oq[:, :, :, :, :].rearrange("p b g e n -> p b (g e) n")
            link(v.reciprocal(rd3[:, :, :], heads[:, :, :, DH]))
            link(v.tensor_tensor(att3[:, :, :, :], heads[:, :, :, 0:DH],
                                 rd3[:, :, :].unsqueeze(3).to_broadcast([128, B, H, DH]), ALU.mult))
            v.tensor_tensor(ob[:, :, :], att3[:, :, :, :].rearrange("p b h n -> p b (h n)"),
                            row("x1_bv").unsqueeze(1).to_broadcast([128, B, D]), ALU.add).then_inc(sem("att3"), 1)
            v.wait_ge(sem("xb"), 3)
            v.wait_ge(sem("part_ps"), 4)
            v.tensor_tensor(X[4][:, :, :], XB[3][:, :, :], bank(1)[:, 0:256].rearrange("p (b d) -> p b d", b=B),
                            ALU.add).then_inc(sem("x_ready"), 1)

            v.wait_ge(sem("x_ready"), 6)
            ln_stats(4)
            with_bias(4, "a1_bo")
            ln_apply(4)
            v.wait_ge(sem("qk4_ps"), 1)
            v.wait_ge(sem("ld_wF"), 16)
            a4 = [r4[:, i, :, :].rearrange("p b d -> p (b d)") for i in range(2)]
            b4 = [n4[:, :, :].rearrange("p b d -> p (b d)"), r4[:, 2, :, :].rearrange("p b d -> p (b d)")]
            rotate(kr4[:, :], bank(1), w("wF", "bka"), w("wF", "bkb"), b4[0], b4[1], w("cst", "A"), w("cst", "B"),
                   "rotated4")
            v.wait_ge(sem("qk4_ps"), 2)
            rotate(qr4[:, :], bank(0), w("wF", "bqa"), w("wF", "bqb"), a4[0], a4[1], w("cst", "A"), w("cst", "B"),
                   "rotated4")
            v.wait_ge(sem("rotated4"), 1)
            for n in range(2):
                v.tensor_tensor(kbd[:, 0, 4 * n:4 * n + 4, :],
                                kr4[:, 0:128].unsqueeze(1).to_broadcast([128, 4, 128]),
                                w("cst", "hm")[:, 4 * n:4 * n + 4].unsqueeze(2).to_broadcast([128, 4, 128]),
                                ALU.mult).then_inc(sem("kbd_dve"), 1)

            def heads4(n):
                return bank(4 + n % 3).rearrange("p (h k) -> p h k", h=4), n // 4, slice(4 * (n % 4), 4 * (n % 4) + 4)

            def sub4(n):
                sc, b, hs = heads4(n)
                v.wait_ge(sem("mx4"), n + 1)
                v.tensor_tensor(sc4[:, b, hs, :], sc, mx4[:, b, hs].unsqueeze(2).to_broadcast([128, 4, S]),
                                ALU.subtract).then_inc(sem("sub4"), 1)

            for n in range(8):
                sc, b, hs = heads4(n)
                v.wait_ge(sem("s4_ps"), n + 1)
                v.tensor_reduce(mx4[:, b, hs], sc, AX.X, ALU.max).then_inc(sem("mx4"), 1)
                if n:
                    sub4(n - 1)
            sub4(7)
            for b in range(B):
                o = bank(6 - 2 * b).rearrange("p (h n) -> p h n", h=H)
                v.wait_ge(sem("o4T_ps"), b + 1)
                v.reciprocal(rd4[:, b, :], o[:, :, DH]).then_inc(sem("rd4"), 1)
                v.wait_ge(sem("rd4"), b + 1)
                v.tensor_tensor(n4[:, b, :].rearrange("p (h n) -> p h n", h=H), o[:, :, 0:DH],
                                rd4[:, b, :].unsqueeze(2).to_broadcast([128, H, DH]), ALU.mult).then_inc(
                    sem("n4"), 1)
                v.wait_ge(sem("n4"), b + 1)
                pairs = n4[:, b, :].rearrange("p (h m t) -> p h m t", m=4, t=2)
                for u, tab in ((0, "na"), (1, "nb")):
                    v.tensor_tensor(r4[:, u, b, :].rearrange("p (h f m) -> p h f m", h=H, f=2),
                                    pairs[:, :, :, u].unsqueeze(2).to_broadcast([128, H, 2, 4]),
                                    w("cst", tab).rearrange("p (f m) -> p f m", f=2).unsqueeze(1).to_broadcast(
                                        [128, H, 2, 4]), ALU.mult).then_inc(sem("rot4"), 1)
                v.wait_ge(sem("rot4"), 2 * b + 2)
                v.tensor_tensor(r4[:, 2, b, :], r4[:, 0, b, :], r4[:, 1, b, :], ALU.add).then_inc(sem("r4"), 1)
            v.wait_ge(sem("xb"), 4)
            v.wait_ge(sem("part_ps"), 5)
            v.tensor_tensor(X[5][:, :, :], XB[4][:, :, :], bank(6)[:, 0:256].rearrange("p (b d) -> p b d", b=B),
                            ALU.add).then_inc(sem("x_ready"), 1)

            v.wait_ge(sem("x_ready"), 7)
            ln_stats(5)
            ln_apply(5)
            v.wait_ge(sem("router_ps"), 2)
            router(1, bank(7)[:, 256:272].rearrange("p (b n) -> p b n", b=B))
            top = router_top(1)
            link(v.memset(top[:, :, 2:8], -1.0))
            for b in range(B):
                v.match_replace(rt[:, 1, 80 + 8 * b:88 + 8 * b], top[:, b, :], rt[:, 1, 36 + 8 * b:44 + 8 * b],
                                -2.0).then_inc(sem("rt_mr"), 1)
            v.wait_ge(sem("rt_mr"), 2)
            link(v.scalar_tensor_tensor(rt[:, 1, 96:112], rt[:, 1, 80:96], 0.0, rt[:, 1, 36:52], ALU.is_lt,
                                        ALU.mult))
            v.tensor_tensor(rt[:, 1, 112:128].rearrange("p (b n) -> p b n", b=B),
                            rt[:, 1, 96:112].rearrange("p (b n) -> p b n", b=B),
                            rt[:, 1, 72:74].unsqueeze(2).to_broadcast([128, B, NE]), ALU.mult).then_inc(
                sem("rw"), 1)
            v.wait_ge(sem("rwT_ps"), 1)
            v.tensor_copy(rsel[:, :], bank(5)[0:NE, 0:256]).then_inc(sem("rsel"), 1)
            for c in range(FC):
                v.wait_ge(sem("gelu"), c + 1 + 4)
                v.wait_ge(sem("rx_ps"), c // 2 + 1)
                v.tensor_tensor(gw[:, c, :], g5[:, c, :], bank(6 if c < 2 else 4)[:, 256 * (c % 2):256 * (c % 2) + 256],
                                ALU.mult).then_inc(sem("gw"), 1)
            for b in range(B):
                v.wait_ge(sem("part_ps"), b + 1 + 5)
                v.tensor_tensor(X[6][:, b, :], X[5][:, b, :], bank(2 + b)[:, 256:384], ALU.add).then_inc(
                    sem("out_ready"), 1)

        @block.tensor
        def _(pe):
            def mm(o, lhsT, rhs, start=True, stop=True, **kw):
                return pe.matmul(o, lhsT, rhs, start=start, stop=stop, **kw)

            def ln_turn(i):
                for b in range(B):
                    pe.wait_ge(sem("ln_h"), 2 * i + b + 1)
                    ins = pe.transpose(bank(4)[:, 128 * b:128 * b + 128], h[i][:, b, :], ident)
                ins.then_inc(sem("ln_hT_ps"), 1)

            pe.wait_ge(sem("ld_cst"), 16)
            ln_turn(0)
            pe.wait_ge(sem("ld_wB"), 16)

            def keys(i):
                b, k = i // 4, (i % 4) * 512
                pe.wait_ge(sem(f"ld_ctxT{i // 2}"), 16)
                if i >= 4:
                    pe.wait_ge(sem("k_res"), i - 1)
                elif i >= 2:
                    pe.wait_ge(sem("probs"), 2)
                mm(bank(KEY_BANK[i]), w("wB", "wk"), ctxT[:, b, k:k + 512]).then_inc(sem("k_ps"), 1)

            def scores0(b, j):
                pe.wait_ge(sem(f"ld_ctxT{2 * b + j // 2}"), 16)
                if b == 1 and j == 0:
                    pe.wait_ge(sem("cwc"), 1)
                elif b == 1 and j < 3:
                    pe.wait_ge(sem("k_res"), j)
                mm(bank(4 * b + j), cm[:, 128 * b:128 * b + 128],
                   ctxT[:, b, 512 * j:512 * j + 512]).then_inc(sem("s0_ps"), 1)

            def turn_p(b, j):
                pe.wait_ge(sem("probs"), b + 1)
                n = 4 * b + j
                if n >= 2:
                    pe.wait_ge(sem("pT_dve") if j % 2 == 0 else sem("pT_act"), n // 2)
                for c in range(4):
                    ins = pe.transpose(bank(j % 2)[:, 128 * c:128 * c + 128],
                                       P0[:, b, 512 * j + 128 * c:512 * j + 128 * c + 128], ident)
                ins.then_inc(sem("pT_ps"), 1)

            def weigh(b, j):
                n = 4 * b + j
                pe.wait_ge(sem("pT_dve") if j % 2 == 0 else sem("pT_act"), n // 2 + 1)
                if j == 0:
                    pe.wait_ge(sem(f"ld_ctxN{b}"), 16)
                for c in range(4):
                    ins = mm(bank(2 + b)[:, 0:128], PT0[:, b, 512 * j + 128 * c:512 * j + 128 * c + 128],
                             ctxN[:, b, 4 * j + c, :], start=(j == 0 and c == 0), stop=(j == 3 and c == 3))
                if j == 3:
                    ins.then_inc(sem("c2q_ps"), 1)

            pe.wait_ge(sem("ld_wB"), 16)
            keys(0)
            pe.wait_ge(sem("cm"), 1)
            scores0(0, 0)
            scores0(0, 1)
            keys(1)
            scores0(0, 2)
            scores0(0, 3)
            pe.wait_ge(sem("ld_wA"), 16)
            for b in range(B):
                ins = mm(bank(4)[:, 256 + b:257 + b], hT[0][:, 128 * b:128 * b + 128], w("wA", "w_c"))
            ins.then_inc(sem("cwc_ps"), 1)
            for j in range(4):
                scores0(1, j)
            turn_p(0, 0)
            turn_p(0, 1)
            keys(2)
            pe.wait_ge(sem("rowmax"), 1)
            pe.transpose(bank(4)[0:B, 0:128], rowmax[:, :], ident).then_inc(sem("rm_ps"), 1)
            weigh(0, 0)
            turn_p(0, 2)
            keys(3)
            weigh(0, 1)
            turn_p(0, 3)
            weigh(0, 2)
            turn_p(1, 0)
            keys(4)
            weigh(0, 3)
            pe.wait_ge(sem("brow"), 1)
            pe.transpose(bank(4)[:, 128:128 + B], brow[:, :], ident[0:B, 0:B]).then_inc(sem("batt_ps"), 1)
            turn_p(1, 1)
            weigh(1, 0)
            turn_p(1, 2)
            keys(5)
            pe.wait_ge(sem("batt"), 1)
            for b in range(B):
                ins = mm(bank(5)[:, b:b + 1], h[0][:, b, :], batt[:, b:b + 1])
            ins.then_inc(sem("q2c_ps"), 1)
            weigh(1, 1)
            turn_p(1, 3)
            keys(6)
            weigh(1, 2)
            keys(7)
            weigh(1, 3)
            for b in range(B):
                pe.wait_ge(sem("c2q"), b + 1)
                ins = pe.transpose(bank(5)[:, 256 + 128 * b:384 + 128 * b], c2q[:, b, :], ident)
            ins.then_inc(sem("turn_ps"), 1)
            wl = w("wA", "wl")
            pe.wait_ge(sem("x4T"), 2)
            pe.wait_ge(sem("batt"), 1)
            for b in range(B):
                q = slice(128 * b, 128 * b + 128)
                to = bank(4)[:, 256 + 128 * b:384 + 128 * b]
                mm(to, hT[0][:, q], wl[:, 0:128], start=True, stop=False)
                mm(to, x4T[:, q], wl[:, 384:512], start=False, stop=False)
                pe.wait_ge(sem("turned"), 1)
                mm(to, c2qT[:, q], wl[:, 128:256], start=False, stop=False)
                pe.wait_ge(sem("x3T"), 1)
                ins = mm(to, x3T[:, q], wl[:, 256:384], start=False, stop=True)
            ins.then_inc(sem("part_ps"), 1)

            ln_turn(1)
            pe.wait_ge(sem("ld_wC"), 16)
            pe.wait_ge(sem("ln_hT"), 2)
            for j in range(2):
                mm(bank(2)[:, 256 * j:256 * j + 256], w("wC", "iq")[:, 128 * j:128 * j + 128], hT[1][:, :])
            mm(bank(3)[:, 0:256], w("wC", "ik"), hT[1][:, :]).then_inc(sem("iq_ps"), 1)
            for b in range(B):
                q = slice(128 * b, 128 * b + 128)
                mm(bank(7)[:, 256 + IH * b:256 + IH * b + IH], hT[1][:, q], w("wC", "iw"))
                ins = mm(bank(7)[:, q], hT[1][:, q], w("wC", "v"))
            ins.then_inc(sem("iw_ps"), 1)
            for j, name in enumerate(("q", "qs", "k", "ks")):
                ins = mm(bank(j // 2)[:, 256 * (j % 2):256 * (j % 2) + 256], w("wC", name), hT[1][:, :])
            ins.then_inc(sem("qk_ps"), 1)
            pe.wait_ge(sem("index_T"), 3)
            for r in range(2):
                p = slice(64 * r, 64 * r + 64)
                for b in range(B):
                    for i in range(IH // 2):
                        c = 256 * i + 128 * b
                        o = 128 * (2 * b + i)
                        ins = mm(bank(5 + r)[:, o:o + 128], iqT[p, c:c + 128], ikT[p, 128 * b:128 * b + 128])
                ins.then_inc(sem("hs_ps"), 1)
            pe.wait_ge(sem("rotated"), 1)
            pe.wait_ge(sem("rotated"), 2)
            pe.wait_ge(sem("V"), 1)
            for b in range(B):
                q = slice(128 * b, 128 * b + 128)
                ins = mm(bank(7)[:, q], qr[:, q], kr[:, q])
            ins.then_inc(sem("lg_ps"), 1)
            for i in range(8):
                if i >= 2:
                    pe.wait_ge(sem("v_set"), i - 1)
                for c in range(4):
                    k = 512 * (i % 4) + 128 * c
                    ins = mm(bank(2 + i % 2)[:, 128 * c:128 * c + 128], ctxT[:, i // 4, k:k + 128], w("wB", "wv"))
                ins.then_inc(sem("v_ps"), 1)
            for b in range(B):
                pe.wait_ge(sem("probs"), b + 1 + 2)
                ins = pe.transpose(bank(0)[:, 128 * b:128 * b + 128], Pm[:, b, :], ident)
            ins.then_inc(sem("turn_ps"), 1)
            pe.wait_ge(sem("turned"), 2)
            for b in range(B):
                q = slice(128 * b, 128 * b + 128)
                ins = mm(bank(1)[:, q], V[:, b, :], PmT[:, q])
            ins.then_inc(sem("turn_ps"), 1)
            pe.wait_ge(sem("turned"), 3)
            pe.wait_ge(sem("v_set"), 8)
            for b in range(B):
                q = slice(128 * b, 128 * b + 128)
                ins = mm(bank(3)[:, q], aT[:, q], w("wC", "o"))
            ins.then_inc(sem("part_ps"), 1)

            ln_turn(2)
            pe.wait_ge(sem("ld_wD"), 16)
            pe.wait_ge(sem("ln_hT"), 3)
            for c in range(FC):
                if c >= 2:
                    pe.wait_ge(sem("gelu"), c - 1)
                mm(bank(5 + c % 2)[:, 0:256], w("wD", "w1")[:, 128 * c:128 * c + 128], hT[2][:, :]).then_inc(sem("hidden_ps"), 1)
                if c == 1:
                    for b in range(B):
                        ins = mm(bank(7)[:, 8 * b:8 * b + 8], hT[2][:, 128 * b:128 * b + 128], w("wD", "r"))
                    ins.then_inc(sem("router_ps"), 1)
            for b in range(B):
                for c in range(FC):
                    pe.wait_ge(sem("gelu"), c + 1)
                    ins = mm(bank(3)[:, 128 * b:128 * b + 128], g0[:, c, 128 * b:128 * b + 128],
                             w("wD", "w2")[:, 128 * c:128 * c + 128], start=(c == 0), stop=(c == FC - 1))
            ins.then_inc(sem("part_ps"), 1)

            pe.wait_ge(sem("onesb"), 1)
            pe.wait_ge(sem("mask_bias"), 4)
            for i in range(8):
                ins = mm(bank(6)[0:1, :], onesb[:, :], mb[:, i // 4, 512 * (i % 4):512 * (i % 4) + 512],
                         start=(i == 0), stop=(i == 7))
            ins.then_inc(sem("flag_ps"), 1)
            ln_turn(3)
            pe.wait_ge(sem("ld_wE"), 16)
            pe.wait_ge(sem("ln_hT"), 4)
            mm(bank(5)[:, 0:256], w("wE", "q"), hT[3][:, :]).then_inc(sem("q3_ps"), 1)
            pe.wait_ge(sem("ld_sel"), 16)
            pe.wait_ge(sem("q3_hi"), 1)
            pe.wait_ge(sem("q3_lo"), 1)
            pe.wait_ge(sem("ld_identb"), 16)
            pe.wait_ge(sem("ld_tail"), 16 * 2 * RING)
            pe.wait_ge(sem("v_set"), 8)

            def stack_queries(g):
                if g == 0:
                    pe.wait_ge(sem("rt_max"), 1)
                elif g == 1:
                    pe.wait_ge(sem("qs"), 2)
                else:
                    pe.wait_ge(sem("qt"), 2 * (B * (g - 2) + 2))
                for a in range(3):
                    ins = mm(bank(7)[:, 0:256], sel[:, g, a, :], qp[:, a, :], start=(a == 0), stop=(a == 2))
                ins.then_inc(sem("stack_ps"), 1)

            def stack_queries_max(u):
                g, b = u // B, u % B
                pe.wait_ge(sem("mt"), u + 1)
                pe.wait_ge(sem("qs"), min(2 * (g + 2), 2 * G))
                if b == 1:
                    pe.wait_ge(sem("qt"), 2 * u)
                    if g >= 1:
                        pe.wait_ge(sem("oq"), g)
                for a in range(3):
                    mm(bank(7)[:, 0:128], sel[:, g, a, :], qp[:, a, 128 * b:128 * b + 128], start=(a == 0),
                       stop=(a == 2))
                mm(bank(7)[:, 0:128], mt[:, g % 2, b, :], identb[:, :], start=False, stop=True,
                   skip_group_check=True).then_inc(sem("stackm_ps"), 1)

            def pair_rows(g, b):
                pe.wait_ge(sem("o_rows"), 2 * g + b + 1)
                if b == 0:
                    pe.wait_ge(sem("qt"), 2 * min(B * (g + 1) + 1, UNITS))
                    if g == G - 1:
                        pe.wait_ge(sem("oq"), G - 1)
                for e in range(2):
                    ins = mm(bank(7)[:, VW * b + (DH + 1) * e:VW * b + (DH + 1) * (e + 1)],
                             O[:, b, S * e:S * e + S], w("cst", "R")[:, (DH + 1) * e:(DH + 1) * (e + 1)])
                ins.then_inc(sem("oq_ps"), 1)

            def wide_attention(masked):
                def score(m):
                    g, b, e, c = m // 16, m // 8 % 2, m // 4 % 2, m % 4
                    if m % 16 == 0:
                        pe.wait_ge(sem("qs"), 2 * g + 2)
                    if m % 8 == 0 and (g == 0 or g >= RING):
                        slot = b if g == 0 else 2 + (g - RING) * 2 + b
                        pe.wait_ge(sem(f"k_in{slot}"), 16 * 2 * NBLK)
                    if m >= 2:
                        pe.wait_ge(sem("s_red"), m - 1)
                    ins = mm(bank(m % 2), qs[:, g % 2, e, b, :], kst[:, g % RING, b, 512 * c:512 * c + 512],
                             stop=not masked)
                    if masked:
                        ins = mm(bank(m % 2), identb[:, :], mb[:, b, 512 * c:512 * c + 512], start=False)
                    ins.then_inc(sem("s_done"), 1)

                def score_t(n):
                    g, b, u = n // 8, n // 4 % 2, n % 4
                    if n >= 2:
                        pe.wait_ge(sem("p3"), n - 1)
                    if u == 0:
                        pe.wait_ge(sem("qt"), 2 * (n // 4) + 2)
                    for c in range(4):
                        k = 128 * (4 * u + c)
                        to = bank(2 + 2 * (n % 2), 2)[:, 256 * c:256 * c + 256]
                        ins = mm(to, kst[:, g % RING, b, k:k + 128],
                                 qt[:, g % 2, b, :, :].rearrange("p e q -> p (e q)"), stop=not masked)
                        if masked:
                            ins = mm(to.rearrange("p (e q) -> p e q", e=2), identb[:, :],
                                     mbT[:, b, 4 * u + c, :].unsqueeze(1).to_broadcast([128, 2, S]), start=False)
                    ins.then_inc(sem("st_done"), 1)

                def weigh_values(n):
                    g, b, u = n // 8, n // 4 % 2, n % 4
                    pe.wait_ge(sem("p3"), n + 1)
                    if n == 0:
                        pe.wait_ge(sem("flag"), 1)
                    elif u == 0:
                        pe.wait_ge(sem("o_rows"), 2 * g + b)
                    for c in range(4):
                        ins = mm(bank(6)[32 * c:32 * c + 32, 0:256], value(b, 4 * u + c, g),
                                 pt_ring[:, n % 4, 256 * c:256 * c + 256], start=(u == 0), stop=(u == 3),
                                 tile_position=(0, 32 * c))
                    ins.then_inc(sem("pv_done"), 1)

                m = 0
                while m < 8:
                    score(m)
                    m += 1
                stack_queries(1)
                for _ in range(2):
                    score(m)
                    m += 1
                stack_queries_max(0)
                for n in range(8 * G):
                    g, j = n // 8, n % 8
                    if n % 4 == 3 and n // 4 + 1 < UNITS:
                        stack_queries_max(n // 4 + 1)
                    if j == 5 and g + 2 < G:
                        stack_queries(g + 2)
                    goal = min(8 + S_LEAD + 2 * (n + 1), 16 * G)
                    if m < goal:
                        score(m)
                        m += 1
                    score_t(n)
                    if m < goal:
                        score(m)
                        m += 1
                    if n:
                        weigh_values(n - 1)
                    if m < goal:
                        score(m)
                        m += 1
                    if j == 1 and g:
                        pair_rows(g - 1, 0)
                        pair_rows(g - 1, 1)
                weigh_values(8 * G - 1)
                pair_rows(G - 1, 0)
                pair_rows(G - 1, 1)

            stack_queries(0)
            pe.wait_ge(sem("flag"), 1)
            any_masked = pe.value_load(flag[0:1, 0:1], min_val=0, max_val=1)
            with pe.If(any_masked != 0):
                wide_attention(True)
            with pe.Else():
                wide_attention(False)
            for b in range(B):
                pe.wait_ge(sem("att3"), 1)
                ins = pe.transpose(bank(0)[:, 128 * b:128 * b + 128], ob[:, b, :], ident)
            ins.then_inc(sem("turn_ps"), 1)
            pe.wait_ge(sem("turned"), 4)
            for b in range(B):
                q = slice(128 * b, 128 * b + 128)
                ins = mm(bank(1)[:, q], att3T[:, q], w("wE", "o"))
            ins.then_inc(sem("part_ps"), 1)

            ln_turn(4)
            pe.wait_ge(sem("ld_wF"), 16)
            pe.wait_ge(sem("ln_hT"), 5)
            for side, names in ((1, ("ka", "kb")), (0, ("qa", "qb"))):
                for j, name in enumerate(names):
                    ins = mm(bank(side)[:, 256 * j:256 * j + 256], w("wF", name), hT[4][:, :])
                ins.then_inc(sem("qk4_ps"), 1)
            for b in range(B):
                ins = mm(bank(2)[:, 256 * b:256 * b + 256], hT[4][:, 128 * b:128 * b + 128], w("wF", "v"))
            ins.then_inc(sem("v4_ps"), 1)

            def scores4(n):
                b, j = n // 4, n % 4
                if n < 2:
                    pe.wait_ge(sem("kbd_dve"), n + 1)
                else:
                    pe.wait_ge(sem("kbd_pool"), n - 1)
                if n >= 3:
                    pe.wait_ge(sem("sub4"), n - 2)
                mm(bank(4 + n % 3), qr4[:, 128 * b:128 * b + 128],
                   kbd[:, b, 4 * j:4 * j + 4, :].rearrange("p h k -> p (h k)")).then_inc(sem("s4_ps"), 1)

            def turn4(n):
                b, j = n // 4, n % 4
                pe.wait_ge(sem("exp4"), n + 1)
                if n >= 2:
                    pe.wait_ge(sem("p4T"), n - 1)
                for i in range(4):
                    ins = pe.transpose(bank(3 if n % 2 else 7)[:, 128 * i:128 * i + 128], sc4[:, b, 4 * j + i, :],
                                       ident)
                ins.then_inc(sem("p4T_ps"), 1)

            def weigh4(n):
                b, quad = n // 4, n % 4
                if n == 0:
                    pe.wait_ge(sem("v4"), 1)
                pe.wait_ge(sem("p4T"), n + 1)
                for j in range(4):
                    hd = 4 * quad + j
                    ins = mm(bank(b)[32 * j:32 * j + 32, 128 * quad:128 * quad + 128], v4[:, b, hd, :],
                             pT4[:, b, hd, :], tile_position=(0, 32 * j))
                if quad == 3:
                    ins.then_inc(sem("o4_ps"), 1)

            def turn_out4(b):
                pe.wait_ge(sem("o4"), b + 1)
                pe.wait_ge(sem("sub4"), 8)
                for quad in range(4):
                    ins = pe.transpose(bank(6 - 2 * b)[:, 128 * quad:128 * quad + 128],
                                       o4[:, b, 128 * quad:128 * quad + 128], ident)
                ins.then_inc(sem("o4T_ps"), 1)

            pe.wait_ge(sem("rotated4"), 2)
            for n in range(3):
                scores4(n)
            for n in range(8):
                if n + 3 < 8:
                    scores4(n + 3)
                turn4(n)
                if n == 5:
                    for i in range(4):
                        weigh4(i)
                if n > 5:
                    weigh4(n - 2)
            weigh4(6)
            turn_out4(0)
            weigh4(7)
            turn_out4(1)
            for b in range(B):
                pe.wait_ge(sem("r4"), b + 1)
                ins = pe.transpose(bank(7)[:, 128 * b:128 * b + 128], r4[:, 2, b, :], ident)
            ins.then_inc(sem("turn_ps"), 1)
            pe.wait_ge(sem("turned"), 5)
            for b in range(B):
                q = slice(128 * b, 128 * b + 128)
                ins = mm(bank(6)[:, q], r4T[:, q], w("wF", "o"))
            ins.then_inc(sem("part_ps"), 1)

            ln_turn(5)
            pe.wait_ge(sem("ld_wG"), 16)
            pe.wait_ge(sem("ln_hT"), 6)
            pe.wait_ge(sem("x_ready"), 7)
            for b in range(B):
                ins = mm(bank(7)[:, 256 + 8 * b:264 + 8 * b], hT[5][:, 128 * b:128 * b + 128], w("wG", "r"))
            ins.then_inc(sem("router_ps"), 1)
            pe.wait_ge(sem("o4"), 2)
            for c in range(FC):
                mm(bank(c)[:, 0:256], w("wG", "w1")[:, 128 * c:128 * c + 128], hT[5][:, :]).then_inc(sem("hidden_ps"), 1)
            pe.wait_ge(sem("rw"), 1)
            for b in range(B):
                ins = pe.transpose(bank(5)[0:NE, 128 * b:128 * b + 128], rt[:, 1, 112 + 8 * b:120 + 8 * b], ident)
            ins.then_inc(sem("rwT_ps"), 1)
            pe.wait_ge(sem("rsel"), 1)
            pe.wait_ge(sem("ld_b2e"), 32)
            for c in range(FC):
                ins = mm(bank(6 if c < 2 else 4)[:, 256 * (c % 2):256 * (c % 2) + 256], E8[:, 128 * c:128 * c + 128],
                         rsel[:, :])
                if c % 2:
                    ins.then_inc(sem("rx_ps"), 1)
            pe.wait_ge(sem("gelu"), FC + 4)
            for b in range(B):
                q = slice(128 * b, 128 * b + 128)
                o = bank(2 + b)[:, 256:384]
                mm(o, rsel[:, q], b2e[:, :], start=True, stop=False)
                for c in range(FC):
                    pe.wait_ge(sem("gw"), c + 1)
                    ins = mm(o, gw[:, c, q], w("wG", "w2")[:, 128 * c:128 * c + 128], start=False, stop=(c == FC - 1))
                ins.then_inc(sem("part_ps"), 1)


def constants():
    f = np.float32
    cst = {"ident": np.eye(128, dtype=f)}
    half = D // 2
    inv = f(1.0) / f(10000.0) ** (np.arange(half, dtype=f) / f(half))
    ang = np.arange(S, dtype=f)[:, None] * inv[None, :].astype(f)
    cos, sin = np.cos(ang).astype(f).T, np.sin(ang).astype(f).T
    cst["cos"] = np.concatenate([cos, cos])
    cst["sin"] = np.concatenate([-sin, sin])
    theta = f(10000.0) ** (-np.arange(0, DH, 2, dtype=f) / f(DH))
    fr = np.arange(S, dtype=f)[:, None] * theta[None, :].astype(f)
    rope = np.concatenate([np.cos(fr), np.sin(fr)], axis=1).astype(f)
    c, s = rope[:, ::2], rope[:, 1::2]
    va, vb = np.concatenate([c, s], 1), np.concatenate([-s, c], 1)
    cst["va"], cst["vb"], cst["na"], cst["nb"] = va, vb, -va, -vb
    cst["A"], cst["B"] = np.tile(va.T, (H, 1)), np.tile(vb.T, (H, 1))
    feat = np.arange(128)
    cst["hm"] = (feat[:, None] // DH == np.arange(H)[None, :]).astype(f)
    R = np.zeros((128, VW), f)
    for j in range(4):
        for i in range(VW):
            R[32 * j + i, i] = 1.0
    cst["R"] = R
    sel = np.zeros((128, G, 3, 128), f)
    for g in range(G):
        for e in range(2):
            for blk, a in enumerate(Q_PARTS):
                for d in range(DH):
                    sel[(2 * g + e) * DH + d, g, a, 64 * e + DH * blk + d] = 1.0
    tail = np.zeros((64 - MAX_ROW, B * SK), f)
    tail[0:3] = 1.0
    E8 = np.repeat(np.eye(NE, dtype=f), FC * D // NE, axis=1)
    return cst, sel.reshape(128, -1), tail, E8


def kernel(**inp):
    import ml_dtypes
    import concourse.bacc as bacc
    from concourse.bass_utils import run_bass_kernel_spmd

    a = {k: np.asarray(v) for k, v in inp.items()}
    bf = ml_dtypes.bfloat16
    cst, sel, tail, E8 = constants()

    def blocks(m):
        return np.concatenate([m[128 * i:128 * (i + 1)] for i in range(m.shape[0] // 128)], axis=1)

    def col(x):
        return x.reshape(-1, 1)

    wq, wk, wv = (a["L0_attn_w_qkv"][i * D:(i + 1) * D] for i in range(3))
    bq, bk, bv = (a["L0_attn_b_qkv"][i * D:(i + 1) * D] for i in range(3))
    swap = (np.arange(D) + D // 2) % D
    hj = np.arange(D)
    pa = (hj // DH) * DH + 2 * (hj % (DH // 2))
    pb = pa + 1
    w1e = np.concatenate(list(a["L1_ffn_W1"]), axis=1)
    w2e = np.concatenate(list(a["L1_ffn_W2"]), axis=0)
    fields = {
        "wA": dict(wl=blocks(a["L0_xattn_W_l"].T), w_cq=col(a["L0_xattn_w_cq"]), w_q=col(a["L0_xattn_w_q"]),
                   w_c=col(a["L0_xattn_w_c"])),
        "wB": dict(wk=a["L1_xattn_Wk"].T, wv=a["L1_xattn_Wv"].T, bk=col(a["L1_xattn_bk"])),
        "wC": dict(q=wq.T, qs=wq[swap].T, k=wk.T, ks=wk[swap].T, v=wv.T, iq=a["L0_attn_w_iq"].T,
                   ik=np.concatenate([a["L0_attn_w_ik"].T] * 2, axis=1), iw=a["L0_attn_w_iw"].T,
                   o=a["L0_attn_w_o"].T, bq=col(bq), bqs=col(bq[swap]), bk=col(bk), bks=col(bk[swap]),
                   biq=a["L0_attn_b_iq"].reshape(2, D).T, bik=col(np.concatenate([a["L0_attn_b_ik"]] * 2))),
        "wD": dict(r=a["L0_ffn_router_w"], w1=a["L0_ffn_w1"], w2=blocks(a["L0_ffn_w2"]),
                   b1=a["L0_ffn_b1"].reshape(FC, D).T),
        "wE": dict(q=a["L1_xattn_Wq"].T, o=a["L1_xattn_Wo"].T, bq=col(a["L1_xattn_bq"])),
        "wF": dict(qa=a["L1_attn_Wq"][pa].T, qb=a["L1_attn_Wq"][pb].T, ka=a["L1_attn_Wk"][pa].T,
                   kb=a["L1_attn_Wk"][pb].T,
                   v=np.concatenate([a["L1_attn_Wv"][pa].T, a["L1_attn_Wv"][pb].T], axis=1),
                   o=a["L1_attn_Wo"].T, bqa=col(a["L1_attn_bq"][pa]), bqb=col(a["L1_attn_bq"][pb]),
                   bka=col(a["L1_attn_bk"][pa]), bkb=col(a["L1_attn_bk"][pb])),
        "wG": dict(r=a["L1_ffn_router_w"], w1=w1e, w2=blocks(w2e), b1=a["L1_ffn_b1"].reshape(FC, D).T),
        "cst": cst,
    }
    arrays = {}
    for name, order in PACKS.items():
        arrays[name] = np.concatenate([fields[name][f] for f, _ in order], axis=1)
    rows = dict(b3=np.concatenate([a[f"L0_xattn_b_{k}"].reshape(1) for k in ("c", "q", "cq")]),
                b_l=a["L0_xattn_b_l"], a0_bv=bv, b_iw=a["L0_attn_b_iw"], a0_bo=a["L0_attn_b_o"],
                f0_b2=a["L0_ffn_b2"], x1_bv=a["L1_xattn_bv"], x1_bo=a["L1_xattn_bo"],
                a1_bv=np.concatenate([a["L1_attn_bv"][pa], a["L1_attn_bv"][pb]]), a1_bo=a["L1_attn_bo"],
                f1_rb=a["L1_ffn_router_b"])
    arrays["rows"] = np.concatenate([rows[f] for f, _ in ROWS]).reshape(1, -1)
    arrays["x"] = a["x"]
    arrays["ctx"] = a["ctx_1024"]
    arrays["ctxT"] = a["ctx_1024"].transpose(0, 2, 1)
    arrays["mask"] = a["mask_BxSxS2_if1"]
    arrays["maskT"] = a["mask_BxSxS2_if1"].transpose(0, 2, 1)
    arrays["b2e"] = a["L1_ffn_b2"]
    arrays["E8"] = E8
    arrays["identb"] = np.eye(128, dtype=bf)
    arrays["sel"] = sel.astype(bf)
    arrays["tail"] = tail.astype(bf)
    arrays = {f"in_{k}": np.ascontiguousarray(x) for k, x in arrays.items()}

    nc = bacc.Bacc("TRN2", target_bir_lowering=False, num_devices=1)
    A = {k[3:]: nc.dram_tensor(k, x.shape, mybir.dt.from_np(x.dtype), kind="ExternalInput").ap()
         for k, x in arrays.items()}
    out = nc.dram_tensor("out_dram", (B, S, D), F32, kind="ExternalOutput").ap()
    build(nc, A, out)
    r = run_bass_kernel_spmd(nc, [arrays], core_ids=[0])
    return r.results[0]["out_dram"]
```

```python
from contextlib import ExitStack

import numpy as np

import concourse.bass as bass
from concourse import mybir

F32 = mybir.dt.float32
BF16 = mybir.dt.bfloat16
I32 = mybir.dt.int32
ALU = mybir.AluOpType
ACT = mybir.ActivationFunctionType
AX = mybir.AxisListType

B, S, D, SK = 2, 128, 128, 2048
H, DH = 16, 8
G = H // 2
CH = SK // 128
IH, TOPK = 4, 32
NE = 8
FC = 4
EPS = 1e-5
MASK_BIG = float(2.0 ** 100)
GONE = -3.0e38
VW = 2 * (DH + 1)
RING = 4
Q_RING = 3
UNITS = B * G
V_BANK = (1, 0)
S_LEAD = 7

K_PARTS = (0, 1, 2, 0, 1, 0)
Q_PARTS = (0, 0, 0, 1, 1, 2)
NBLK = len(K_PARTS)
PART_ROWS = (0, 8, 16, 24, 48, 56)
MAX_ROW = 32

ROWS = (("b3", 3), ("b_l", D), ("a0_bv", D), ("b_iw", IH), ("a0_bo", D), ("f0_b2", D), ("x1_bv", D), ("x1_bo", D),
        ("a1_bv", 2 * D), ("a1_bo", D), ("f1_rb", NE))
PACKS = {
    "wA": (("wl", 4 * D),),
    "wB": (("wk", D), ("wv", D), ("bk", 1)),
    "wC": (("q", D), ("qs", D), ("k", D), ("ks", D), ("v", D), ("iq", 2 * D), ("ik", D), ("iw", IH), ("o", D),
           ("bq", 1), ("bqs", 1), ("bk", 1), ("bks", 1), ("biq", 2), ("bik", 1)),
    "wD": (("r", NE), ("w1", FC * D), ("w2", FC * D), ("b1", FC)),
    "wE": (("q", D), ("o", D), ("bq", 1)),
    "wF": (("qa", D), ("qb", D), ("ka", D), ("kb", D), ("v", 2 * D), ("o", D),
           ("bqa", 1), ("bqb", 1), ("bka", 1), ("bkb", 1)),
    "wG": (("r", NE), ("w1", FC * D), ("w2", FC * D), ("b1", FC)),
    "first": (("ident", D), ("w_cq", 1), ("w_q", 1), ("w_c", 1)),
    "cst": (("cos", S), ("sin", S), ("A", S), ("B", S), ("va", DH), ("vb", DH), ("na", DH), ("nb", DH),
            ("hm", H)),
}


def offsets(fields):
    at, out = 0, {}
    for name, n in fields:
        out[name] = (at, at + n)
        at += n
    return out, at


def build(nc, A, out):
    rows_at, n_rows = offsets(ROWS)
    with ExitStack() as ctx:
        def sb(name, shape, dt=F32):
            return ctx.enter_context(nc.sbuf_tensor(name, shape, dt))

        names = {}

        def sem(name):
            if name not in names:
                names[name] = ctx.enter_context(nc.semaphore(name))
            return names[name]

        packs, at = {}, {}
        for name, fields in PACKS.items():
            at[name], n = offsets(fields)
            packs[name] = sb(name, [128, n])

        def w(pack, field):
            a, b = at[pack][field]
            return packs[pack][:, a:b]

        rows = sb("rows", [128, n_rows])

        def row(field):
            a, b = rows_at[field]
            return rows[:, a:b]

        X = [sb(f"x{i}", [128, B, D]) for i in range(7)]
        XB = [sb(f"xb{i}", [128, B, D]) for i in range(2)] * 3
        h = [sb(f"h{i}", [128, B, D]) for i in range(2)] * 3
        hT = [sb(f"hT{i}", [128, B * S]) for i in range(2)] * 3
        stats = sb("stats", [128, 6, B, 6])
        mv = sb("mv", [128, 6, B, 2])
        veps = sb("veps", [128, 6, B])
        rstd = sb("rstd", [128, 6, B])
        half = sb("half", [128, B])
        identb = sb("identb", [128, 128], BF16)
        sel = sb("sel", [128, G, 3, 128], BF16)
        ctxT = sb("ctxT", [128, B, SK])
        ctxN = sb("ctxN", [128, B, CH, D])
        kparts = sb("kparts", [128, B, 3, SK], BF16)
        kst = sb("kst", [128, RING, B, SK], BF16)
        kres = sb("kres", [128, 2, 512])
        vext = sb("vext", [128, B * CH * G * VW + 32 - VW])
        P0 = sb("P0", [128, B, SK])
        PT0 = sb("PT0", [128, B, SK])
        ident = w("first", "ident")

        mask_q = P0[:, :, :].rearrange("p b k -> p (b k)").bitcast(I32)
        mask_k = PT0[:, :, :].rearrange("p b k -> p (b k)").bitcast(I32)
        mb = ctxN[:, 0, :, :].rearrange("p c d -> p (c d)").bitcast(BF16).rearrange("p (b k) -> p b k", b=B)
        mbT = ctxN[:, 1, :, :].rearrange("p c d -> p (c d)").bitcast(BF16).rearrange(
            "p (b c q) -> p b c q", b=B, c=CH)
        pt_ring = PT0[:, :, :].rearrange("p b k -> p (b k)").rearrange("p (r n) -> p r n", r=4)
        late = kparts[:, :, :, :].rearrange("p b a k -> p (b a k)").bitcast(F32)
        cut = [0]

        def lt(n):
            cut[0] += n
            return late[:, cut[0] - n:cut[0]]

        cm = sb("cm", [128, B * S])
        mx0 = sb("mx0", [128, B])
        den0 = sb("den0", [128, B])
        rden0 = sb("rden0", [128, B])
        pm0 = sb("pm0", [128, B, 4])
        cwc = sb("cwc", [128, B])
        after_keys = P0[:, 0, 0:1024]
        c2q = after_keys[:, 0:256].rearrange("p (b d) -> p b d", b=B)
        c2qT, x3T, x4T = (after_keys[:, 256 * i:256 * (i + 1)] for i in range(1, 4))
        b3 = sb("b3", [128, 1])
        rowmax = sb("rowmax", [128, B])
        rmT = sb("rmT", [B, 128])
        rsm = sb("rsm", [B, 4])
        erow = sb("erow", [B, 128])
        brow = sb("brow", [B, 128])
        batt = sb("batt", [128, B])
        q2c = sb("q2c", [128, B])
        t_region = lt(1024)
        t1, t2, t3, t4 = (t_region[:, 256 * i:256 * (i + 1)] for i in range(4))
        qr, kr = lt(256), lt(256)
        iqT, ikT = lt(512), lt(256)
        V = lt(256).rearrange("p (b d) -> p b d", b=B)
        relu_region = lt(1024)
        relu = relu_region.rearrange("p (r b i k) -> p r b i k", r=2, b=B, i=IH // 2)
        idx = [lt(256).rearrange("p (b k) -> p b k", b=B) for _ in range(2)]
        keep = lt(256).rearrange("p (b k) -> p b k", b=B)
        lg = lt(256).rearrange("p (b k) -> p b k", b=B)
        Pm = lt(256).rearrange("p (b k) -> p b k", b=B)
        PmT, aT = lt(256), lt(256)
        iw = sb("iw", [128, B, IH])
        m8 = sb("m8", [128, B, TOPK // 8, 8])
        nmx1 = sb("nmx1", [128, B])
        den1 = sb("den1", [128, B])
        rden1 = sb("rden1", [128, B])
        g0 = relu_region.rearrange("p (c t) -> p c t", c=FC)
        g5 = g0
        gw = t_region.rearrange("p (c t) -> p c t", c=FC)
        rt = sb("rt", [128, 2, 160])
        rsel = sb("rsel", [8, 256])
        E8 = sb("E8", [NE, FC * D])
        b2e = sb("b2e", [NE, D])
        ob = sb("ob", [128, B, D])
        qp = sb("qp", [128, 3, B * S], BF16)
        cut[0] = 4 * 256
        O = lt(512).rearrange("p (b n) -> p b n", b=B)
        qres, att3T, r4T = lt(256), lt(256), lt(256)
        att3 = lt(256).rearrange("p (b h n) -> p b h n", b=B, h=H)
        assert cut[0] == 4 * 256 + 6 * 256
        cut[0] += 4 * 256
        v4 = lt(1024).rearrange("p (b h n) -> p b h n", b=B, h=H)
        qr4, kr4 = lt(256), lt(256)
        n4 = lt(256).rearrange("p (b d) -> p b d", b=B)
        r4 = lt(768).rearrange("p (u b d) -> p u b d", u=3, b=B)
        qs = sb("qs", [128, Q_RING, 2, B, S], BF16)
        mt = sb("mt", [128, 2, B, 128], BF16)
        pmx = sb("pmx", [128, 2, 4, 4])
        nmx3 = sb("nmx3", [128, 2, 4])
        mres = sb("mres", [128, 2, 4])
        oq = sb("oq", [128, B, G, 2, DH + 1])
        rd3 = sb("rd3", [128, B, H])
        flagf = sb("flagf", [1, 1])
        flag = sb("flag", [1, 1], I32)
        onesb = sb("onesb", [128, 1], BF16)
        kbd = ctxT[:, :, :].rearrange("p b (h k) -> p b h k", h=H)
        sc4 = P0[:, :, :].rearrange("p b (h k) -> p b h k", h=H)
        pT4 = PT0[:, :, :].rearrange("p b (h q) -> p b h q", h=H)
        va4 = kst[:, 0, 0, :].bitcast(F32).rearrange("p (b n) -> p b n", b=B)
        vt4 = kst[:, 0, 1, :].bitcast(F32).rearrange("p (u b n) -> p u b n", u=4, b=B)
        mx4 = sb("mx4", [128, B, H])
        o4 = kst[:, 1, :, :].bitcast(F32)
        rd4 = rd3

        PS = ctx.enter_context(nc.psum_tensor("psum", [128, 8 * 512], F32))

        def bank(i, n=1):
            return PS[:, 512 * i:512 * (i + n)]

        def hidden2(c):
            return bank(4)[:, 256:512] if c == 3 else bank((5, 6, 2)[c])[:, 0:256]

        def weights_ps(c):
            return bank((6, 4, 7, 5)[c])[:, 256:512]

        def part2(b):
            return bank(7)[:, 256:384] if b else bank(3)[:, 0:128]

        kdram = nc.dram_tensor("k_parts_dram", [3, 128, B, SK], BF16, kind="Internal").ap()

        def value(b, c, g):
            o = ((b * CH + c) * G + g) * VW
            return vext[:, o:o + 32]

        block = ctx.enter_context(nc.Block())

        @block.sync
        def _(sp):
            sp.dma_start(X[0][:, :, :], A["x"].rearrange("b s d -> s b d")).then_inc(sem("ld_x"), 16)
            sp.dma_start(packs["first"][:, :], A["first"]).then_inc(sem("ld_first"), 16)
            for i in range(4):
                b, k = i // 2, (i % 2) * 1024
                sp.dma_start(ctxT[:, b, k:k + 1024], A["ctxT"][b, :, k:k + 1024]).then_inc(sem(f"ld_ctxT{i}"), 16)
            for b in range(B):
                sp.dma_start(ctxN[:, b, :, :], A["ctx"][b].rearrange("(c k) d -> k c d", k=128)).then_inc(
                    sem(f"ld_ctxN{b}"), 16)
            sp.dma_start(packs["cst"][:, :], A["cst"]).then_inc(sem("ld_cst"), 16)
            for name in ("wC", "wD", "wE"):
                sp.dma_start(packs[name][:, :], A[name]).then_inc(sem("ld_" + name), 16)
            sp.dma_start(sel[:, :, :, :].rearrange("p g a r -> p (g a r)"), A["sel"]).then_inc(sem("ld_sel"), 16)
            for b in range(B):
                sp.wait_ge(sem("k_hi"), 4 * b + 4)
                sp.wait_ge(sem("k_mid"), 4 * b + 4)
                sp.wait_ge(sem("k_lo"), 4 * b + 4)
                for a in range(3):
                    sp.dma_start(kdram[a, :, b, :], kparts[:, b, a, :]).then_inc(sem(f"k_out{b}"), 16)
            sp.wait_ge(sem("part_ps"), 1)
            for b in range(B):
                sp.dma_start(mask_q.rearrange("p (b k) -> p b k", b=B)[:, b],
                              A["mask"][b]).then_inc(sem("ld_mask"), 16)
            for b in range(B):
                sp.dma_start(mask_k.rearrange("p (b c q) -> p b c q", b=B, c=CH)[:, b],
                              A["maskT"][b].rearrange("(c k) q -> k c q", k=128)).then_inc(sem("ld_maskT"), 16)

            for e in range(2):
                for r in range(RING):
                    sp.dma_start(kst[64 * e + MAX_ROW:64 * e + PART_ROWS[4], r, :, :].rearrange("p b k -> p (b k)"),
                                 A["tail"]).then_inc(sem("ld_tail"), 16)

            def stack(g0_, n, b, to):
                for blk in range(NBLK):
                    for e in range(2):
                        src = kdram[K_PARTS[blk], :, b, :].rearrange("(g e d) k -> e d g k", e=2, d=DH)[
                            e, :, g0_:g0_ + n, :]
                        r = g0_ % RING
                        at = 64 * e + PART_ROWS[blk]
                        dst = kst[at:at + DH, r:r + n, b, :]
                        sp.dma_start(dst, src).then_inc(to, 16)

            for b in range(B):
                sp.wait_ge(sem(f"k_out{b}"), 48)
                stack(0, RING, b, sem(f"k_in{b}"))
            for name in ("wF", "wG"):
                sp.dma_start(packs[name][:, :], A[name]).then_inc(sem("ld_" + name), 16)
            sp.dma_start(E8[:, :], A["E8"]).then_inc(sem("ld_b2e"), 16)
            sp.dma_start(b2e[:, :], A["b2e"]).then_inc(sem("ld_b2e"), 16)
            for g in range(RING, G):
                sp.wait_ge(sem("st_done"), 8 * (g - RING + 1))
                for b in range(B):
                    stack(g, 1, b, sem(f"k_in_pair{g}"))
            sp.wait_ge(sem("out_ready"), 2)
            sp.dma_start(out.rearrange("b s d -> s b d"), X[6][:, :, :]).then_inc(sem("stored"), 16)
            sp.wait_ge(sem("stored"), 16)

        @block.gpsimd
        def _(pool):
            pool.memset(half[:, :], -0.5).then_inc(sem("half"), 1)

            def ln_power(i):
                pool.wait_ge(sem("ln_mv"), 2 * (i + 1))
                pool.tensor_scalar(veps[:, i, :], mv[:, i, :, 1], EPS, None, ALU.add).then_inc(sem("ln_veps"), 1)
                pool.wait_ge(sem("ln_veps"), i + 1)
                pool.wait_ge(sem("half"), 1)
                pool.tensor_tensor(rstd[:, i, :], veps[:, i, :], half[:, :], ALU.pow).then_inc(sem("ln_rstd"), 1)

            pool.memset(mt[:, :, :, :], 0.0).then_inc(sem("zeros"), 1)
            pool.memset(qs[:, :, :, :, :], 0.0).then_inc(sem("zeros"), 1)
            ln_power(0)
            pool.memset(vext[:, :], 1.0).then_inc(sem("v_ones"), 1)
            pool.memset(onesb[:, :], 1.0).then_inc(sem("onesb"), 1)
            for i in range(8):
                b, k = i // 4, (i % 4) * 512
                pool.wait_ge(sem("k_mid"), i + 1)
                pool.tensor_tensor(kparts[:, b, 2, k:k + 512], kres[:, i % 2, :], kparts[:, b, 1, k:k + 512],
                                   ALU.subtract).then_inc(sem("k_lo"), 1)
            ln_power(1)
            pool.wait_ge(sem("ld_cst"), 16)
            for i, (t, tab) in enumerate(((t3, "cos"), (t4, "sin"))):
                pool.wait_ge(sem("qk_b"), i + 1)
                pool.tensor_tensor(t.rearrange("p (b s) -> p b s", b=B), t.rearrange("p (b s) -> p b s", b=B),
                                   w("cst", tab).unsqueeze(1).to_broadcast([128, B, S]), ALU.mult).then_inc(
                    sem("qk_turn"), 1)
            pool.wait_ge(sem("qk_turn"), 2)
            pool.tensor_tensor(kr, t3, t4, ALU.add).then_inc(sem("k_rotated"), 1)
            ln_power(2)
            ln_power(3)
            pool.memset(v4, 0.0).then_inc(sem("v4_set"), 1)
            pool.wait_ge(sem("v4_set"), 1)
            pool.memset(v4[:, :, :, DH:DH + 1], 1.0).then_inc(sem("v4_set"), 1)

            def max_parts(u):
                g, b = u // B, u % B
                pool.wait_ge(sem("nmx3"), u + 1)
                if u >= 2 * B:
                    pool.wait_ge(sem("stackm_ps"), u - 2 * B + 1)
                at_part = [mt[:, g % 2, b, :].rearrange("p (e m) -> p e m", e=2)[:, :, MAX_ROW + a]
                           for a in range(3)]
                nm, mr = nmx3[:, g % 2, 2 * b:2 * b + 2], mres[:, g % 2, 2 * b:2 * b + 2]
                pool.tensor_copy(at_part[0], nm).then_inc(sem("mt_part"), 1)
                pool.wait_ge(sem("mt_part"), 3 * u + 1)
                pool.tensor_tensor(mr, nm, at_part[0], ALU.subtract).then_inc(sem("mt_part"), 1)
                pool.wait_ge(sem("mt_part"), 3 * u + 2)
                pool.tensor_copy(at_part[1], mr).then_inc(sem("mt_part"), 1)
                pool.wait_ge(sem("mt_part"), 3 * u + 3)
                pool.tensor_tensor(at_part[2], mr, at_part[1], ALU.subtract).then_inc(sem("mt"), 1)

            pool.wait_ge(sem("zeros"), 2)
            for u in range(UNITS):
                max_parts(u)
            ln_power(4)
            pool.wait_ge(sem("rotated4"), 1)
            for n in (0, *range(2, 8)):
                b, hs = n // 4, slice(4 * (n % 4), 4 * (n % 4) + 4)
                pool.tensor_tensor(kbd[:, b, hs, :],
                                   kr4[:, 128 * b:128 * b + 128].unsqueeze(1).to_broadcast([128, 4, 128]),
                                   w("cst", "hm")[:, hs].unsqueeze(2).to_broadcast([128, 4, 128]),
                                   ALU.mult).then_inc(sem("kbd_pool"), 1)
            pool.wait_ge(sem("va4"), 1)
            pool.wait_ge(sem("ld_rows"), 16)
            pool.tensor_tensor(va4[:, :, 0:256], va4[:, :, 0:256],
                               row("a1_bv").unsqueeze(1).to_broadcast([128, B, 2 * D]), ALU.add).then_inc(
                sem("vb4"), 1)
            pool.wait_ge(sem("vb4"), 1)

            def by_head(ap):
                return ap.rearrange("p b (h n) -> p b h n", h=H)

            for u, tab in ((0, "va"), (1, "vb")):
                pool.tensor_tensor(by_head(vt4[:, u, :, :]), by_head(va4[:, :, D * u:D * (u + 1)]),
                                   w("cst", tab).unsqueeze(1).unsqueeze(1).to_broadcast([128, B, H, DH]),
                                   ALU.mult).then_inc(sem("vt4"), 1)
            pool.wait_ge(sem("vt4"), 2)
            pool.wait_ge(sem("v4_set"), 2)
            pool.tensor_tensor(v4[:, :, :, 0:DH], by_head(vt4[:, 0, :, :]), by_head(vt4[:, 1, :, :]),
                               ALU.add).then_inc(sem("v4"), 1)
            ln_power(5)

        @block.scalar
        def _(act):
            act.dma_start(rows[:, :], A["rows"].to_broadcast([128, n_rows])).then_inc(sem("ld_rows"), 16)
            act.dma_start(packs["wB"][:, :], A["wB"]).then_inc(sem("ld_wB"), 16)
            act.dma_start(packs["wA"][:, :], A["wA"]).then_inc(sem("ld_wA"), 16)
            act.dma_start(identb[:, :], A["identb"]).then_inc(sem("ld_identb"), 16)
            act.preload_act_table(ACT.Exp)

            def ln_turned(i, src):
                act.wait_ge(sem("ln_hT_ps"), i + 1)
                act.activation(hT[i][:, :], src, ACT.Copy).then_inc(sem("ln_hT"), 1)

            ln_turned(0, bank(4)[:, 0:256])

            def key_hi(i):
                b, k = i // 4, (i % 4) * 512
                act.wait_ge(sem("k_ps"), i + 1)
                act.activation(kparts[:, b, 0, k:k + 512], bank(6 + i % 2), ACT.Identity,
                               bias=w("wB", "bk")).then_inc(sem("k_hi"), 1)

            def probs0(b):
                act.wait_ge(sem("mx0"), b + 1)
                act.activation(P0[:, b, :], bank(4 * b, 4), ACT.Exp, bias=mx0[:, b:b + 1],
                               accum_out=den0[:, b:b + 1]).then_inc(sem("probs"), 1)

            def turned0(b, j):
                act.wait_ge(sem("pT_ps"), 4 * b + j + 1)
                act.activation(PT0[:, b, 512 * j:512 * (j + 1)], bank(1), ACT.Copy).then_inc(sem("pT_act"), 1)

            probs0(0)
            probs0(1)
            turned0(0, 1)
            act.wait_ge(sem("ld_wB"), 16)
            key_hi(0)
            act.wait_ge(sem("rm_max"), 1)
            act.activation(erow[:, :], rmT[:, :], ACT.Exp, bias=rsm[:, 0:1], accum_out=rsm[:, 1:2]).then_inc(
                sem("erow"), 1)
            key_hi(1)
            turned0(0, 3)
            key_hi(2)
            key_hi(3)
            turned0(1, 1)
            key_hi(4)
            key_hi(5)
            turned0(1, 3)
            key_hi(6)
            act.wait_ge(sem("turn_ps"), 1)
            act.activation(c2qT, bank(5)[:, 256:512], ACT.Copy).then_inc(sem("turned"), 1)
            key_hi(7)
            def value_out(i):
                act.wait_ge(sem("v_ones"), 1)
                act.wait_ge(sem("v_ps"), i + 1)
                o = (4 * i) * G * VW
                act.activation(
                    vext[:, o:o + 4 * G * VW].rearrange("p (m n) -> p m n", n=DH + 1)[:, :, 0:DH],
                    bank(V_BANK[i % 2]).rearrange("p (m n) -> p m n", n=DH), ACT.Copy).then_inc(sem("v_set"), 1)

            for i in range(3):
                value_out(i)
            ln_turned(1, bank(4)[:, 0:256])
            act.wait_ge(sem("k_out0"), 48)
            act.wait_ge(sem("iq_ps"), 1)
            for j in range(2):
                act.activation(iqT[:, 256 * j:256 * (j + 1)], bank(2)[:, 256 * j:256 * (j + 1)], ACT.Identity,
                               bias=w("wC", "biq")[:, j:j + 1]).then_inc(sem("index_T"), 1)
            act.activation(ikT, bank(3)[:, 0:256], ACT.Identity, bias=w("wC", "bik")).then_inc(sem("index_T"), 1)
            act.wait_ge(sem("k_out1"), 48)
            for r in range(2):
                act.wait_ge(sem("hs_ps"), r + 1)
                act.activation(relu_region[:, 512 * r:512 * r + 512], bank(5 + r), ACT.Relu).then_inc(
                    sem("relu"), 1)
            act.wait_ge(sem("qk_ps"), 2)
            for i, (t, bias) in enumerate(((t3, "bk"), (t4, "bks"))):
                act.activation(t, bank(1)[:, 256 * i:256 * i + 256], ACT.Identity,
                               bias=w("wC", bias)).then_inc(sem("qk_b"), 1)
            for i in range(3, 6):
                value_out(i)

            for b in range(B):
                act.wait_ge(sem("nmx1"), b + 1)
                act.activation(Pm[:, b, :], lg[:, b, :], ACT.Exp, bias=nmx1[:, b:b + 1],
                               accum_out=den1[:, b:b + 1]).then_inc(sem("probs"), 1)
            act.wait_ge(sem("turn_ps"), 2)
            act.activation(PmT, bank(0)[:, 0:256], ACT.Copy).then_inc(sem("turned"), 1)
            act.wait_ge(sem("turn_ps"), 3)
            act.activation(aT, bank(1)[:, 0:256], ACT.Copy).then_inc(sem("turned"), 1)

            ln_turned(2, bank(4)[:, 0:256])

            def router_exp(i):
                act.wait_ge(sem("rt_max"), i + 1)
                for b in range(B):
                    act.activation(rt[:, i, 8 * b:8 * b + 8], rt[:, i, 16 + 8 * b:24 + 8 * b], ACT.Exp,
                                   bias=rt[:, i, 32 + b:33 + b],
                                   accum_out=rt[:, i, 34 + b:35 + b]).then_inc(sem("rt_exp"), 1)

            router_exp(0)
            act.preload_act_table(ACT.Gelu_apprx_tanh)
            for c in range(FC):
                act.wait_ge(sem("hidden_ps"), c + 1)
                act.activation(g0[:, c, :], hidden2(c), ACT.Gelu_apprx_tanh,
                               bias=w("wD", "b1")[:, c:c + 1]).then_inc(sem("gelu"), 1)
            act.preload_act_table(ACT.Exp)
            value_out(6)
            value_out(7)

            ln_turned(3, bank(4)[:, 0:256])
            act.wait_ge(sem("q3_ps"), 1)
            act.activation(qp[:, 0, :], bank(5)[:, 0:256], ACT.Identity, bias=w("wE", "bq")).then_inc(
                sem("q3_hi"), 1)

            def query_stack(g):
                act.wait_ge(sem("stack_ps"), g + 1)
                if g == 0:
                    act.wait_ge(sem("zeros"), 2)
                if g >= Q_RING:
                    act.wait_ge(sem("st_done"), 8 * (g - Q_RING + 1))
                for e in range(2):
                    p = slice(64 * e, 64 * e + 64)
                    act.activation(qs[p, g % Q_RING, e, :, :].rearrange("p b q -> p (b q)"), bank(7)[p, 0:256],
                                   ACT.Copy).then_inc(sem("qs"), 1)

            def query_stack_max(u):
                g, b = u // B, u % B
                act.wait_ge(sem("stackm_ps"), u + 1)
                act.wait_ge(sem("s_done"), 8 * u + 8)
                for e in range(2):
                    p = slice(64 * e + MAX_ROW, 64 * e + MAX_ROW + 3)
                    act.activation(qs[p, g % Q_RING, e, b, :], bank(7)[p, 0:128], ACT.Copy).then_inc(sem("qt"), 1)

            def out_rows(g, b):
                act.wait_ge(sem("pv_done"), 8 * g + 4 * b + 4)
                if g >= 1:
                    act.wait_ge(sem("oq_ps"), 2 * g - 1 + b)
                act.activation(O[:, b, :], bank(6)[:, 0:256], ACT.Copy).then_inc(sem("o_rows"), 1)

            query_stack(0)
            query_stack(1)
            query_stack_max(0)
            for n in range(8 * G):
                g, j = n // 8, n % 8
                if j == 5 and g + 2 < G:
                    query_stack(g + 2)
                if n % 4 == 3 and n // 4 + 1 < UNITS:
                    query_stack_max(n // 4 + 1)
                act.wait_ge(sem("st_done"), n + 1)
                if n == 0:
                    act.wait_ge(sem("mask_bias"), 4)
                if n >= 4:
                    act.wait_ge(sem("pv_done"), n - 3)
                act.activation(pt_ring[:, n % 4, :], bank(2 + 2 * (n % 2), 2), ACT.Exp, scale=DH ** -0.5).then_inc(
                    sem("p3"), 1)
                if j == 4:
                    out_rows(g, 0)
                if j == 0 and g:
                    out_rows(g - 1, 1)
            out_rows(G - 1, 1)
            act.wait_ge(sem("turn_ps"), 4)
            act.activation(att3T[:, :], bank(0)[:, 0:256], ACT.Copy).then_inc(sem("turned"), 1)

            ln_turned(4, bank(4)[:, 0:256])
            act.wait_ge(sem("v4_ps"), 1)
            act.activation(va4[:, :, 0:256], bank(2).rearrange("p (b n) -> p b n", b=B), ACT.Copy).then_inc(
                sem("va4"), 1)

            def probs4(n):
                act.wait_ge(sem("p4T_ps"), n + 1)
                act.activation(pT4[:, n // 4, 4 * (n % 4):4 * (n % 4) + 4, :].rearrange("p h q -> p (h q)"),
                               bank(3 if n % 2 else 7), ACT.Copy).then_inc(sem("p4T"), 1)

            def out4(b):
                act.wait_ge(sem("o4_ps"), b + 1)
                act.activation(o4[:, b, 0:512], bank(b), ACT.Copy).then_inc(sem("o4"), 1)

            for n in range(8):
                b, hs = n // 4, slice(4 * (n % 4), 4 * (n % 4) + 4)
                act.wait_ge(sem("sub4"), n + 1)
                act.activation(sc4[:, b, hs, :], sc4[:, b, hs, :], ACT.Exp, scale=DH ** -0.5).then_inc(
                    sem("exp4"), 1)
                if n == 7:
                    out4(0)
                if n:
                    probs4(n - 1)
            probs4(7)
            out4(1)
            act.wait_ge(sem("turn_ps"), 5)
            act.activation(r4T[:, :], bank(7)[:, 0:256], ACT.Copy).then_inc(sem("turned"), 1)

            ln_turned(5, bank(4)[:, 0:256])
            router_exp(1)
            act.preload_act_table(ACT.Gelu)
            for c in range(FC):
                act.wait_ge(sem("hidden_ps"), c + 1 + 4)
                act.activation(g5[:, c, :], bank(c)[:, 0:256], ACT.Gelu, bias=w("wG", "b1")[:, c:c + 1]).then_inc(
                    sem("gelu"), 1)

        @block.vector
        def _(v):
            links = [0]

            def link(ins):
                links[0] += 1
                ins.then_inc(sem("dve_link"), 1)
                v.wait_ge(sem("dve_link"), links[0])

            def ln_stats(i):
                for b in range(B):
                    v.bn_stats(stats[:, i, b, :], X[i][:, b, :]).then_inc(sem("ln_stats"), 1)
                for b in range(B):
                    v.wait_ge(sem("ln_stats"), 2 * i + b + 1)
                    v.bn_aggr(mv[:, i, b, :], stats[:, i, b, :]).then_inc(sem("ln_mv"), 1)

            def ln_apply(i):
                v.wait_ge(sem("ln_mv"), 2 * i + 2)
                v.wait_ge(sem("ln_rstd"), i + 1)
                for b in range(B):
                    v.tensor_scalar(h[i][:, b, :], X[i][:, b, :], mv[:, i, b, 0:1], rstd[:, i, b:b + 1],
                                    ALU.subtract, ALU.mult).then_inc(sem("ln_h"), 1)

            def with_bias(i, name):
                v.tensor_tensor(XB[i][:, :, :], X[i][:, :, :], row(name).unsqueeze(1).to_broadcast([128, B, D]),
                                ALU.add).then_inc(sem("xb"), 1)

            v.wait_ge(sem("ld_x"), 16)
            ln_stats(0)
            ln_apply(0)
            v.wait_ge(sem("ld_rows"), 16)
            link(v.tensor_reduce(b3[:, :], row("b3"), AX.X, ALU.add))
            v.wait_ge(sem("ln_hT"), 1)
            v.wait_ge(sem("ld_first"), 16)
            v.tensor_scalar(cm[:, :], hT[0][:, :], w("first", "w_cq"), w("first", "w_q"), ALU.mult, ALU.add).then_inc(
                sem("cm"), 1)

            def key_rest(i):
                b, k = i // 4, (i % 4) * 512
                v.wait_ge(sem("k_hi"), i + 1)
                if i >= 2:
                    v.wait_ge(sem("k_lo"), i - 1)
                v.scalar_tensor_tensor(kres[:, i % 2, :], bank(6 + i % 2), w("wB", "bk"), kparts[:, b, 0, k:k + 512],
                                       ALU.add, ALU.subtract).then_inc(sem("k_res"), 1)
                v.wait_ge(sem("k_res"), i + 1)
                v.tensor_copy(kparts[:, b, 1, k:k + 512], kres[:, i % 2, :]).then_inc(sem("k_mid"), 1)

            def chunk_max(b, j):
                v.wait_ge(sem("s0_ps"), 4 * b + j + 1)
                v.tensor_reduce(pm0[:, b, j:j + 1], bank(4 * b + j), AX.X, ALU.max).then_inc(sem("pm0"), 1)

            def row_max(b):
                v.wait_ge(sem("pm0"), 4 * b + 4)
                v.tensor_reduce(mx0[:, b:b + 1], pm0[:, b, :], AX.X, ALU.max, negate=True).then_inc(sem("mx0"), 1)

            def turned(b, j):
                v.wait_ge(sem("pT_ps"), 4 * b + j + 1)
                v.tensor_copy(PT0[:, b, 512 * j:512 * (j + 1)], bank(0)).then_inc(sem("pT_dve"), 1)

            for j in range(4):
                chunk_max(0, j)
            row_max(0)
            v.wait_ge(sem("cwc_ps"), 1)
            v.tensor_scalar(cwc[:, :], bank(7)[:, 0:B], b3[:, 0:1], None, ALU.add).then_inc(sem("cwc"), 1)
            for j in range(4):
                chunk_max(1, j)
            row_max(1)
            v.wait_ge(sem("mx0"), 2)
            v.wait_ge(sem("cwc"), 1)
            v.tensor_tensor(rowmax[:, :], cwc[:, :], mx0[:, :], ALU.subtract).then_inc(sem("rowmax"), 1)
            turned(0, 0)
            with_bias(0, "b_l")
            turned(0, 2)
            v.wait_ge(sem("ld_wB"), 16)
            v.wait_ge(sem("rm_ps"), 1)
            link(v.tensor_copy(rmT[:, :], bank(4)[0:B, 0:128]))
            v.tensor_reduce(rsm[:, 0:1], rmT[:, :], AX.X, ALU.max, negate=True).then_inc(sem("rm_max"), 1)
            key_rest(0)
            key_rest(1)
            v.wait_ge(sem("erow"), 1)
            link(v.reciprocal(rsm[:, 2:3], rsm[:, 1:2]))
            v.tensor_scalar(brow[:, :], erow[:, :], rsm[:, 2:3], None, ALU.mult).then_inc(sem("brow"), 1)
            key_rest(2)
            turned(1, 0)
            v.wait_ge(sem("batt_ps"), 1)
            v.tensor_copy(batt[:, :], bank(4)[:, 128:128 + B]).then_inc(sem("batt"), 1)
            v.wait_ge(sem("probs"), 2)
            link(v.reciprocal(rden0[:, :], den0[:, :]))
            key_rest(3)

            def c2q_out(b):
                v.wait_ge(sem("c2q_ps"), b + 1)
                v.tensor_scalar(c2q[:, b, :], bank(2 + b)[:, 0:128], rden0[:, b:b + 1], None, ALU.mult).then_inc(
                    sem("c2q"), 1)

            c2q_out(0)
            key_rest(4)
            v.wait_ge(sem("q2c_ps"), 1)
            link(v.tensor_copy(q2c[:, :], bank(5)[:, 0:B]))
            v.tensor_scalar(x4T[:, 0:128], hT[0][:, 0:128], q2c[:, 0:1], None, ALU.mult).then_inc(sem("x4T"), 1)
            v.tensor_scalar(x4T[:, 128:256], hT[0][:, 128:256], q2c[:, 1:2], None, ALU.mult).then_inc(sem("x4T"), 1)
            turned(1, 2)
            key_rest(5)
            c2q_out(1)
            key_rest(6)
            v.wait_ge(sem("turned"), 1)
            v.tensor_tensor(x3T[:, :], hT[0][:, :], c2qT[:, :], ALU.mult).then_inc(sem("x3T"), 1)
            key_rest(7)
            v.wait_ge(sem("xb"), 1)
            v.wait_ge(sem("part_ps"), 1)
            v.tensor_tensor(X[1][:, :, :], XB[0][:, :, :], bank(4)[:, 256:512].rearrange("p (b d) -> p b d", b=B),
                            ALU.add).then_inc(sem("x_ready"), 1)

            v.wait_ge(sem("x_ready"), 1)
            ln_stats(1)
            with_bias(1, "a0_bo")
            ln_apply(1)
            v.wait_ge(sem("k_out0"), 48)
            v.wait_ge(sem("ld_wC"), 16)

            def over_b(ap):
                return ap.unsqueeze(1).to_broadcast([128, B, S])

            def by_b(ap):
                return ap.rearrange("p (b s) -> p b s", b=B)

            def rotate(dst, ps, bias, bias_s, ta, tb, cos, sin, name):
                v.scalar_tensor_tensor(by_b(ta), by_b(ps[:, 0:256]), bias, over_b(cos), ALU.add,
                                       ALU.mult).then_inc(sem("rot"), 1)
                v.scalar_tensor_tensor(by_b(tb), by_b(ps[:, 256:512]), bias_s, over_b(sin), ALU.add,
                                       ALU.mult).then_inc(sem("rot"), 1)
                rots[0] += 2
                v.wait_ge(sem("rot"), rots[0])
                v.tensor_tensor(dst, ta, tb, ALU.add).then_inc(sem(name), 1)

            rots = [0]
            v.wait_ge(sem("ld_cst"), 16)
            v.wait_ge(sem("qk_ps"), 1)
            rotate(qr, bank(0), w("wC", "bq"), w("wC", "bqs"), t1, t2, w("cst", "cos"), w("cst", "sin"), "rotated")
            v.wait_ge(sem("iw_ps"), 1)
            v.tensor_tensor(iw[:, :, :], bank(7)[:, 256:256 + B * IH].rearrange("p (b h) -> p b h", b=B),
                            row("b_iw").unsqueeze(1).to_broadcast([128, B, IH]), ALU.add).then_inc(sem("iw"), 1)
            v.tensor_tensor(V, bank(7)[:, 0:256].rearrange("p (b d) -> p b d", b=B),
                            row("a0_bv").unsqueeze(1).to_broadcast([128, B, D]), ALU.add).then_inc(sem("V"), 1)

            v.wait_ge(sem("iw"), 1)
            v.wait_ge(sem("k_out1"), 48)
            for i in range(IH):
                for b in range(B):
                    v.wait_ge(sem("relu"), i % 2 + 1)
                    if i == 0:
                        v.tensor_scalar(idx[0][:, b, :], relu[:, 0, b, 0, :], iw[:, b, 0:1], None, ALU.mult).then_inc(
                            sem("idx"), 1)
                    else:
                        v.wait_ge(sem("idx"), 2 * (i - 1) + b + 1)
                        v.scalar_tensor_tensor(idx[i % 2][:, b, :], relu[:, i % 2, b, i // 2, :], iw[:, b, i:i + 1],
                                               idx[(i - 1) % 2][:, b, :], ALU.mult, ALU.add).then_inc(sem("idx"), 1)
            for r in range(TOPK // 8):
                src, dst = idx[(IH - 1 + r) % 2], idx[(IH + r) % 2]
                for b in range(B):
                    if r == 0:
                        v.wait_ge(sem("idx"), 2 * (IH - 1) + b + 1)
                    else:
                        v.wait_ge(sem("taken"), 2 * (r - 1) + b + 1)
                    v.max(m8[:, b, r, :], src[:, b, :]).then_inc(sem("m8"), 1)
                for b in range(B):
                    v.wait_ge(sem("m8"), 2 * r + b + 1)
                    v.match_replace(dst[:, b, :], m8[:, b, r, :], src[:, b, :], GONE).then_inc(sem("taken"), 1)
            last = idx[(IH + TOPK // 8 - 1) % 2]
            v.wait_ge(sem("lg_ps"), 1)
            for b in range(B):
                v.wait_ge(sem("taken"), 2 * (TOPK // 8 - 1) + b + 1)
                link(v.tensor_scalar(keep[:, b, :], last[:, b, :], GONE * 0.99, -1.0e30, ALU.is_gt, ALU.mult))
                link(v.scalar_tensor_tensor(lg[:, b, :], bank(7)[:, 128 * b:128 * b + 128], float(D) ** -0.5,
                                            keep[:, b, :], ALU.mult, ALU.add))
                v.tensor_reduce(nmx1[:, b:b + 1], lg[:, b, :], AX.X, ALU.max, negate=True).then_inc(sem("nmx1"), 1)
            v.wait_ge(sem("probs"), 4)
            link(v.reciprocal(rden1[:, :], den1[:, :]))

            def mask_bias(to, of, loaded, halves=(0, 1)):
                v.wait_ge(sem(loaded), 16 * B)
                v.wait_ge(sem("c2q_ps"), 2)
                for i in halves:
                    part = slice(i * SK, (i + 1) * SK)
                    v.tensor_scalar(to[:, part], of[:, part], 0.0, -MASK_BIG, ALU.is_equal, ALU.mult).then_inc(
                        sem("mask_bias"), 1)

            mask_bias(mb.rearrange("p b k -> p (b k)"), mask_q, "ld_mask")
            v.wait_ge(sem("xb"), 2)
            v.wait_ge(sem("part_ps"), 2)
            for b in range(B):
                v.scalar_tensor_tensor(X[2][:, b, :], bank(3)[:, 128 * b:128 * b + 128], rden1[:, b:b + 1],
                                       XB[1][:, b, :], ALU.mult, ALU.add).then_inc(sem("x_ready"), 1)

            v.wait_ge(sem("x_ready"), 3)
            ln_stats(2)
            ln_apply(2)
            v.wait_ge(sem("flag_ps"), 1)
            link(v.tensor_reduce(flagf[:, :], bank(1)[0:1, :], AX.X, ALU.min))
            v.tensor_scalar(flag[:, :], flagf[:, :], 0.0, None, ALU.is_lt).then_inc(sem("flag"), 1)

            def router(i, ps):
                lgt = rt[:, i, 16:32].rearrange("p (b n) -> p b n", b=B)
                if i == 0:
                    link(v.tensor_copy(lgt, ps))
                else:
                    link(v.tensor_tensor(lgt, ps, row("f1_rb").unsqueeze(1).to_broadcast([128, B, NE]), ALU.add))
                v.tensor_reduce(rt[:, i, 32:34], lgt, AX.X, ALU.max, negate=True).then_inc(sem("rt_max"), 1)

            def router_top(i):
                v.wait_ge(sem("rt_exp"), 2 * i + 2)
                link(v.reciprocal(rt[:, i, 68:70], rt[:, i, 34:36]))
                for b in range(B):
                    ins = v.tensor_scalar(rt[:, i, 36 + 8 * b:44 + 8 * b], rt[:, i, 8 * b:8 * b + 8],
                                          rt[:, i, 68 + b:69 + b], None, ALU.mult)
                    ins.then_inc(sem("rt_p"), 1)
                for b in range(B):
                    v.wait_ge(sem("rt_p"), 2 * i + b + 1)
                    v.max(rt[:, i, 52 + 8 * b:60 + 8 * b], rt[:, i, 36 + 8 * b:44 + 8 * b]).then_inc(sem("rt_m8"), 1)
                v.wait_ge(sem("rt_m8"), 2 * i + 2)
                top = rt[:, i, 52:68].rearrange("p (b n) -> p b n", b=B)
                link(v.tensor_tensor(rt[:, i, 70:72], top[:, :, 0], top[:, :, 1], ALU.add))
                link(v.reciprocal(rt[:, i, 72:74], rt[:, i, 70:72]))
                return top

            v.wait_ge(sem("router_ps"), 1)
            router(0, bank(7)[:, 0:16].rearrange("p (b n) -> p b n", b=B))
            top = router_top(0)
            link(v.tensor_tensor(rt[:, 0, 74:78].rearrange("p (b n) -> p b n", b=B), top[:, :, 0:2],
                                 rt[:, 0, 72:74].unsqueeze(2).to_broadcast([128, B, 2]), ALU.mult))
            link(v.tensor_reduce(rt[:, 0, 78:80], rt[:, 0, 74:78].rearrange("p (b n) -> p b n", b=B), AX.X, ALU.add))
            for b in range(B):
                v.scalar_tensor_tensor(XB[2][:, b, :], row("f0_b2"), rt[:, 0, 78 + b:79 + b], X[2][:, b, :],
                                       ALU.mult, ALU.add).then_inc(sem("xb"), 1)
            mask_bias(mbT.rearrange("p b c q -> p (b c q)"), mask_k, "ld_maskT", halves=(0,))
            v.wait_ge(sem("xb"), 4)
            v.wait_ge(sem("part_ps"), 3)
            for b in range(B):
                v.scalar_tensor_tensor(X[3][:, b, :], part2(b), rt[:, 0, 78 + b:79 + b],
                                       XB[2][:, b, :], ALU.mult, ALU.add).then_inc(sem("x_ready"), 1)

            v.wait_ge(sem("x_ready"), 5)
            ln_stats(3)
            with_bias(3, "x1_bo")
            ln_apply(3)
            mask_bias(mbT.rearrange("p b c q -> p (b c q)"), mask_k, "ld_maskT", halves=(1,))
            v.wait_ge(sem("ld_wE"), 16)
            v.wait_ge(sem("q3_hi"), 1)
            link(v.scalar_tensor_tensor(qres[:, :], bank(5)[:, 0:256], w("wE", "bq"), qp[:, 0, :], ALU.add,
                                        ALU.subtract))
            v.tensor_copy(qp[:, 1, :], qres[:, :]).then_inc(sem("q3_mid"), 1)
            v.wait_ge(sem("q3_mid"), 1)
            v.tensor_tensor(qp[:, 2, :], qres[:, :], qp[:, 1, :], ALU.subtract).then_inc(sem("q3_lo"), 1)
            def unit_max(u):
                r, of = u // B % 2, slice(2 * (u % B), 2 * (u % B) + 2)
                v.wait_ge(sem("s_red"), 8 * u + 8)
                if u >= 2 * B:
                    v.wait_ge(sem("mt"), u - 2 * B + 1)
                v.tensor_reduce(nmx3[:, r, of], pmx[:, r, of, :], AX.X, ALU.max, negate=True).then_inc(
                    sem("nmx3"), 1)

            def pair_out(g):
                v.wait_ge(sem("oq_ps"), 2 * g + 2)
                tiles = bank(7).rearrange("p (b e c r) -> p b e r c", b=B, e=2, c=4)
                for e in range(2):
                    v.tensor_reduce(oq[:, :, g, e, :], tiles[:, :, e, (DH + 1) * e:(DH + 1) * (e + 1), :], AX.X,
                                    ALU.add).then_inc(sem("oq"), 1)

            for m in range(16 * G):
                g, i = m // 16, m % 16
                v.wait_ge(sem("s_done"), m + 1)
                v.tensor_reduce(pmx[:, g % 2, i // 4, i % 4:i % 4 + 1], bank(m % 2), AX.X, ALU.max).then_inc(
                    sem("s_red"), 1)
                if m == 7:
                    unit_max(0)
                elif m > 8 and m % 8 == 0:
                    unit_max(m // 8 - 1)
                if i == 2 and g >= 2:
                    pair_out(g - 2)
            unit_max(UNITS - 1)
            heads = oq[:, :, :, :, :].rearrange("p b g e n -> p b (g e) n")
            for k, hs in ((G - 2, slice(0, H - 2)), (G - 1, slice(H - 2, H))):
                pair_out(k)
                v.wait_ge(sem("oq"), 2 * (k + 1))
                n = hs.stop - hs.start
                link(v.reciprocal(rd3[:, :, hs], heads[:, :, hs, DH]))
                link(v.tensor_tensor(att3[:, :, hs, :], heads[:, :, hs, 0:DH],
                                     rd3[:, :, hs].unsqueeze(3).to_broadcast([128, B, n, DH]), ALU.mult))
                v.tensor_tensor(ob[:, :, DH * hs.start:DH * hs.stop].rearrange("p b (h n) -> p b h n", h=n),
                                att3[:, :, hs, :],
                                row("x1_bv")[:, DH * hs.start:DH * hs.stop].rearrange(
                                    "p (h n) -> p h n", h=n).unsqueeze(1).to_broadcast([128, B, n, DH]),
                                ALU.add).then_inc(sem("att3"), 1)
            v.wait_ge(sem("xb"), 5)
            v.wait_ge(sem("part_ps"), 4)
            v.tensor_tensor(X[4][:, :, :], XB[3][:, :, :], bank(1)[:, 0:256].rearrange("p (b d) -> p b d", b=B),
                            ALU.add).then_inc(sem("x_ready"), 1)

            v.wait_ge(sem("x_ready"), 6)
            ln_stats(4)
            with_bias(4, "a1_bo")
            ln_apply(4)
            v.wait_ge(sem("qk4_ps"), 1)
            v.wait_ge(sem("ld_wF"), 16)
            a4 = [r4[:, i, :, :].rearrange("p b d -> p (b d)") for i in range(2)]
            b4 = [n4[:, :, :].rearrange("p b d -> p (b d)"), r4[:, 2, :, :].rearrange("p b d -> p (b d)")]
            rotate(kr4[:, :], bank(1), w("wF", "bka"), w("wF", "bkb"), b4[0], b4[1], w("cst", "A"), w("cst", "B"),
                   "rotated4")
            v.wait_ge(sem("qk4_ps"), 2)
            rotate(qr4[:, :], bank(0), w("wF", "bqa"), w("wF", "bqb"), a4[0], a4[1], w("cst", "A"), w("cst", "B"),
                   "rotated4")
            v.wait_ge(sem("rotated4"), 1)
            v.tensor_tensor(kbd[:, 0, 4:8, :], kr4[:, 0:128].unsqueeze(1).to_broadcast([128, 4, 128]),
                            w("cst", "hm")[:, 4:8].unsqueeze(2).to_broadcast([128, 4, 128]),
                            ALU.mult).then_inc(sem("kbd_dve"), 1)

            def heads4(n):
                return bank(4 + n % 3).rearrange("p (h k) -> p h k", h=4), n // 4, slice(4 * (n % 4), 4 * (n % 4) + 4)

            def sub4(n):
                sc, b, hs = heads4(n)
                v.wait_ge(sem("mx4"), n + 1)
                v.tensor_tensor(sc4[:, b, hs, :], sc, mx4[:, b, hs].unsqueeze(2).to_broadcast([128, 4, S]),
                                ALU.subtract).then_inc(sem("sub4"), 1)

            for n in range(8):
                sc, b, hs = heads4(n)
                v.wait_ge(sem("s4_ps"), n + 1)
                v.tensor_reduce(mx4[:, b, hs], sc, AX.X, ALU.max).then_inc(sem("mx4"), 1)
                if n:
                    sub4(n - 1)
            sub4(7)
            for b in range(B):
                o = bank(6 - 2 * b).rearrange("p (h n) -> p h n", h=H)
                v.wait_ge(sem("o4T_ps"), b + 1)
                v.reciprocal(rd4[:, b, :], o[:, :, DH]).then_inc(sem("rd4"), 1)
                v.wait_ge(sem("rd4"), b + 1)
                v.tensor_tensor(n4[:, b, :].rearrange("p (h n) -> p h n", h=H), o[:, :, 0:DH],
                                rd4[:, b, :].unsqueeze(2).to_broadcast([128, H, DH]), ALU.mult).then_inc(
                    sem("n4"), 1)
                v.wait_ge(sem("n4"), b + 1)
                pairs = n4[:, b, :].rearrange("p (h m t) -> p h m t", m=4, t=2)
                for u, tab in ((0, "na"), (1, "nb")):
                    v.tensor_tensor(r4[:, u, b, :].rearrange("p (h f m) -> p h f m", h=H, f=2),
                                    pairs[:, :, :, u].unsqueeze(2).to_broadcast([128, H, 2, 4]),
                                    w("cst", tab).rearrange("p (f m) -> p f m", f=2).unsqueeze(1).to_broadcast(
                                        [128, H, 2, 4]), ALU.mult).then_inc(sem("rot4"), 1)
                v.wait_ge(sem("rot4"), 2 * b + 2)
                v.tensor_tensor(r4[:, 2, b, :], r4[:, 0, b, :], r4[:, 1, b, :], ALU.add).then_inc(sem("r4"), 1)
            v.wait_ge(sem("xb"), 6)
            v.wait_ge(sem("part_ps"), 5)
            v.tensor_tensor(X[5][:, :, :], XB[4][:, :, :], bank(6)[:, 0:256].rearrange("p (b d) -> p b d", b=B),
                            ALU.add).then_inc(sem("x_ready"), 1)

            v.wait_ge(sem("x_ready"), 7)
            ln_stats(5)
            ln_apply(5)
            v.wait_ge(sem("router_ps"), 2)
            router(1, bank(7)[:, 256:272].rearrange("p (b n) -> p b n", b=B))
            top = router_top(1)
            link(v.memset(top[:, :, 2:8], -1.0))
            for b in range(B):
                v.match_replace(rt[:, 1, 80 + 8 * b:88 + 8 * b], top[:, b, :], rt[:, 1, 36 + 8 * b:44 + 8 * b],
                                -2.0).then_inc(sem("rt_mr"), 1)
            v.wait_ge(sem("rt_mr"), 2)
            link(v.scalar_tensor_tensor(rt[:, 1, 96:112], rt[:, 1, 80:96], 0.0, rt[:, 1, 36:52], ALU.is_lt,
                                        ALU.mult))
            v.tensor_tensor(rt[:, 1, 112:128].rearrange("p (b n) -> p b n", b=B),
                            rt[:, 1, 96:112].rearrange("p (b n) -> p b n", b=B),
                            rt[:, 1, 72:74].unsqueeze(2).to_broadcast([128, B, NE]), ALU.mult).then_inc(
                sem("rw"), 1)
            v.wait_ge(sem("rwT_ps"), 1)
            v.tensor_copy(rsel[:, :], bank(5)[0:NE, 0:256]).then_inc(sem("rsel"), 1)
            for c in range(FC):
                v.wait_ge(sem("gelu"), c + 1 + 4)
                v.wait_ge(sem("rx_ps"), c + 1)
                v.tensor_tensor(gw[:, c, :], g5[:, c, :], weights_ps(c),
                                ALU.mult).then_inc(sem("gw"), 1)
            for b in range(B):
                v.wait_ge(sem("part_ps"), b + 1 + 5)
                v.tensor_tensor(X[6][:, b, :], X[5][:, b, :], bank(2 + b)[:, 256:384], ALU.add).then_inc(
                    sem("out_ready"), 1)

        @block.tensor
        def _(pe):
            def mm(o, lhsT, rhs, start=True, stop=True, **kw):
                return pe.matmul(o, lhsT, rhs, start=start, stop=stop, **kw)

            def ln_turn(i):
                for b in range(B):
                    pe.wait_ge(sem("ln_h"), 2 * i + b + 1)
                    ins = pe.transpose(bank(4)[:, 128 * b:128 * b + 128], h[i][:, b, :], ident)
                ins.then_inc(sem("ln_hT_ps"), 1)

            def awake(n, to=5, cols=512):
                for _ in range(n):
                    mm(bank(to)[:, 0:cols], identb[:, :],
                       sel[:, :, :, :].rearrange("p g a r -> p (g a r)")[:, 0:cols])

            pe.wait_ge(sem("ld_x"), 16)
            for _ in range(5):
                mm(bank(7)[:, 0:128], X[0][:, 0, :], X[0][:, 0, :])
            pe.wait_ge(sem("ld_first"), 16)
            ln_turn(0)
            for _ in range(3):
                mm(bank(7)[:, 0:128], X[0][:, 0, :], X[0][:, 0, :])

            def keys(i):
                b, k = i // 4, (i % 4) * 512
                pe.wait_ge(sem(f"ld_ctxT{i // 2}"), 16)
                if i < 2:
                    pe.wait_ge(sem("probs"), 2)
                else:
                    pe.wait_ge(sem("k_res"), i - 1)
                mm(bank(6 + i % 2), w("wB", "wk"), ctxT[:, b, k:k + 512]).then_inc(sem("k_ps"), 1)

            def scores0(b, j):
                pe.wait_ge(sem(f"ld_ctxT{2 * b + j // 2}"), 16)
                if b == 1 and j == 3:
                    pe.wait_ge(sem("cwc"), 1)
                mm(bank(4 * b + j), cm[:, 128 * b:128 * b + 128],
                   ctxT[:, b, 512 * j:512 * j + 512]).then_inc(sem("s0_ps"), 1)

            def turn_p(b, j):
                pe.wait_ge(sem("probs"), b + 1)
                n = 4 * b + j
                if n >= 2:
                    pe.wait_ge(sem("pT_dve") if j % 2 == 0 else sem("pT_act"), n // 2)
                for c in range(4):
                    ins = pe.transpose(bank(j % 2)[:, 128 * c:128 * c + 128],
                                       P0[:, b, 512 * j + 128 * c:512 * j + 128 * c + 128], ident)
                ins.then_inc(sem("pT_ps"), 1)

            def weigh(b, j):
                n = 4 * b + j
                pe.wait_ge(sem("pT_dve") if j % 2 == 0 else sem("pT_act"), n // 2 + 1)
                if j == 0:
                    pe.wait_ge(sem(f"ld_ctxN{b}"), 16)
                for c in range(4):
                    ins = mm(bank(2 + b)[:, 0:128], PT0[:, b, 512 * j + 128 * c:512 * j + 128 * c + 128],
                             ctxN[:, b, 4 * j + c, :], start=(j == 0 and c == 0), stop=(j == 3 and c == 3))
                if j == 3:
                    ins.then_inc(sem("c2q_ps"), 1)

            pe.wait_ge(sem("cm"), 1)
            for j in range(4):
                scores0(0, j)
            for b in range(B):
                ins = mm(bank(7)[:, b:1 + b], hT[0][:, 128 * b:128 * b + 128], w("first", "w_c"))
            ins.then_inc(sem("cwc_ps"), 1)
            for j in range(4):
                scores0(1, j)
            turn_p(0, 0)
            turn_p(0, 1)
            turn_p(0, 2)
            weigh(0, 0)
            pe.wait_ge(sem("rowmax"), 1)
            pe.wait_ge(sem("probs"), 2)
            pe.transpose(bank(4)[0:B, 0:128], rowmax[:, :], ident).then_inc(sem("rm_ps"), 1)
            pe.wait_ge(sem("ld_wB"), 16)
            keys(0)
            weigh(0, 1)
            turn_p(0, 3)
            keys(1)
            weigh(0, 2)
            keys(2)
            turn_p(1, 0)
            weigh(0, 3)
            pe.wait_ge(sem("brow"), 1)
            pe.transpose(bank(4)[:, 128:128 + B], brow[:, :], ident[0:B, 0:B]).then_inc(sem("batt_ps"), 1)
            keys(3)
            turn_p(1, 1)
            weigh(1, 0)
            keys(4)
            pe.wait_ge(sem("batt"), 1)
            for b in range(B):
                ins = mm(bank(5)[:, b:b + 1], h[0][:, b, :], batt[:, b:b + 1])
            ins.then_inc(sem("q2c_ps"), 1)
            turn_p(1, 2)
            weigh(1, 1)
            keys(5)
            turn_p(1, 3)
            weigh(1, 2)
            keys(6)
            weigh(1, 3)
            keys(7)
            for b in range(B):
                pe.wait_ge(sem("c2q"), b + 1)
                ins = pe.transpose(bank(5)[:, 256 + 128 * b:384 + 128 * b], c2q[:, b, :], ident)
            ins.then_inc(sem("turn_ps"), 1)
            wl = w("wA", "wl")
            pe.wait_ge(sem("ld_wA"), 16)
            pe.wait_ge(sem("x4T"), 2)
            pe.wait_ge(sem("batt"), 1)
            for b in range(B):
                q = slice(128 * b, 128 * b + 128)
                to = bank(4)[:, 256 + 128 * b:384 + 128 * b]
                mm(to, hT[0][:, q], wl[:, 0:128], start=True, stop=False)
                mm(to, x4T[:, q], wl[:, 384:512], start=False, stop=False)
                pe.wait_ge(sem("turned"), 1)
                mm(to, c2qT[:, q], wl[:, 128:256], start=False, stop=False)
                pe.wait_ge(sem("x3T"), 1)
                ins = mm(to, x3T[:, q], wl[:, 256:384], start=False, stop=True)
            ins.then_inc(sem("part_ps"), 1)

            def values(i):
                if i >= 2:
                    pe.wait_ge(sem("v_set"), i - 1)
                for c in range(4):
                    k = 512 * (i % 4) + 128 * c
                    ins = mm(bank(V_BANK[i % 2])[:, 128 * c:128 * c + 128], ctxT[:, i // 4, k:k + 128], w("wB", "wv"))
                ins.then_inc(sem("v_ps"), 1)

            for i in range(3):
                values(i)
            ln_turn(1)
            pe.wait_ge(sem("ld_wC"), 16)
            pe.wait_ge(sem("ln_hT"), 2)
            for j in range(2):
                mm(bank(2)[:, 256 * j:256 * j + 256], w("wC", "iq")[:, 128 * j:128 * j + 128], hT[1][:, :])
            mm(bank(3)[:, 0:256], w("wC", "ik"), hT[1][:, :]).then_inc(sem("iq_ps"), 1)
            pe.wait_ge(sem("v_set"), 3)

            def query_key(i):
                for j, name in enumerate((("q", "qs"), ("k", "ks"))[i]):
                    ins = mm(bank(i)[:, 256 * j:256 * j + 256], w("wC", name), hT[1][:, :])
                ins.then_inc(sem("qk_ps"), 1)

            query_key(0)
            for b in range(B):
                q = slice(128 * b, 128 * b + 128)
                mm(bank(7)[:, 256 + IH * b:256 + IH * b + IH], hT[1][:, q], w("wC", "iw"))
                ins = mm(bank(7)[:, q], hT[1][:, q], w("wC", "v"))
            ins.then_inc(sem("iw_ps"), 1)
            pe.wait_ge(sem("index_T"), 3)
            for r in range(2):
                p = slice(64 * r, 64 * r + 64)
                for b in range(B):
                    for i in range(IH // 2):
                        c = 256 * i + 128 * b
                        o = 128 * (2 * b + i)
                        ins = mm(bank(5 + r)[:, o:o + 128], iqT[p, c:c + 128], ikT[p, 128 * b:128 * b + 128])
                ins.then_inc(sem("hs_ps"), 1)
            query_key(1)
            pe.wait_ge(sem("rotated"), 1)
            values(3)
            pe.wait_ge(sem("qk_b"), 2)
            values(4)
            pe.wait_ge(sem("rotated"), 1)
            pe.wait_ge(sem("k_rotated"), 1)
            pe.wait_ge(sem("V"), 1)
            for b in range(B):
                q = slice(128 * b, 128 * b + 128)
                ins = mm(bank(7)[:, q], qr[:, q], kr[:, q])
            ins.then_inc(sem("lg_ps"), 1)
            values(5)
            pe.wait_ge(sem("ld_identb"), 16)
            pe.wait_ge(sem("ld_sel"), 16)
            awake(8, to=2, cols=256)
            pe.wait_ge(sem("v_set"), 6)
            for b in range(B):
                pe.wait_ge(sem("probs"), b + 1 + 2)
                ins = pe.transpose(bank(0)[:, 128 * b:128 * b + 128], Pm[:, b, :], ident)
                if b == B - 1:
                    ins.then_inc(sem("turn_ps"), 1)
                awake(3, to=2, cols=256)
            pe.wait_ge(sem("turned"), 2)
            for b in range(B):
                q = slice(128 * b, 128 * b + 128)
                ins = mm(bank(1)[:, q], V[:, b, :], PmT[:, q])
            ins.then_inc(sem("turn_ps"), 1)
            awake(3, to=2, cols=256)
            pe.wait_ge(sem("turned"), 3)
            for b in range(B):
                q = slice(128 * b, 128 * b + 128)
                ins = mm(bank(3)[:, q], aT[:, q], w("wC", "o"))
            ins.then_inc(sem("part_ps"), 1)

            pe.wait_ge(sem("onesb"), 1)
            pe.wait_ge(sem("mask_bias"), 2)
            for i in range(8):
                ins = mm(bank(1)[0:1, :], onesb[:, :], mb[:, i // 4, 512 * (i % 4):512 * (i % 4) + 512],
                         start=(i == 0), stop=(i == 7))
            ins.then_inc(sem("flag_ps"), 1)
            awake(9, cols=256)
            ln_turn(2)
            awake(3, cols=256)
            pe.wait_ge(sem("ld_wD"), 16)
            pe.wait_ge(sem("ln_hT"), 3)
            for b in range(B):
                ins = mm(bank(7)[:, 8 * b:8 * b + 8], hT[2][:, 128 * b:128 * b + 128], w("wD", "r"))
            ins.then_inc(sem("router_ps"), 1)
            for c in range(FC):
                mm(hidden2(c), w("wD", "w1")[:, 128 * c:128 * c + 128],
                   hT[2][:, :]).then_inc(sem("hidden_ps"), 1)
            pe.wait_ge(sem("x_ready"), 3)
            pe.wait_ge(sem("rt_max"), 1)
            for c in range(FC):
                pe.wait_ge(sem("gelu"), c + 1)
                for b in range(B):
                    ins = mm(part2(b), g0[:, c, 128 * b:128 * b + 128], w("wD", "w2")[:, 128 * c:128 * c + 128],
                             start=(c == 0), stop=(c == FC - 1))
            ins.then_inc(sem("part_ps"), 1)

            pe.wait_ge(sem("ld_identb"), 16)
            pe.wait_ge(sem("ld_sel"), 16)
            pe.wait_ge(sem("flag"), 1)
            values(6)
            values(7)
            awake(4)
            ln_turn(3)
            pe.wait_ge(sem("ld_wE"), 16)
            pe.wait_ge(sem("v_set"), 8)
            pe.wait_ge(sem("ln_hT"), 4)
            mm(bank(5)[:, 0:256], w("wE", "q"), hT[3][:, :]).then_inc(sem("q3_ps"), 1)
            pe.wait_ge(sem("mask_bias"), 4)
            any_masked = pe.value_load(flag[0:1, 0:1], min_val=0, max_val=1)
            awake(7, to=6)
            pe.wait_ge(sem("ld_cst"), 16)
            pe.wait_ge(sem("ld_sel"), 16)
            pe.wait_ge(sem("ld_identb"), 16)
            pe.wait_ge(sem("ld_tail"), 16 * 2 * RING)
            pe.wait_ge(sem("v_set"), 8)

            def stack_queries(g):
                if g == 0:
                    pe.wait_ge(sem("rt_max"), 1)
                elif g == 1:
                    pe.wait_ge(sem("qs"), 2)
                else:
                    pe.wait_ge(sem("qt"), 2 * (B * (g - 2) + 2))
                for a in range(3):
                    if g == 0:
                        pe.wait_ge(sem(("q3_hi", "q3_mid", "q3_lo")[a]), 1)
                    ins = mm(bank(7)[:, 0:256], sel[:, g, a, :], qp[:, a, :], start=(a == 0), stop=(a == 2))
                ins.then_inc(sem("stack_ps"), 1)

            def stack_queries_max(u):
                g, b = u // B, u % B
                pe.wait_ge(sem("mt"), u + 1)
                pe.wait_ge(sem("qs"), min(2 * (g + 2), 2 * G))
                if b == 1:
                    pe.wait_ge(sem("qt"), 2 * u)
                    if g >= 1:
                        pe.wait_ge(sem("oq"), 2 * g)
                mm(bank(7)[:, 0:128], mt[:, g % 2, b, :], identb[:, :]).then_inc(sem("stackm_ps"), 1)

            def pair_rows(g, b):
                pe.wait_ge(sem("o_rows"), 2 * g + b + 1)
                if b == 0:
                    pe.wait_ge(sem("qt"), 2 * min(B * (g + 1) + 1, UNITS))
                    if g == G - 1:
                        pe.wait_ge(sem("oq"), 2 * (G - 1))
                for e in range(2):
                    ins = pe.transpose(bank(7)[:, 256 * b + S * e:256 * b + S * e + S], O[:, b, S * e:S * e + S],
                                       ident)
                ins.then_inc(sem("oq_ps"), 1)

            def wide_attention(masked):
                def score(m):
                    g, b, e, c = m // 16, m // 8 % 2, m // 4 % 2, m % 4
                    if m % 16 in (0, 4):
                        pe.wait_ge(sem("qs"), 2 * g + 1 + e)
                    if m % 8 == 0 and (g == 0 or g >= RING):
                        if g == 0:
                            pe.wait_ge(sem(f"k_in{b}"), 16 * 2 * NBLK)
                        elif b == 0:
                            pe.wait_ge(sem(f"k_in_pair{g}"), B * 16 * 2 * NBLK)
                    if m >= 2:
                        pe.wait_ge(sem("s_red"), m - 1)
                    ins = mm(bank(m % 2), qs[:, g % Q_RING, e, b, :], kst[:, g % RING, b, 512 * c:512 * c + 512],
                             stop=not masked)
                    if masked:
                        ins = mm(bank(m % 2), identb[:, :], mb[:, b, 512 * c:512 * c + 512], start=False)
                    ins.then_inc(sem("s_done"), 1)

                def score_t(n):
                    g, b, u = n // 8, n // 4 % 2, n % 4
                    if n >= 2:
                        pe.wait_ge(sem("p3"), n - 1)
                    if u == 0:
                        pe.wait_ge(sem("qt"), 2 * (n // 4) + 2)
                    for c in range(4):
                        k = 128 * (4 * u + c)
                        to = bank(2 + 2 * (n % 2), 2)[:, 256 * c:256 * c + 256].rearrange("p (e q) -> p e q", e=2)
                        ins = mm(to, kst[:, g % RING, b, k:k + 128], qs[:, g % Q_RING, :, b, :], stop=not masked)
                        if masked:
                            ins = mm(to, identb[:, :],
                                     mbT[:, b, 4 * u + c, :].unsqueeze(1).to_broadcast([128, 2, S]), start=False)
                    ins.then_inc(sem("st_done"), 1)

                def weigh_values(n):
                    g, b, u = n // 8, n // 4 % 2, n % 4
                    pe.wait_ge(sem("p3"), n + 1)
                    if n == 0:
                        pe.wait_ge(sem("flag"), 1)
                    elif u == 0:
                        pe.wait_ge(sem("o_rows"), 2 * g + b)
                    for c in range(4):
                        ins = mm(bank(6)[32 * c:32 * c + 32, 0:256], value(b, 4 * u + c, g),
                                 pt_ring[:, n % 4, 256 * c:256 * c + 256], start=(u == 0), stop=(u == 3),
                                 tile_position=(0, 32 * c))
                    ins.then_inc(sem("pv_done"), 1)

                m = 0
                while m < 8:
                    score(m)
                    awake(1, to=6, cols=128)
                    m += 1
                stack_queries(1)
                for _ in range(3):
                    score(m)
                    m += 1
                stack_queries_max(0)
                for n in range(8 * G):
                    g, j = n // 8, n % 8
                    if n % 4 == 3 and n // 4 + 1 < UNITS:
                        stack_queries_max(n // 4 + 1)
                    if j == 5 and g + 2 < G:
                        stack_queries(g + 2)
                    goal = min(8 + S_LEAD + 2 * (n + 1), 16 * G)
                    if m < goal:
                        score(m)
                        m += 1
                    score_t(n)
                    if m < goal:
                        score(m)
                        m += 1
                    if n:
                        weigh_values(n - 1)
                    if m < goal:
                        score(m)
                        m += 1
                    if j == 1 and g:
                        pair_rows(g - 1, 0)
                        pair_rows(g - 1, 1)
                weigh_values(8 * G - 1)
                pair_rows(G - 1, 0)
                pair_rows(G - 1, 1)

            stack_queries(0)
            with pe.If(any_masked != 0):
                wide_attention(True)
            with pe.Else():
                wide_attention(False)
            for b in range(B):
                pe.wait_ge(sem("att3"), 2)
                ins = pe.transpose(bank(0)[:, 128 * b:128 * b + 128], ob[:, b, :], ident)
            ins.then_inc(sem("turn_ps"), 1)
            awake(3, cols=256)
            pe.wait_ge(sem("turned"), 4)
            for b in range(B):
                q = slice(128 * b, 128 * b + 128)
                ins = mm(bank(1)[:, q], att3T[:, q], w("wE", "o"))
            ins.then_inc(sem("part_ps"), 1)

            awake(7)
            ln_turn(4)
            awake(3, cols=256)
            pe.wait_ge(sem("ld_wF"), 16)
            pe.wait_ge(sem("ln_hT"), 5)
            for side, names in ((1, ("ka", "kb")), (0, ("qa", "qb"))):
                for j, name in enumerate(names):
                    ins = mm(bank(side)[:, 256 * j:256 * j + 256], w("wF", name), hT[4][:, :])
                ins.then_inc(sem("qk4_ps"), 1)
            for b in range(B):
                ins = mm(bank(2)[:, 256 * b:256 * b + 256], hT[4][:, 128 * b:128 * b + 128], w("wF", "v"))
            ins.then_inc(sem("v4_ps"), 1)

            def scores4(n):
                b, j = n // 4, n % 4
                if n == 1:
                    pe.wait_ge(sem("kbd_dve"), 1)
                else:
                    pe.wait_ge(sem("kbd_pool"), max(n, 1))
                if n >= 3:
                    pe.wait_ge(sem("sub4"), n - 2)
                mm(bank(4 + n % 3), qr4[:, 128 * b:128 * b + 128],
                   kbd[:, b, 4 * j:4 * j + 4, :].rearrange("p h k -> p (h k)")).then_inc(sem("s4_ps"), 1)

            def turn4(n):
                b, j = n // 4, n % 4
                pe.wait_ge(sem("exp4"), n + 1)
                if n >= 2:
                    pe.wait_ge(sem("p4T"), n - 1)
                for i in range(4):
                    ins = pe.transpose(bank(3 if n % 2 else 7)[:, 128 * i:128 * i + 128], sc4[:, b, 4 * j + i, :],
                                       ident)
                ins.then_inc(sem("p4T_ps"), 1)

            def weigh4(n):
                b, quad = n // 4, n % 4
                if n == 0:
                    pe.wait_ge(sem("v4"), 1)
                pe.wait_ge(sem("p4T"), n + 1)
                for j in range(4):
                    hd = 4 * quad + j
                    ins = mm(bank(b)[32 * j:32 * j + 32, 128 * quad:128 * quad + 128], v4[:, b, hd, :],
                             pT4[:, b, hd, :], tile_position=(0, 32 * j))
                if quad == 3:
                    ins.then_inc(sem("o4_ps"), 1)

            def turn_out4(b):
                pe.wait_ge(sem("o4"), b + 1)
                pe.wait_ge(sem("sub4"), 8)
                for quad in range(4):
                    ins = pe.transpose(bank(6 - 2 * b)[:, 128 * quad:128 * quad + 128],
                                       o4[:, b, 128 * quad:128 * quad + 128], ident)
                ins.then_inc(sem("o4T_ps"), 1)

            awake(9, to=3, cols=256)
            pe.wait_ge(sem("rotated4"), 2)
            for n in range(3):
                scores4(n)
            for n in range(8):
                if n + 3 < 8:
                    scores4(n + 3)
                turn4(n)
                if n == 5:
                    for i in range(4):
                        weigh4(i)
                if n > 5:
                    weigh4(n - 2)
            turn_out4(0)
            weigh4(6)
            weigh4(7)
            awake(4, to=2, cols=256)
            turn_out4(1)
            for b in range(B):
                awake(6 * b, to=2, cols=256)
                pe.wait_ge(sem("r4"), b + 1)
                ins = pe.transpose(bank(7)[:, 128 * b:128 * b + 128], r4[:, 2, b, :], ident)
            ins.then_inc(sem("turn_ps"), 1)
            awake(3, to=2, cols=256)
            pe.wait_ge(sem("turned"), 5)
            for b in range(B):
                q = slice(128 * b, 128 * b + 128)
                ins = mm(bank(6)[:, q], r4T[:, q], w("wF", "o"))
            ins.then_inc(sem("part_ps"), 1)

            awake(9)
            ln_turn(5)
            awake(3, cols=256)
            pe.wait_ge(sem("ld_wG"), 16)
            pe.wait_ge(sem("ln_hT"), 6)
            pe.wait_ge(sem("x_ready"), 7)
            for b in range(B):
                ins = mm(bank(7)[:, 256 + 8 * b:264 + 8 * b], hT[5][:, 128 * b:128 * b + 128], w("wG", "r"))
            ins.then_inc(sem("router_ps"), 1)
            for c in range(FC):
                mm(bank(c)[:, 0:256], w("wG", "w1")[:, 128 * c:128 * c + 128], hT[5][:, :]).then_inc(
                    sem("hidden_ps"), 1)
            pe.wait_ge(sem("rt_max"), 2)
            awake(3, to=7)
            pe.wait_ge(sem("rw"), 1)
            for b in range(B):
                ins = pe.transpose(bank(5)[0:NE, 128 * b:128 * b + 128], rt[:, 1, 112 + 8 * b:120 + 8 * b], ident)
            ins.then_inc(sem("rwT_ps"), 1)
            pe.wait_ge(sem("rsel"), 1)
            pe.wait_ge(sem("ld_b2e"), 32)
            for c in range(FC):
                mm(weights_ps(c), E8[:, 128 * c:128 * c + 128], rsel[:, :]).then_inc(sem("rx_ps"), 1)
            pe.wait_ge(sem("gelu"), FC + 4)
            for b in range(B):
                mm(bank(2 + b)[:, 256:384], rsel[:, 128 * b:128 * b + 128], b2e[:, :], start=True, stop=False)
            for c in range(FC):
                pe.wait_ge(sem("gw"), c + 1)
                for b in range(B):
                    ins = mm(bank(2 + b)[:, 256:384], gw[:, c, 128 * b:128 * b + 128],
                             w("wG", "w2")[:, 128 * c:128 * c + 128], start=False, stop=(c == FC - 1))
                    if c == FC - 1:
                        ins.then_inc(sem("part_ps"), 1)


def constants():
    f = np.float32
    cst = {}
    half = D // 2
    inv = f(1.0) / f(10000.0) ** (np.arange(half, dtype=f) / f(half))
    ang = np.arange(S, dtype=f)[:, None] * inv[None, :].astype(f)
    cos, sin = np.cos(ang).astype(f).T, np.sin(ang).astype(f).T
    cst["cos"] = np.concatenate([cos, cos])
    cst["sin"] = np.concatenate([-sin, sin])
    theta = f(10000.0) ** (-np.arange(0, DH, 2, dtype=f) / f(DH))
    fr = np.arange(S, dtype=f)[:, None] * theta[None, :].astype(f)
    rope = np.concatenate([np.cos(fr), np.sin(fr)], axis=1).astype(f)
    c, s = rope[:, ::2], rope[:, 1::2]
    va, vb = np.concatenate([c, s], 1), np.concatenate([-s, c], 1)
    cst["va"], cst["vb"], cst["na"], cst["nb"] = va, vb, -va, -vb
    cst["A"], cst["B"] = np.tile(va.T, (H, 1)), np.tile(vb.T, (H, 1))
    feat = np.arange(128)
    cst["hm"] = (feat[:, None] // DH == np.arange(H)[None, :]).astype(f)
    sel = np.zeros((128, G, 3, 128), f)
    for g in range(G):
        for e in range(2):
            for blk, a in enumerate(Q_PARTS):
                for d in range(DH):
                    sel[(2 * g + e) * DH + d, g, a, 64 * e + PART_ROWS[blk] + d] = 1.0
    tail = np.zeros((PART_ROWS[4] - MAX_ROW, B * SK), f)
    tail[0:3] = 1.0
    E8 = np.repeat(np.eye(NE, dtype=f), FC * D // NE, axis=1)
    return cst, sel.reshape(128, -1), tail, E8


def kernel(**inp):
    import ml_dtypes
    import concourse.bacc as bacc
    from concourse.bass_utils import run_bass_kernel_spmd

    a = {k: np.asarray(v) for k, v in inp.items()}
    bf = ml_dtypes.bfloat16
    cst, sel, tail, E8 = constants()

    def blocks(m):
        return np.concatenate([m[128 * i:128 * (i + 1)] for i in range(m.shape[0] // 128)], axis=1)

    def col(x):
        return x.reshape(-1, 1)

    wq, wk, wv = (a["L0_attn_w_qkv"][i * D:(i + 1) * D] for i in range(3))
    bq, bk, bv = (a["L0_attn_b_qkv"][i * D:(i + 1) * D] for i in range(3))
    swap = (np.arange(D) + D // 2) % D
    hj = np.arange(D)
    pa = (hj // DH) * DH + 2 * (hj % (DH // 2))
    pb = pa + 1
    w1e = np.concatenate(list(a["L1_ffn_W1"]), axis=1)
    w2e = np.concatenate(list(a["L1_ffn_W2"]), axis=0)
    fields = {
        "first": dict(ident=np.eye(128, dtype=np.float32), w_cq=col(a["L0_xattn_w_cq"]), w_q=col(a["L0_xattn_w_q"]),
                      w_c=col(a["L0_xattn_w_c"])),
        "wA": dict(wl=blocks(a["L0_xattn_W_l"].T)),
        "wB": dict(wk=a["L1_xattn_Wk"].T, wv=a["L1_xattn_Wv"].T, bk=col(a["L1_xattn_bk"])),
        "wC": dict(q=wq.T, qs=wq[swap].T, k=wk.T, ks=wk[swap].T, v=wv.T, iq=a["L0_attn_w_iq"].T,
                   ik=np.concatenate([a["L0_attn_w_ik"].T] * 2, axis=1), iw=a["L0_attn_w_iw"].T,
                   o=a["L0_attn_w_o"].T, bq=col(bq), bqs=col(bq[swap]), bk=col(bk), bks=col(bk[swap]),
                   biq=a["L0_attn_b_iq"].reshape(2, D).T, bik=col(np.concatenate([a["L0_attn_b_ik"]] * 2))),
        "wD": dict(r=a["L0_ffn_router_w"], w1=a["L0_ffn_w1"], w2=blocks(a["L0_ffn_w2"]),
                   b1=a["L0_ffn_b1"].reshape(FC, D).T),
        "wE": dict(q=a["L1_xattn_Wq"].T, o=a["L1_xattn_Wo"].T, bq=col(a["L1_xattn_bq"])),
        "wF": dict(qa=a["L1_attn_Wq"][pa].T, qb=a["L1_attn_Wq"][pb].T, ka=a["L1_attn_Wk"][pa].T,
                   kb=a["L1_attn_Wk"][pb].T,
                   v=np.concatenate([a["L1_attn_Wv"][pa].T, a["L1_attn_Wv"][pb].T], axis=1),
                   o=a["L1_attn_Wo"].T, bqa=col(a["L1_attn_bq"][pa]), bqb=col(a["L1_attn_bq"][pb]),
                   bka=col(a["L1_attn_bk"][pa]), bkb=col(a["L1_attn_bk"][pb])),
        "wG": dict(r=a["L1_ffn_router_w"], w1=w1e, w2=blocks(w2e), b1=a["L1_ffn_b1"].reshape(FC, D).T),
        "cst": cst,
    }
    arrays = {}
    for name, order in PACKS.items():
        arrays[name] = np.concatenate([fields[name][f] for f, _ in order], axis=1)
    rows = dict(b3=np.concatenate([a[f"L0_xattn_b_{k}"].reshape(1) for k in ("c", "q", "cq")]),
                b_l=a["L0_xattn_b_l"], a0_bv=bv, b_iw=a["L0_attn_b_iw"], a0_bo=a["L0_attn_b_o"],
                f0_b2=a["L0_ffn_b2"], x1_bv=a["L1_xattn_bv"], x1_bo=a["L1_xattn_bo"],
                a1_bv=np.concatenate([a["L1_attn_bv"][pa], a["L1_attn_bv"][pb]]), a1_bo=a["L1_attn_bo"],
                f1_rb=a["L1_ffn_router_b"])
    arrays["rows"] = np.concatenate([rows[f] for f, _ in ROWS]).reshape(1, -1)
    arrays["x"] = a["x"]
    arrays["ctx"] = a["ctx_1024"]
    arrays["ctxT"] = a["ctx_1024"].transpose(0, 2, 1)
    arrays["mask"] = a["mask_BxSxS2_if1"]
    arrays["maskT"] = a["mask_BxSxS2_if1"].transpose(0, 2, 1)
    arrays["b2e"] = a["L1_ffn_b2"]
    arrays["E8"] = E8
    arrays["identb"] = np.eye(128, dtype=bf)
    arrays["sel"] = sel.astype(bf)
    arrays["tail"] = tail.astype(bf)
    arrays = {f"in_{k}": np.ascontiguousarray(x) for k, x in arrays.items()}

    nc = bacc.Bacc("TRN2", target_bir_lowering=False, num_devices=1)
    A = {k[3:]: nc.dram_tensor(k, x.shape, mybir.dt.from_np(x.dtype), kind="ExternalInput").ap()
         for k, x in arrays.items()}
    out = nc.dram_tensor("out_dram", (B, S, D), F32, kind="ExternalOutput").ap()
    build(nc, A, out)
    r = run_bass_kernel_spmd(nc, [arrays], core_ids=[0])
    return r.results[0]["out_dram"]
```
